# Optimizing a Trainium2 kernel written in Bass

```python
import numpy as np
import jax
import jax.numpy as jnp

def _softmax(x, axis=-1):
    return jax.nn.softmax(x, axis=axis)

def _gelu(x):
    return jax.nn.gelu(x, approximate=True)

def _silu(x):
    return jax.nn.silu(x)

def _sigmoid(x):
    return jax.nn.sigmoid(x)

def _layernorm(x, axis=-1, eps=1e-05):
    m = jnp.mean(x, axis=axis, keepdims=True)
    v = jnp.var(x, axis=axis, keepdims=True)
    return (x - m) / jnp.sqrt(v + eps)

def _scatter_add(tgt, idx, src, axis=0):
    return tgt.at[idx].add(src)

def _segment_sum(src, seg, n):
    return jax.ops.segment_sum(src, seg, n)
kernel_name = 'mk_macaron_d2_jaxref_r8_8c9dd1'

def setup_inputs(seed: int=0):
    np.random.seed(seed)
    _w = jnp.asarray

    def _L0_attn_setup():
        import jax, jax.numpy as jnp
        import numpy as np
        import math
        B, N, DIM = (4, 512, 128)
        HEADS, DHEAD, NRF = (16, 64, 64)
        STAB = 1e-06

        def _phi(t, RF):
            return jax.nn.relu(jnp.einsum('bhnd,hdr->bhnr', t, RF))
        key = jax.random.key(seed)
        k1, k2, k3, k4 = jax.random.split(key, 4)
        x = jax.random.normal(k1, (B, N, DIM), dtype=jnp.float32)
        W_qkv = jax.random.normal(k2, (DIM, 3 * HEADS * DHEAD), dtype=jnp.float32) * (1.0 / math.sqrt(DIM))
        RF = jax.random.normal(k3, (HEADS, DHEAD, NRF), dtype=jnp.float32) / math.sqrt(NRF)
        W_out = jax.random.normal(k4, (HEADS * DHEAD, DIM), dtype=jnp.float32) * (1.0 / math.sqrt(HEADS * DHEAD))
        b_out = jnp.zeros((DIM,), dtype=jnp.float32)
        return {'x': x, 'W_qkv': W_qkv, 'RF': RF, 'W_out': W_out, 'b_out': b_out}
    _L0_attn_in = _L0_attn_setup()

    def _L0_ffn_setup():
        import jax, jax.numpy as jnp
        import numpy as np
        B, S, H = (2, 128, 128)
        E, F = (16, 64)
        G, TOPK_G, TOPK = (4, 2, 4)
        N_SHARED = 2
        ROUTE_SCALE = 1.0
        FS = N_SHARED * F

        def _gate(x, w_gate):
            T = x.shape[0]
            scores = jax.nn.sigmoid(x @ w_gate.T)
            sv = scores.reshape(T, G, E // G)
            group_scores = jax.lax.top_k(sv, 2)[0].sum(-1)
            top_groups = jax.lax.top_k(group_scores, TOPK_G)[1]
            allowed = jnp.zeros((T, G), dtype=bool).at[jnp.arange(T)[:, None], top_groups].set(True)
            masked = jnp.where(allowed[:, :, None], sv, -jnp.inf).reshape(T, E)
            _, idx = jax.lax.top_k(masked, TOPK)
            w = jnp.take_along_axis(scores, idx, axis=1)
            w = w / (w.sum(-1, keepdims=True) + 1e-06) * ROUTE_SCALE
            return (w, idx)

        def _swiglu(x, w1, w3, w2):
            return jax.nn.silu(x @ w1.T) * (x @ w3.T) @ w2.T
        key = jax.random.key(seed)
        ks = jax.random.split(key, 8)
        scale = 0.02
        return {'hidden_states': jax.random.normal(ks[0], (B, S, H), dtype=jnp.float32), 'w_gate': jax.random.normal(ks[1], (E, H), dtype=jnp.float32) * scale, 'w1_e': jax.random.normal(ks[2], (E, F, H), dtype=jnp.float32) * scale, 'w3_e': jax.random.normal(ks[3], (E, F, H), dtype=jnp.float32) * scale, 'w2_e': jax.random.normal(ks[4], (E, H, F), dtype=jnp.float32) * scale, 'w1_s': jax.random.normal(ks[5], (FS, H), dtype=jnp.float32) * scale, 'w3_s': jax.random.normal(ks[6], (FS, H), dtype=jnp.float32) * scale, 'w2_s': jax.random.normal(ks[7], (H, FS), dtype=jnp.float32) * scale}
    _L0_ffn_in = _L0_ffn_setup()

    def _L1_attn_setup():
        import jax, jax.numpy as jnp
        import numpy as np
        import math
        B, L, H, D, HID = (2, 128, 16, 64, 128)

        def _rope_tables(seq_len, dim):
            inv_freq = 1.0 / 10000.0 ** (jnp.arange(0, dim, 2, dtype=jnp.float32) / dim)
            t = jnp.arange(seq_len, dtype=jnp.float32)
            freqs = jnp.outer(t, inv_freq)
            emb = jnp.concatenate([freqs, freqs], -1)
            return (jnp.cos(emb), jnp.sin(emb))

        def _rotate_half(x):
            x1, x2 = jnp.split(x, 2, axis=-1)
            return jnp.concatenate([-x2, x1], axis=-1)

        def _apply_rope(x, cos, sin):
            return x * cos + _rotate_half(x) * sin

        def _forward(x, w_qkv, w_o, log_p, log_a, w1, b1, w2, b2):
            Bx, Lx, _ = x.shape
            qkv = jnp.dot(x, w_qkv).reshape(Bx, Lx, 3, H, D)
            qkv = jnp.transpose(qkv, (2, 0, 3, 1, 4))
            q, k, v = (qkv[0], qkv[1], qkv[2])
            cos, sin = _rope_tables(Lx, D)
            cos, sin = (cos[None, None], sin[None, None])
            q = _apply_rope(q, cos, sin)
            k = _apply_rope(k, cos, sin)
            scale = 1.0 / math.sqrt(D)
            scores = jnp.einsum('bhid,bhjd->bhij', q, k) * scale
            pos = jnp.arange(Lx, dtype=jnp.float32)
            dist = jnp.abs(pos[None, :] - pos[:, None])
            p = jax.nn.softplus(log_p)
            a = jax.nn.softplus(log_a)
            kerple = -p * jnp.log1p(a * dist[None])
            attn_t = jnp.transpose(scores, (0, 2, 3, 1))
            kerple_t = jnp.broadcast_to(jnp.transpose(kerple, (1, 2, 0))[None], attn_t.shape)
            combined = jnp.concatenate([attn_t, kerple_t], axis=-1)
            hdn = jax.nn.gelu(jnp.dot(combined, w1) + b1, approximate=False)
            refined = jnp.dot(hdn, w2) + b2
            refined = jnp.transpose(refined, (0, 3, 1, 2))
            scores = scores + kerple[None] + refined
            causal = jnp.tril(jnp.ones((Lx, Lx), dtype=bool))
            scores = jnp.where(causal[None, None], scores, -jnp.inf)
            weights = jax.nn.softmax(scores, axis=-1)
            out = jnp.einsum('bhij,bhjd->bhid', weights, v)
            out = jnp.transpose(out, (0, 2, 1, 3)).reshape(Bx, Lx, H * D)
            return jnp.dot(out, w_o)
        key = jax.random.key(seed)
        ks = jax.random.split(key, 8)
        s = 0.02
        return {'x': jax.random.normal(ks[0], (B, L, HID), jnp.float32), 'w_qkv': jax.random.normal(ks[1], (HID, 3 * H * D), jnp.float32) * s, 'w_o': jax.random.normal(ks[2], (H * D, HID), jnp.float32) * s, 'log_p': jax.random.normal(ks[3], (H, 1, 1), jnp.float32) * 0.02, 'log_a': jax.random.normal(ks[4], (H, 1, 1), jnp.float32) * 0.02, 'w1': jax.random.normal(ks[5], (2 * H, 2 * H), jnp.float32) * s, 'b1': jnp.zeros((2 * H,), jnp.float32), 'w2': jax.random.normal(ks[6], (2 * H, H), jnp.float32) * s, 'b2': jnp.zeros((H,), jnp.float32)}
    _L1_attn_in = _L1_attn_setup()

    def _L1_ffn_setup():
        import jax, jax.numpy as jnp
        import numpy as np
        B, T, D = (2, 256, 128)
        DCD = 512
        RET = 128
        NEXP = 512
        NKEYS = 64
        H = 4
        KPH = 8
        key = jax.random.key(seed)
        ks = jax.random.split(key, 10)
        s = lambda k, shape, scale: jax.random.normal(k, shape, jnp.float32) * scale
        return {'hidden_states': jax.random.normal(ks[0], (B, T, D), jnp.float32), 'Wg': s(ks[1], (D, DCD), 0.02), 'bg': jnp.zeros((DCD,), jnp.float32), 'Wu': s(ks[2], (D, DCD), 0.02), 'bu': jnp.zeros((DCD,), jnp.float32), 'Wd': s(ks[3], (DCD, D), 0.02), 'bd': jnp.zeros((D,), jnp.float32), 'Wq': s(ks[4], (D, RET * H), 0.02), 'keys': s(ks[5], (H, NKEYS, 2, RET // 2), 0.02), 'down_embed': s(ks[6], (NEXP, D), 0.02), 'up_embed': s(ks[7], (NEXP, D), 0.02)}
    _L1_ffn_in = _L1_ffn_setup()
    _d = {'L0_attn_x': _L0_attn_in['x'], 'L0_attn_W_qkv': _L0_attn_in['W_qkv'], 'L0_attn_RF': _L0_attn_in['RF'], 'L0_attn_W_out': _L0_attn_in['W_out'], 'L0_attn_b_out': _L0_attn_in['b_out'], 'L0_ffn_w_gate': _L0_ffn_in['w_gate'], 'L0_ffn_w1_e': _L0_ffn_in['w1_e'], 'L0_ffn_w3_e': _L0_ffn_in['w3_e'], 'L0_ffn_w2_e': _L0_ffn_in['w2_e'], 'L0_ffn_w1_s': _L0_ffn_in['w1_s'], 'L0_ffn_w3_s': _L0_ffn_in['w3_s'], 'L0_ffn_w2_s': _L0_ffn_in['w2_s'], 'L1_attn_w_qkv': _L1_attn_in['w_qkv'], 'L1_attn_w_o': _L1_attn_in['w_o'], 'L1_attn_log_p': _L1_attn_in['log_p'], 'L1_attn_log_a': _L1_attn_in['log_a'], 'L1_attn_w1': _L1_attn_in['w1'], 'L1_attn_b1': _L1_attn_in['b1'], 'L1_attn_w2': _L1_attn_in['w2'], 'L1_attn_b2': _L1_attn_in['b2'], 'L1_ffn_Wg': _L1_ffn_in['Wg'], 'L1_ffn_bg': _L1_ffn_in['bg'], 'L1_ffn_Wu': _L1_ffn_in['Wu'], 'L1_ffn_bu': _L1_ffn_in['bu'], 'L1_ffn_Wd': _L1_ffn_in['Wd'], 'L1_ffn_bd': _L1_ffn_in['bd'], 'L1_ffn_Wq': _L1_ffn_in['Wq'], 'L1_ffn_keys': _L1_ffn_in['keys'], 'L1_ffn_down_embed': _L1_ffn_in['down_embed'], 'L1_ffn_up_embed': _L1_ffn_in['up_embed']}
    _x0 = _d['L0_attn_x']
    _d['L0_attn_x'] = jax.random.normal(jax.random.fold_in(jax.random.key(seed), 1), (4, 512, 128), dtype=_x0.dtype)
    del _x0
    return _d

def reference(L0_attn_x, L0_attn_W_qkv, L0_attn_RF, L0_attn_W_out, L0_attn_b_out, L0_ffn_w_gate, L0_ffn_w1_e, L0_ffn_w3_e, L0_ffn_w2_e, L0_ffn_w1_s, L0_ffn_w3_s, L0_ffn_w2_s, L1_attn_w_qkv, L1_attn_w_o, L1_attn_log_p, L1_attn_log_a, L1_attn_w1, L1_attn_b1, L1_attn_w2, L1_attn_b2, L1_ffn_Wg, L1_ffn_bg, L1_ffn_Wu, L1_ffn_bu, L1_ffn_Wd, L1_ffn_bd, L1_ffn_Wq, L1_ffn_keys, L1_ffn_down_embed, L1_ffn_up_embed):

    def _L0_attn_ref(x, W_qkv, RF, W_out, b_out):
        import jax, jax.numpy as jnp
        import numpy as np
        import math
        B, N, DIM = (4, 512, 128)
        HEADS, DHEAD, NRF = (16, 64, 64)
        STAB = 1e-06

        def _phi(t, RF):
            return jax.nn.relu(jnp.einsum('bhnd,hdr->bhnr', t, RF))
        b, n, _ = x.shape
        qkv = x @ W_qkv
        q, k, v = jnp.split(qkv, 3, axis=-1)

        def to_heads(t):
            return t.reshape(b, n, HEADS, DHEAD).transpose(0, 2, 1, 3)
        q, k, v = (to_heads(q), to_heads(k), to_heads(v))
        phi_q = _phi(q, RF)
        phi_k = _phi(k, RF)
        kv = jnp.einsum('bhnr,bhnd->bhrd', phi_k, v)
        out = jnp.einsum('bhnr,bhrd->bhnd', phi_q, kv)
        k_sum = phi_k.sum(axis=2)
        normalizer = jnp.einsum('bhnr,bhr->bhn', phi_q, k_sum)[..., None] + STAB
        out = out / normalizer
        out = out.transpose(0, 2, 1, 3).reshape(b, n, HEADS * DHEAD)
        out = out @ W_out + b_out
        return out

    def _L0_ffn_ref(hidden_states, w_gate, w1_e, w3_e, w2_e, w1_s, w3_s, w2_s):
        import jax, jax.numpy as jnp
        import numpy as np
        B, S, H = (2, 128, 128)
        E, F = (16, 64)
        G, TOPK_G, TOPK = (4, 2, 4)
        N_SHARED = 2
        ROUTE_SCALE = 1.0
        FS = N_SHARED * F

        def _gate(x, w_gate):
            T = x.shape[0]
            scores = jax.nn.sigmoid(x @ w_gate.T)
            sv = scores.reshape(T, G, E // G)
            group_scores = jax.lax.top_k(sv, 2)[0].sum(-1)
            top_groups = jax.lax.top_k(group_scores, TOPK_G)[1]
            allowed = jnp.zeros((T, G), dtype=bool).at[jnp.arange(T)[:, None], top_groups].set(True)
            masked = jnp.where(allowed[:, :, None], sv, -jnp.inf).reshape(T, E)
            _, idx = jax.lax.top_k(masked, TOPK)
            w = jnp.take_along_axis(scores, idx, axis=1)
            w = w / (w.sum(-1, keepdims=True) + 1e-06) * ROUTE_SCALE
            return (w, idx)

        def _swiglu(x, w1, w3, w2):
            return jax.nn.silu(x @ w1.T) * (x @ w3.T) @ w2.T
        shape = hidden_states.shape
        x = hidden_states.reshape(-1, H)
        weights, idx = _gate(x, w_gate)
        combine = (jax.nn.one_hot(idx, E, dtype=x.dtype) * weights[..., None]).sum(1)
        g = jax.nn.silu(jnp.einsum('th,efh->tef', x, w1_e))
        u = jnp.einsum('th,efh->tef', x, w3_e)
        routed = jnp.einsum('tef,ehf,te->th', g * u, w2_e, combine)
        shared = _swiglu(x, w1_s, w3_s, w2_s)
        return (routed + shared).reshape(shape)

    def _L1_attn_ref(x, w_qkv, w_o, log_p, log_a, w1, b1, w2, b2):
        import jax, jax.numpy as jnp
        import numpy as np
        import math
        B, L, H, D, HID = (2, 128, 16, 64, 128)

        def _rope_tables(seq_len, dim):
            inv_freq = 1.0 / 10000.0 ** (jnp.arange(0, dim, 2, dtype=jnp.float32) / dim)
            t = jnp.arange(seq_len, dtype=jnp.float32)
            freqs = jnp.outer(t, inv_freq)
            emb = jnp.concatenate([freqs, freqs], -1)
            return (jnp.cos(emb), jnp.sin(emb))

        def _rotate_half(x):
            x1, x2 = jnp.split(x, 2, axis=-1)
            return jnp.concatenate([-x2, x1], axis=-1)

        def _apply_rope(x, cos, sin):
            return x * cos + _rotate_half(x) * sin

        def _forward(x, w_qkv, w_o, log_p, log_a, w1, b1, w2, b2):
            Bx, Lx, _ = x.shape
            qkv = jnp.dot(x, w_qkv).reshape(Bx, Lx, 3, H, D)
            qkv = jnp.transpose(qkv, (2, 0, 3, 1, 4))
            q, k, v = (qkv[0], qkv[1], qkv[2])
            cos, sin = _rope_tables(Lx, D)
            cos, sin = (cos[None, None], sin[None, None])
            q = _apply_rope(q, cos, sin)
            k = _apply_rope(k, cos, sin)
            scale = 1.0 / math.sqrt(D)
            scores = jnp.einsum('bhid,bhjd->bhij', q, k) * scale
            pos = jnp.arange(Lx, dtype=jnp.float32)
            dist = jnp.abs(pos[None, :] - pos[:, None])
            p = jax.nn.softplus(log_p)
            a = jax.nn.softplus(log_a)
            kerple = -p * jnp.log1p(a * dist[None])
            attn_t = jnp.transpose(scores, (0, 2, 3, 1))
            kerple_t = jnp.broadcast_to(jnp.transpose(kerple, (1, 2, 0))[None], attn_t.shape)
            combined = jnp.concatenate([attn_t, kerple_t], axis=-1)
            hdn = jax.nn.gelu(jnp.dot(combined, w1) + b1, approximate=False)
            refined = jnp.dot(hdn, w2) + b2
            refined = jnp.transpose(refined, (0, 3, 1, 2))
            scores = scores + kerple[None] + refined
            causal = jnp.tril(jnp.ones((Lx, Lx), dtype=bool))
            scores = jnp.where(causal[None, None], scores, -jnp.inf)
            weights = jax.nn.softmax(scores, axis=-1)
            out = jnp.einsum('bhij,bhjd->bhid', weights, v)
            out = jnp.transpose(out, (0, 2, 1, 3)).reshape(Bx, Lx, H * D)
            return jnp.dot(out, w_o)
        return _forward(x, w_qkv, w_o, log_p, log_a, w1, b1, w2, b2)

    def _L1_ffn_ref(hidden_states, Wg, bg, Wu, bu, Wd, bd, Wq, keys, down_embed, up_embed):
        import jax, jax.numpy as jnp
        import numpy as np
        B, T, D = (2, 256, 128)
        DCD = 512
        RET = 128
        NEXP = 512
        NKEYS = 64
        H = 4
        KPH = 8
        b, t, d = hidden_states.shape
        q = (hidden_states @ Wq).reshape(b, t, 2, H, RET // 2)
        sim = jnp.einsum('btphn,hkpn->pbthk', q, keys)
        sc, ix = jax.lax.top_k(sim, KPH)
        sx, sy = (sc[0], sc[1])
        ixx, ixy = (ix[0], ix[1])
        all_sc = (sx[..., :, None] + sy[..., None, :]).reshape(b, t, H, KPH * KPH)
        all_ix = (ixx[..., :, None] * NKEYS + ixy[..., None, :]).reshape(b, t, H, KPH * KPH)
        scores, pk = jax.lax.top_k(all_sc, KPH)
        idx = jnp.take_along_axis(all_ix, pk, axis=-1)
        de = down_embed[idx]
        ue = up_embed[idx]
        w = jnp.einsum('btd,bthkd->bthk', hidden_states, de)
        w = jax.nn.silu(w) * jax.nn.softmax(scores, axis=-1)
        experts_states = jnp.einsum('bthk,bthkd->btd', w, ue)
        mlp = jax.nn.silu(hidden_states @ Wg + bg) * (hidden_states @ Wu + bu) @ Wd + bd
        return mlp + experts_states
    x = L0_attn_x
    x = x + 0.5 * _L0_ffn_ref(_layernorm(x, axis=-1), L0_ffn_w_gate, L0_ffn_w1_e, L0_ffn_w3_e, L0_ffn_w2_e, L0_ffn_w1_s, L0_ffn_w3_s, L0_ffn_w2_s)
    x = x + _L0_attn_ref(_layernorm(x, axis=-1), L0_attn_W_qkv, L0_attn_RF, L0_attn_W_out, L0_attn_b_out)
    x = x + 0.5 * _L0_ffn_ref(_layernorm(x, axis=-1), L0_ffn_w_gate, L0_ffn_w1_e, L0_ffn_w3_e, L0_ffn_w2_e, L0_ffn_w1_s, L0_ffn_w3_s, L0_ffn_w2_s)
    x = x + 0.5 * _L1_ffn_ref(_layernorm(x, axis=-1), L1_ffn_Wg, L1_ffn_bg, L1_ffn_Wu, L1_ffn_bu, L1_ffn_Wd, L1_ffn_bd, L1_ffn_Wq, L1_ffn_keys, L1_ffn_down_embed, L1_ffn_up_embed)
    x = x + _L1_attn_ref(_layernorm(x, axis=-1), L1_attn_w_qkv, L1_attn_w_o, L1_attn_log_p, L1_attn_log_a, L1_attn_w1, L1_attn_b1, L1_attn_w2, L1_attn_b2)
    x = x + 0.5 * _L1_ffn_ref(_layernorm(x, axis=-1), L1_ffn_Wg, L1_ffn_bg, L1_ffn_Wu, L1_ffn_bu, L1_ffn_Wd, L1_ffn_bd, L1_ffn_Wq, L1_ffn_keys, L1_ffn_down_embed, L1_ffn_up_embed)
    return x

_drawn_inputs = setup_inputs


def setup_inputs(seed=0):
    import zlib

    import numpy as np

    out = dict(_drawn_inputs(seed))
    spreads = {'L0_attn_b_out': (0.0, 0.1),
     'L1_attn_b1': (0.0, 2.0),
     'L1_attn_b2': (0.0, 2.0),
     'L1_ffn_bg': (0.0, 0.8),
     'L1_ffn_bu': (0.0, 0.8),
     'L1_ffn_bd': (0.0, 0.308)}
    factors = {'L0_ffn_w_gate': 8.0,
     'L0_ffn_w1_e': 8.0,
     'L0_ffn_w3_e': 8.0,
     'L0_ffn_w2_e': 8.0,
     'L0_ffn_w1_s': 8.0,
     'L0_ffn_w3_s': 8.0,
     'L0_ffn_w2_s': 8.0,
     'L1_attn_log_p': 64.0,
     'L1_attn_log_a': 64.0,
     'L1_attn_w1': 64.0,
     'L1_attn_w2': 64.0,
     'L1_ffn_Wg': 4.448,
     'L1_ffn_Wu': 4.418,
     'L1_ffn_Wd': 4.031,
     'L1_ffn_Wq': 24.5,
     'L1_ffn_keys': 24.473,
     'L1_ffn_down_embed': 7.012,
     'L1_ffn_up_embed': 7.43,
     'L1_attn_w_qkv': 6.206,
     'L1_attn_w_o': 6.072}
    for name, (base, spread) in spreads.items():
        noise = np.random.default_rng([zlib.crc32(name.encode()), seed]).standard_normal(out[name].shape)
        drawn = base * np.exp(spread * noise) if base else spread * noise
        out[name] = jnp.asarray(drawn.astype(out[name].dtype))
    for name, factor in factors.items():
        out[name] = (out[name] * factor).astype(out[name].dtype)
    return out
```

```python
from contextlib import ExitStack

from concourse import mybir

F32 = mybir.dt.float32
F16 = mybir.dt.float16
BF16 = mybir.dt.bfloat16
ALU = mybir.AluOpType
ACT = mybir.ActivationFunctionType
AX_X = mybir.AxisListType.X


class Lane:

    def __init__(self, sem):
        self.sem = sem
        self.items = []
        self.n = 0

    def add(self, fn, after=(), mark=True):
        self.items.append((fn, tuple(after), mark))
        if mark:
            self.n += 1
        return (self.sem, self.n)

    def issue(self, eng):
        seen = {}
        for fn, after, mark in self.items:
            for sem, value in after:
                if seen.get(sem.name, 0) < value:
                    eng.wait_ge(sem, value)
                    seen[sem.name] = value
            ins = fn(eng)
            if mark:
                ins.then_inc(self.sem, 1)


class Slot:

    def __init__(self, ap):
        self.ap = ap
        self.free = []

    def take(self):
        waits, self.free = self.free, []
        return waits


class Ring:
    def __init__(self, slots):
        self.slots = slots
        self.i = 0

    def next(self):
        s = self.slots[self.i % len(self.slots)]
        self.i += 1
        return s


def build(nc, t, out):
    with ExitStack() as ctx:
        def sb(name, shape, dt=F32):
            return ctx.enter_context(nc.sbuf_tensor(name, shape, dt))

        def sem(name):
            return ctx.enter_context(nc.semaphore(name))

        pe, act, dve, pool, sp = (Lane(sem(n)) for n in ("s_pe", "s_act", "s_dve", "s_pool", "s_sp"))
        PS = [Slot(ctx.enter_context(nc.psum_tensor(f"ps{i}", [128, 512], F32))) for i in range(8)]

        x = sb("x", [128, 16, 128])
        xth = sb("xth", [128, 2048], F16)
        xtl = sb("xtl", [128, 2048], F16)
        idf = sb("idf", [128, 128])
        idb = sb("idb", [128, 128], BF16)
        ones = sb("ones", [128, 128])
        sel = sb("sel", [48, 8, 128], BF16)
        tri = sb("tri", [128, 4, 4])
        small = sb("small", [128, 1024])

        wgu_h, wgu_l = sb("wgu_h", [128, 1024], F16), sb("wgu_l", [128, 1024], F16)
        wk_h, wk_l = sb("wk_h", [128, 512], F16), sb("wk_l", [128, 512], F16)
        de_h, de_l = sb("de_h", [128, 512], F16), sb("de_l", [128, 512], F16)
        wdue = sb("wdue", [128, 8, 128])
        bgu = sb("bgu", [128, 8])
        rows = sb("rows", [1, 256])

        wa_h, wa_l = sb("wa_h", [128, 5120], F16), sb("wa_l", [128, 5120], F16)
        wo = sb("wo", [128, 8, 128])
        cs = sb("cs", [128, 2, 512])
        w1s, w1k = sb("w1s", [128, 128]), sb("w1k", [128, 128])
        w2b = sb("w2b", [128, 64])
        b1c = sb("b1c", [128, 1])
        b2r = sb("b2r", [64, 1])
        ktab = sb("ktab", [128, 640])
        pa = sb("pa", [128, 4])
        pab = sb("pab", [128, 2, 16])
        b2b = sb("b2b", [128, 16])

        reg0 = sb("reg0", [128, 8192])
        o = 0

        def r0(n, dt=F32):
            nonlocal o
            w = n if dt == F32 else n // 2
            v = reg0[:, o:o + w]
            o += w
            return v if dt == F32 else v.bitcast(dt)

        w13_h, w13_l = r0(2304, F16), r0(2304, F16)
        w2 = r0(1152).rearrange("p (b n) -> p b n", b=9)
        wg_h, wg_l = r0(16, F16), r0(16, F16)
        wq_h, wq_l = r0(1024, F16), r0(1024, F16)
        wkr_h, wkr_l = r0(1024, F16), r0(1024, F16)
        wv_h, wv_l = r0(1024, F16), r0(1024, F16)
        wout = r0(1024).rearrange("p (b n) -> p b n", b=8)
        assert o <= 8192
        kn = reg0[:, :].rearrange("p (h v) -> p h v", h=16)

        NW = 24096
        work = sb("work", [128, NW])

        def wk(a, n, dt=F32):
            assert a + n <= NW
            v = work[:, a:a + n]
            return v if dt == F32 else v.bitcast(dt)

        ctb = wk(23000, 1024, BF16)[0:48, :]

        def mm(o_, l, r, start, stop, after=(), mark=False):
            return pe.add(lambda e: e.matmul(o_, l, r, start=start, stop=stop), after, mark)

        def tp(o_, i_, ident, after=(), mark=False):
            return pe.add(lambda e: e.transpose(o_, i_, ident), after, mark)

        def af(o_, i_, f, after=(), **kw):
            return act.add(lambda e: e.activation(o_, i_, f, **kw), after)

        def tt(lane, o_, a, b, op, after=()):
            return lane.add(lambda e: e.tensor_tensor(o_, a, b, op), after)

        def ts(lane, o_, a, s1, s2, op0, op1=None, after=()):
            if op1 is None:
                return lane.add(lambda e: e.tensor_scalar(o_, a, s1, None, op0), after)
            return lane.add(lambda e: e.tensor_scalar(o_, a, s1, s2, op0, op1), after)

        def stt(o_, a, s, b, op0, op1, after=(), **kw):
            return dve.add(lambda e: e.scalar_tensor_tensor(out=o_, in0=a, scalar=s, in1=b, op0=op0, op1=op1, **kw),
                           after)

        def cp(lane, o_, i_, after=()):
            return lane.add(lambda e: e.tensor_copy(o_, i_), after)

        def red(o_, i_, op, after=()):
            return dve.add(lambda e: e.tensor_reduce(o_, i_, AX_X, op), after)

        def ms(lane, o_, v, after=()):
            return lane.add(lambda e: e.memset(o_, v), after)

        loads = {}

        def load(key, dst, src, after=(), lane=sp):
            if key not in loads:
                loads[key] = [sem(f"l_{key}"), 0]
            s = loads[key]
            s[1] += 16
            sm = s[0]
            lane.add(lambda e: e.dma_start(dst, src).then_inc(sm, 16), after, False)

        def got(key):
            return (loads[key][0], loads[key][1])

        xin = t["x"].rearrange("b (q p) d -> p (b q) d", p=128)
        for c in range(4):
            load(f"x{c}", x[:, 4 * c:4 * c + 4, :], xin[:, 4 * c:4 * c + 4, :])
        load("id", idf[:, :], t["c_id"])
        st = 14000
        s_w13 = wk(st, 2304)
        s_gate = wk(st + 2304, 16)
        load("w13", s_gate, t["w_gate"])
        load("w13", s_w13, t["w13"])
        load("cst", tri[:, :, :], t["c_tri"])
        load("cst", wk(23000, 1024)[0:48, :].rearrange("p (b n) -> p b n", b=8), t["c_sel"])
        load("w2", w2, t["w2"])
        s_qk = wk(st + 2320, 2048).rearrange("p (b n) -> p b n", b=16)
        s_wv = wk(st + 4368, 1024)
        s_rf = wk(st + 5392, 1024).rearrange("p (b n) -> p b n", b=8)
        load("a0", s_qk, t["wqkT"])
        load("a0", s_rf, t["rf"])
        load("a0", s_wv, t["wv0"])
        load("a0", wout, t["wout"])
        s_gu = wk(st + 6416, 1024)
        s_wqT = wk(st + 7440, 512).rearrange("p (b n) -> p b n", b=4)
        s_key = wk(st + 7952, 512).rearrange("p (b n) -> p b n", b=4)
        s_de = wk(st + 8464, 512)
        load("f1", s_gu, t["wgu"])
        load("f1", s_wqT, t["wqT"])
        load("f1", s_key, t["keys"])
        load("f1", s_de, t["deT"])
        load("f1", wdue[:, :, :], t["wdue"])
        load("f1", bgu[:, :], t["bgu"])
        load("f1", rows[:, :], t["rows"])
        load("a1", wo[:, :, :], t["wo"])
        load("a1", cs[:, :, :], t["c_rope"])
        load("a1", w1s[:, :], t["w1s"])
        load("a1", w1k[:, :], t["w1k"])
        load("a1", w2b[:, :], t["w2b"])
        load("a1", b1c[:, :], t["b1c"])
        load("a1", b2r[:, :], t["b2r"])
        load("a1", pa[:, 0:1], t["lp_c"])
        load("a1", pa[:, 1:2], t["la_c"])
        load("a1", pab[:, :, :], t["pab"])
        load("a1", b2b[:, :], t["b2b"])

        k_ones = ms(dve, ones[:, :], 1.0)
        k_idb = cp(dve, idb[:, :], idf[:, :], [got("id")])
        k_idf = got("id")
        k_sel = cp(dve, sel[:, :, :].rearrange("p b n -> p (b n)"), wk(23000, 1024)[0:48, :], [got("cst")])

        def split(hi, lo, src, after, lane):
            a = af(hi, src, ACT.Copy, after)
            return tt(lane, lo, src, hi, ALU.subtract, [a, *after])

        k_gate = split(wg_h, wg_l, s_gate, [got("w13")], dve)
        k_w13 = split(w13_h, w13_l, s_w13, [got("w13")], dve)
        k_wv = split(wv_h, wv_l, s_wv, [got("a0")], pool)
        k_gu = split(wgu_h[:, :], wgu_l[:, :], s_gu, [got("f1")], pool)
        k_de = split(de_h[:, :], de_l[:, :], s_de, [got("f1")], pool)

        def fold(dst_h, dst_l, lefts, rights, n, after, ring):
            done = []
            for q in range(n):
                bk = ring.next()
                w = bk.take()
                for j in range(4):
                    m = mm(bk.ap[:, 128 * j:128 * j + 128], lefts[4 * q + j], rights[4 * q + j], True, True,
                           [*after, *w], j == 3)
                h, l = dst_h[:, 512 * q:512 * q + 512], dst_l[:, 512 * q:512 * q + 512]
                a = af(h, bk.ap[:, :], ACT.Copy, [m])
                d = tt(dve, l, bk.ap[:, :], h, ALU.subtract, [a, m])
                bk.free = [d]
                done.append(d)
            return done[-1]

        mv = small[:, 0:32].rearrange("p (t s) -> p t s", s=2)
        rs = small[:, 32:96].rearrange("p (k t) -> p k t", t=16)
        bst = small[:, 96:192].rearrange("p (t s) -> p t s", s=6)
        XH = [Slot(sb(f"xhat{i}", [128, 4, 128])) for i in range(2)]
        xh_ring = Ring(XH)
        xt_free = []
        EPS = 1e-5

        def layernorm(x_ready, banks):
            nonlocal xt_free
            xt_wait, xt_free = xt_free, []
            done = []
            ring = Ring(banks)
            for c in range(4):
                r = slice(4 * c, 4 * c + 4)
                for i in range(4 * c, 4 * c + 4):
                    b = dve.add(lambda e, i=i: e.bn_stats(bst[:, i, :], x[:, i, :]), x_ready[c])
                for i in range(4 * c, 4 * c + 4):
                    a = dve.add(lambda e, i=i: e.bn_aggr(mv[:, i, :], bst[:, i, :]), [b])
                v = ts(dve, rs[:, 0, r], mv[:, r, 1], EPS, None, ALU.add, after=[a])
                s = af(rs[:, 1, r], rs[:, 0, r], ACT.Sqrt, [v])
                i0 = dve.add(lambda e, r=r: e.reciprocal(rs[:, 2, r], rs[:, 1, r]), [s])
                n1 = tt(dve, rs[:, 1, r], rs[:, 2, r], rs[:, 2, r], ALU.mult, [i0])
                n2 = tt(dve, rs[:, 1, r], rs[:, 1, r], rs[:, 0, r], ALU.mult, [n1])
                n3 = ts(dve, rs[:, 1, r], rs[:, 1, r], -0.5, 1.5, ALU.mult, ALU.add, [n2])
                n4 = tt(dve, rs[:, 2, r], rs[:, 2, r], rs[:, 1, r], ALU.mult, [n3])
                xs = xh_ring.next()
                w = xs.take()
                for j in range(4):
                    i = 4 * c + j
                    h = ts(dve, xs.ap[:, j, :], x[:, i, :], mv[:, i, 0:1], rs[:, 2, i:i + 1], ALU.subtract,
                           ALU.mult, [n4, *w])
                bk = ring.next()
                w = bk.take()
                for j in range(4):
                    m = tp(bk.ap[:, 128 * j:128 * j + 128], xs.ap[:, j, :], idf[:, :], [h, k_idf, *w], j == 3)
                xs.free = [m]
                s_ = slice(512 * c, 512 * c + 512)
                a = af(xth[:, s_], bk.ap[:, :], ACT.Copy, [m, *xt_wait])
                d = tt(dve, xtl[:, s_], bk.ap[:, :], xth[:, s_], ALU.subtract, [a, m, *xt_wait])
                bk.free = [d]
                done.append(d)
            return done

        def proj_t(o_, wh, wl, c, after, mark=True):
            s_ = slice(512 * c, 512 * c + 512)
            mm(o_, wh, xth[:, s_], True, False, after)
            mm(o_, wh, xtl[:, s_], False, False)
            return mm(o_, wl, xth[:, s_], False, True, mark=mark)

        def proj_n(o_, wh, wl, i, after, mark=True):
            s_ = slice(128 * i, 128 * i + 128)
            mm(o_, xth[:, s_], wh, True, False, after)
            mm(o_, xth[:, s_], wl, False, False)
            return mm(o_, xtl[:, s_], wh, False, True, mark=mark)

        spl = small[:, 192:576].bitcast(BF16).rearrange("p (t k e) -> p t k e", t=16, k=3)
        rem = small[:, 576:832].rearrange("p (t e) -> p t e", t=16)
        ct_free = []

        def spread(src, tiles, after, bk):
            nonlocal ct_free
            r = slice(tiles[0], tiles[-1] + 1)
            a = cp(dve, spl[:, r, 0, :], src, after)
            b = tt(dve, rem[:, r, :], src, spl[:, r, 0, :], ALU.subtract, [a, *after])
            a = cp(dve, spl[:, r, 1, :], rem[:, r, :], [b])
            b = tt(dve, spl[:, r, 2, :], rem[:, r, :], spl[:, r, 1, :], ALU.subtract, [a])
            done = []
            for q in range(len(tiles) // 4):
                w = bk.take()
                v = bk.ap[0:48, 0:256].bitcast(BF16)
                for j in range(4):
                    i = tiles[4 * q + j]
                    m = tp(v[:, 128 * j:128 * j + 128], spl[:, i, :, :].rearrange("p k e -> p (k e)"), idb[:, :],
                           [b, k_idb, *w], j == 3)
                s_ = slice(128 * tiles[4 * q], 128 * tiles[4 * q] + 512)
                d = cp(dve, ctb[:, s_], v, [m, *ct_free])
                bk.free = [d]
                done.append(d)
            ct_free = []
            return done

        def ffn0(x_ready):
            nonlocal ct_free, xt_free
            H = [Slot(wk(4608 * i, 4608).rearrange("p (b n) -> p b n", b=9)) for i in range(2)]
            SG = Ring([Slot(wk(9216 + 512 * i, 512)) for i in range(3)])
            HU = Ring([Slot(wk(10752 + 512 * i, 512)) for i in range(3)])
            xt = layernorm(x_ready, [PS[7], PS[6]])
            G = wk(12288, 1600)
            S = G[:, 0:256].rearrange("p (t e) -> p t e", t=16)
            S4 = G[:, 0:256].rearrange("p (t g e) -> p t g e", t=16, g=4)
            A1 = G[:, 256:384].rearrange("p (t g e) -> p t g e", t=16, g=4)
            A2 = G[:, 384:512].rearrange("p (t g e) -> p t g e", t=16, g=4)
            g1 = G[:, 512:576].rearrange("p (t g) -> p t g", t=16)
            g2 = G[:, 576:640].rearrange("p (t g) -> p t g", t=16)
            g3 = G[:, 640:704].rearrange("p (t g) -> p t g", t=16)
            q1 = G[:, 704:960].rearrange("p (t g e) -> p t g e", t=16, g=4)
            q2 = G[:, 960:1216].rearrange("p (t g e) -> p t g e", t=16, g=4)
            q2f = G[:, 960:1216].rearrange("p (t e) -> p t e", t=16)
            q1f = G[:, 704:960].rearrange("p (t e) -> p t e", t=16)
            m8 = G[:, 1216:1344].rearrange("p (t e) -> p t e", t=16)
            w1_ = G[:, 1344:1360]
            gb = PS[5]
            w = gb.take()
            for i in range(16):
                m = proj_n(gb.ap[:, 16 * i:16 * i + 16], wg_h, wg_l, i, [xt[i // 4], k_gate, *w], i == 15)
            z = af(G[:, 0:256], gb.ap[:, 0:256], ACT.Sigmoid, [m, *work_free])
            gb.free = [z]
            a = tt(dve, A1, S4[:, :, :, 0:2], S4[:, :, :, 2:4], ALU.max, [z])
            b = tt(dve, A2, S4[:, :, :, 0:2], S4[:, :, :, 2:4], ALU.min, [z])
            c_ = tt(dve, g1, A1[:, :, :, 0], A1[:, :, :, 1], ALU.max, [a])
            d = tt(dve, g2, A1[:, :, :, 0], A1[:, :, :, 1], ALU.min, [a])
            f = tt(dve, g3, A2[:, :, :, 0], A2[:, :, :, 1], ALU.max, [b])
            f = tt(dve, g2, g2, g3, ALU.max, [d, f])
            f = tt(dve, g1, g1, g2, ALU.add, [c_, f])
            other = g1.unsqueeze(2).to_broadcast([128, 16, 4, 4])
            own = g1.unsqueeze(3).to_broadcast([128, 16, 4, 4])
            a = tt(dve, q1, other, own, ALU.is_gt, [f])
            b = tt(dve, q2, other, own, ALU.is_equal, [f])
            trb = tri[:, :, :].unsqueeze(1).to_broadcast([128, 16, 4, 4])
            b = tt(dve, q2, q2, trb, ALU.mult, [b, got("cst")])
            b = tt(dve, q1, q1, q2, ALU.add, [a, b])
            b = red(g2, q1, ALU.add, [b])
            b = ts(dve, g2, g2, 1.5, None, ALU.is_lt, after=[b])
            al = g2.unsqueeze(3).to_broadcast([128, 16, 4, 4])
            a = tt(dve, q1, S4, al, ALU.mult, [b])
            b = ts(dve, g3, g2, -1.0, None, ALU.add, after=[b])
            am = g3.unsqueeze(3).to_broadcast([128, 16, 4, 4])
            a = tt(dve, q1, q1, am, ALU.add, [a, b])
            for i in range(16):
                b = dve.add(lambda e, i=i: e.max(m8[:, i, :], q1f[:, i, :]), [a])
            thr = m8[:, :, 3:4].to_broadcast([128, 16, 16])
            b = tt(dve, q2f, q1f, thr, ALU.is_ge, [b])
            b = tt(dve, q2f, q2f, S, ALU.mult, [b])
            a = red(w1_, q2f, ALU.add, [b])
            a = ts(dve, w1_, w1_, 1e-6, None, ALU.add, after=[a])
            a = dve.add(lambda e: e.reciprocal(w1_, w1_), [a])
            a = tt(dve, q2f, q2f, w1_.unsqueeze(2).to_broadcast([128, 16, 16]), ALU.mult, [a, b])
            ct = spread(q2f, list(range(16)), [a], PS[7])

            gr, ur, cr = Ring([PS[0], PS[1]]), Ring([PS[2], PS[3]]), Ring([PS[4], PS[5]])
            x_done = []

            def up(c):
                hs = H[c % 2]
                hw = hs.take()
                done = []
                for b_ in range(9):
                    g_, u_ = gr.next(), ur.next()
                    mg = proj_t(g_.ap[:, :], w13_h[:, 128 * b_:128 * b_ + 128], w13_l[:, 128 * b_:128 * b_ + 128], c,
                                [xt[c], k_w13, *g_.take()])
                    n = 1152 + 128 * b_
                    mu = proj_t(u_.ap[:, :], w13_h[:, n:n + 128], w13_l[:, n:n + 128], c, u_.take())
                    sg = SG.next()
                    z = af(sg.ap, g_.ap[:, :], ACT.Silu, [mg, *sg.take(), *work_free])
                    g_.free = [z]
                    if b_ == 8:
                        f = tt(dve, hs.ap[:, b_, :], sg.ap, u_.ap[:, :], ALU.mult, [z, mu, *hw, *work_free])
                        sg.free = [f]
                        u_.free = [f]
                    else:
                        k_ = cr.next()
                        mc = mm(k_.ap[:, :], sel[:, b_, :], ctb[:, 512 * c:512 * c + 512], True, True,
                                [ct[c], k_sel, *k_.take()], True)
                        hu = HU.next()
                        y = tt(dve, hu.ap, sg.ap, u_.ap[:, :], ALU.mult, [z, mu, *hu.take(), *work_free])
                        sg.free = [y]
                        u_.free = [y]
                        f = tt(dve, hs.ap[:, b_, :], hu.ap, k_.ap[:, :], ALU.mult, [y, mc, *hw])
                        hu.free = [f]
                        k_.free = [f]
                    done.append(f)
                return done[-1]

            def down(c, h_done):
                bk = PS[6]
                w = bk.take()
                for j in range(4):
                    for b_ in range(9):
                        m = mm(bk.ap[:, 128 * j:128 * j + 128], H[c % 2].ap[:, b_, 128 * j:128 * j + 128], w2[:, b_, :],
                               b_ == 0, b_ == 8, [h_done, got("w2"), *w], j == 3 and b_ == 8)
                H[c % 2].free = [m]
                xv = x[:, 4 * c:4 * c + 4, :].rearrange("p t d -> p (t d)")
                f = stt(xv, bk.ap[:, :], 0.5, xv, ALU.mult, ALU.add, [m])
                bk.free = [f]
                x_done.append([f])
                return m

            hd = [None] * 4
            for c in range(5):
                if c < 4:
                    hd[c] = up(c)
                if c > 0:
                    m = down(c - 1, hd[c - 1])
            xt_free = [m]
            ct_free = [m]
            return x_done, [m, x_done[-1][0]]

        def attn0(x_ready):
            nonlocal ct_free, xt_free
            PK = wk(0, 4096).rearrange("p (t n) -> p t n", t=4)
            VV = wk(4096, 4096).rearrange("p (t n) -> p t n", t=4)
            PQ = wk(8192, 4096).rearrange("p (b n) -> p b n", b=8)
            KVT = wk(12288, 1024).rearrange("p (b n) -> p b n", b=8)
            KW = wk(13312, 1024).rearrange("p (b n) -> p b n", b=8)
            KS = wk(14336, 16).rearrange("p (b n) -> p b n", b=8)
            NR = wk(14352, 64).rearrange("p (t e) -> p t e", t=4)
            xt = layernorm(x_ready, [PS[7], PS[6]])
            z1 = ms(dve, KVT, 0.0, work_free)
            z1 = ms(dve, KS, 0.0, work_free)
            x_done = []
            ring = Ring([PS[0], PS[1], PS[2], PS[3]])
            kw_free, kv_free, pk_free, pq_free, nr_free, ks_free = [], [z1], [], [], [], [z1]
            for c in range(4):
                ev, evp = [], []
                for j in range(4):
                    for n in range(2):
                        s_ = slice(512 * n, 512 * n + 512)
                        bk = ring.next()
                        m = proj_n(bk.ap[:, :], wkr_h[:, s_], wkr_l[:, s_], 4 * c + j, [xt[c], k_fold0, *bk.take()])
                        a = af(PK[:, j, s_], bk.ap[:, :], ACT.Relu, [m, *pk_free, *work_free])
                        bk.free = [a]
                        bk = ring.next()
                        m = proj_n(bk.ap[:, :], wv_h[:, s_], wv_l[:, s_], 4 * c + j, [k_wv, *bk.take()])
                        b = cp(dve, VV[:, j, s_], bk.ap[:, :], [m, *pk_free, *work_free])
                        bk.free = [b]
                        ev, evp = [a], [b]
                pq = []
                for p in range(8):
                    bk = ring.next()
                    m = proj_t(bk.ap[:, :], wq_h[:, 128 * p:128 * p + 128], wq_l[:, 128 * p:128 * p + 128], c,
                               bk.take())
                    if p % 2:
                        a = af(PQ[:, p, :], bk.ap[:, :], ACT.Relu, [m, *pq_free, *work_free])
                    else:
                        a = ts(dve, PQ[:, p, :], bk.ap[:, :], 0.0, None, ALU.max, after=[m, *pq_free, *work_free])
                    bk.free = [a]
                    pq.append(a)
                kb = PS[5]
                w = kb.take()
                for p in range(8):
                    for j in range(4):
                        m = mm(kb.ap[:, p:p + 1], PK[:, j, 128 * p:128 * p + 128], ones[:, 0:1], j == 0, j == 3,
                               [*ev, k_ones, *w], p == 7 and j == 3)
                a = cp(dve, KS[0:64, :, 0], kb.ap[0:64, 0:8], [m, *ks_free])
                ks = cp(dve, KS[64:128, :, 1], kb.ap[64:128, 0:8], [m, *ks_free])
                kb.free = [ks]
                kd = []
                for q in range(2):
                    bk = PS[6 + q]
                    w = bk.take()
                    for u in range(4):
                        p = 4 * q + u
                        for j in range(4):
                            m = mm(bk.ap[:, 128 * u:128 * u + 128], VV[:, j, 128 * p:128 * p + 128],
                                   PK[:, j, 128 * p:128 * p + 128], j == 0, j == 3, [*ev, *evp, *w], u == 3 and j == 3)
                    bv = bk.ap[:, :].rearrange("p (b n) -> p b n", b=4)
                    a = cp(dve, KVT[0:64, 4 * q:4 * q + 4, 0:64], bv[0:64, :, 0:64], [m, *kv_free])
                    b = cp(dve, KVT[64:128, 4 * q:4 * q + 4, 64:128], bv[64:128, :, 64:128], [m, *kv_free])
                    bk.free = [b]
                    kd.append(b)
                pk_free = [m]
                nb = PS[4]
                w = nb.take()
                for j in range(4):
                    for p in range(8):
                        m = mm(nb.ap[:, 16 * j + 2 * p:16 * j + 2 * p + 2], PQ[:, p, 128 * j:128 * j + 128], KS[:, p, :],
                               True, True, [pq[6], pq[7], ks, *w], j == 3 and p == 7)
                ks_free = [m]
                NRf = NR.rearrange("p t e -> p (t e)")
                a = ts(dve, NRf, nb.ap[:, 0:64], 1e-6, None, ALU.add, after=[m, *nr_free])
                nb.free = [a]
                a = dve.add(lambda e: e.reciprocal(NRf, NRf), [a])
                kw = []
                for q in range(2):
                    bk = PS[6 + q]
                    w = bk.take()
                    for u in range(4):
                        p = 4 * q + u
                        m = mm(bk.ap[:, 128 * u:128 * u + 128], KVT[:, p, :], wout[:, p, :], True, True,
                               [kd[q], got("a0"), *w], u == 3)
                    b = af(KW[:, 4 * q:4 * q + 4, :].rearrange("p b n -> p (b n)"), bk.ap[:, :], ACT.Copy,
                           [m, *kw_free])
                    bk.free = [b]
                    kw.append(b)
                kv_free = [m]
                ct = spread(NR, list(range(4 * c, 4 * c + 4)), [a], PS[5])
                nr_free = [ct[0]]
                for p in range(8):
                    bk = ring.next()
                    m = mm(bk.ap[:, :], sel[:, p, :], ctb[:, 512 * c:512 * c + 512], True, True,
                           [ct[0], *bk.take()], True)
                    b = tt(dve, PQ[:, p, :], PQ[:, p, :], bk.ap[:, :], ALU.mult, [m, pq[p]])
                    bk.free = [b]
                ct_free = [m]
                bk = PS[4]
                w = bk.take()
                for j in range(4):
                    o_ = bk.ap[:, 128 * j:128 * j + 128]
                    mm(o_, ones[0:1, :], rows[0:1, 0:128], True, False, [got("f1"), *w])
                    for p in range(8):
                        m = mm(o_, PQ[:, p, 128 * j:128 * j + 128], KW[:, p, :], False, p == 7, [b, *kw],
                               j == 3 and p == 7)
                pq_free = [m]
                kw_free = [m]
                xv = x[:, 4 * c:4 * c + 4, :].rearrange("p t d -> p (t d)")
                f = tt(dve, xv, bk.ap[:, :], xv, ALU.add, [m])
                bk.free = [f]
                x_done.append([f])
            xt_free = [m]
            return x_done, [m, f]

        def ffn1(x_ready):
            nonlocal xt_free
            PT = wk(0, 8192).rearrange("p (b n) -> p b n", b=4)
            HF = [Slot(wk(8192 + 4096 * i, 4096).rearrange("p (b n) -> p b n", b=8)) for i in range(2)]
            SG = Ring([Slot(wk(16384 + 512 * i, 512)) for i in range(2)])
            SM = Ring([Slot(wk(17408 + 512 * i, 512)) for i in range(2)])
            DD = Ring([Slot(wk(18432 + 2048 * i, 2048)) for i in range(1)])
            EE = Ring([Slot(wk(20480 + 512 * i, 512)) for i in range(3)])
            PP = Ring([Slot(wk(22016 + 512 * i, 512)) for i in range(2)])
            TK = Ring([Slot(wk(23040 + 400 * i, 400)) for i in range(2)])
            xt = layernorm(x_ready, [PS[7], PS[6]])
            sr, tr = Ring([PS[0], PS[1]]), Ring([PS[2], PS[3]])
            ptd = []
            pend = []

            def back(i, pp, f):
                bk = tr.next()
                w = bk.take()
                for q in range(4):
                    m = tp(bk.ap[:, 128 * q:128 * q + 128], pp.ap[:, 128 * q:128 * q + 128], idf[:, :], [f, *w], q == 3)
                pp.free = [m]
                a = af(PT[:, :, 128 * i:128 * i + 128], bk.ap[:, :].rearrange("p (b n) -> p b n", b=4), ACT.Copy,
                       [m, *work_free])
                bk.free = [a]
                ptd.append(a)

            for i in range(16):
                bk = sr.next()
                m = proj_n(bk.ap[:, :], wk_h[:, :], wk_l[:, :], i, [xt[i // 4], k_fold1, *bk.take()])
                sm = SM.next()
                a = af(sm.ap, bk.ap[:, :], ACT.Copy, [m, *sm.take(), *work_free])
                bk.free = [a]
                sv = sm.ap.rearrange("p (s h k) -> p s h k", s=2, h=4)
                tk = TK.next()
                w = [*tk.take(), *work_free]
                top = tk.ap[:, 0:64].rearrange("p (s h k) -> p s h k", s=2, h=4)
                cb = tk.ap[:, 64:320].rearrange("p (h a b) -> p h a b", h=4, a=8)
                cbf = tk.ap[:, 64:320].rearrange("p (h n) -> p h n", h=4)
                v8 = tk.ap[:, 320:352].rearrange("p (h k) -> p h k", h=4)
                e8 = tk.ap[:, 352:384].rearrange("p (h k) -> p h k", h=4)
                nm = tk.ap[:, 384:388]
                zz = tk.ap[:, 388:392]
                acc = tk.ap[:, 392:393]
                dd = DD.next()
                Dv = dd.ap.rearrange("p (h x y) -> p h x y", h=4, x=8)
                xb = sv[:, 0, :, 0:8].unsqueeze(3).to_broadcast([128, 4, 8, 64])
                yb = sv[:, 1, :, :].unsqueeze(2).to_broadcast([128, 4, 8, 64])
                dw = [a, *dd.take(), *work_free]
                dh = [tt(pool, Dv[:, h_], xb[:, h_], yb[:, h_], ALU.add, dw) for h_ in range(4)]
                for s_ in range(2):
                    for h_ in range(4):
                        b = dve.add(lambda e, s_=s_, h_=h_, top=top, sv=sv: e.max(top[:, s_, h_, :], sv[:, s_, h_, :]),
                                    [a, *w])
                b = tt(dve, cb, top[:, 0].unsqueeze(3).to_broadcast([128, 4, 8, 8]),
                       top[:, 1].unsqueeze(2).to_broadcast([128, 4, 8, 8]), ALU.add, [b])
                for h_ in range(4):
                    b = dve.add(lambda e, h_=h_, v8=v8, cbf=cbf: e.max(v8[:, h_, :], cbf[:, h_, :]), [b])
                n_ = ts(dve, nm, v8[:, :, 0], -1.0, None, ALU.mult, after=[b])
                b = tt(dve, e8, v8, nm.unsqueeze(2).to_broadcast([128, 4, 8]), ALU.add, [n_])
                z = af(tk.ap[:, 352:384], tk.ap[:, 352:384], ACT.Exp, [b])
                es = []
                for h_ in range(4):
                    ee = EE.next()
                    y = af(ee.ap, dd.ap[:, 512 * h_:512 * h_ + 512], ACT.Exp, [dh[h_], n_, *ee.take(), *work_free],
                           bias=nm[:, h_:h_ + 1])
                    es.append((ee, y))
                    if h_ == 0:
                        b = red(zz, e8, ALU.add, [z])
                        rz = dve.add(lambda e, zz=zz: e.reciprocal(zz, zz), [b])
                        pp = PP.next()
                        pw = [*pp.take(), *work_free]
                    f = stt(ee.ap, dd.ap[:, 512 * h_:512 * h_ + 512], v8[:, h_, 7:8], ee.ap, ALU.is_ge, ALU.mult,
                            [y])
                    if h_ == 0:
                        p_ = ts(dve, pp.ap, ee.ap, zz[:, 0:1], None, ALU.mult, after=[f, rz, *pw])
                    elif h_ < 3:
                        p_ = stt(pp.ap, ee.ap, zz[:, h_:h_ + 1], pp.ap, ALU.mult, ALU.add, [f, p_])
                    else:
                        p_ = stt(pp.ap, ee.ap, zz[:, h_:h_ + 1], pp.ap, ALU.mult, ALU.add, [f, p_], accum_out=acc)
                    ee.free = [p_]
                dd.free = [f]
                f = ts(dve, pp.ap[:, 511:512], pp.ap[:, 511:512], acc, 4.0, ALU.subtract, ALU.add, [p_])
                tk.free = [f]
                sm.free = [f, dh[3]]
                pend.append((i, pp, f))
                if len(pend) > 1:
                    back(*pend.pop(0))
            back(*pend.pop(0))

            gr, ur = Ring([PS[0], PS[1]]), Ring([PS[4], PS[5]])
            x_done = []

            def up(c):
                hs = HF[c % 2]
                hw = [*hs.take(), *work_free]
                for b_ in range(4):
                    g_, u_ = gr.next(), ur.next()
                    n = 128 * b_
                    mg = proj_t(g_.ap[:, :], wgu_h[:, n:n + 128], wgu_l[:, n:n + 128], c, [xt[c], k_gu, *g_.take()])
                    mu = proj_t(u_.ap[:, :], wgu_h[:, 512 + n:640 + n], wgu_l[:, 512 + n:640 + n], c, u_.take())
                    sg = SG.next()
                    z = af(sg.ap, g_.ap[:, :], ACT.Silu, [mg, got("f1"), *sg.take(), *work_free],
                           bias=bgu[:, b_:b_ + 1])
                    g_.free = [z]
                    f = stt(hs.ap[:, b_, :], u_.ap[:, :], bgu[:, 4 + b_:5 + b_], sg.ap, ALU.add, ALU.mult,
                            [z, mu, *hw])
                    sg.free = [f]
                    u_.free = [f]
                for b_ in range(4):
                    g_ = gr.next()
                    n = 128 * b_
                    mg = proj_t(g_.ap[:, :], de_h[:, n:n + 128], de_l[:, n:n + 128], c, [k_de, *g_.take()])
                    sg = SG.next()
                    z = af(sg.ap, g_.ap[:, :], ACT.Silu, [mg, *sg.take(), *work_free])
                    g_.free = [z]
                    f = tt(dve, hs.ap[:, 4 + b_, :], PT[:, b_, 512 * c:512 * c + 512], sg.ap, ALU.mult,
                           [z, ptd[4 * c + 3], *hw])
                    sg.free = [f]
                return f

            def down(c, h_done):
                bk = PS[6]
                w = bk.take()
                for j in range(4):
                    o_ = bk.ap[:, 128 * j:128 * j + 128]
                    mm(o_, ones[0:1, :], rows[0:1, 128:256], True, False, [got("f1"), k_ones, *w])
                    for b_ in range(8):
                        m = mm(o_, HF[c % 2].ap[:, b_, 128 * j:128 * j + 128], wdue[:, b_, :], False, b_ == 7,
                               [h_done], j == 3 and b_ == 7)
                HF[c % 2].free = [m]
                xv = x[:, 4 * c:4 * c + 4, :].rearrange("p t d -> p (t d)")
                f = stt(xv, bk.ap[:, :], 0.5, xv, ALU.mult, ALU.add, [m])
                bk.free = [f]
                x_done.append([f])
                return m

            hd = [None] * 4
            for c in range(5):
                if c < 4:
                    hd[c] = up(c)
                if c > 0:
                    m = down(c - 1, hd[c - 1])
            xt_free = [m]
            return x_done, [m, x_done[-1][0], dh[3]]

        def tables1():
            w = [*work_free, got("a1"), got("dst")]
            dn = wk(0, 512)
            dt_ = wk(512, 640)
            tmp = wk(1152, 8192).rearrange("p (h v) -> p h v", h=16)
            z = af(pa[:, 0:2], pa[:, 0:2], ACT.Exp, w)
            z = af(pab[:, :, :], pab[:, :, :], ACT.Exp, w)
            z = af(pa[:, 0:2], pa[:, 0:2], ACT.Ln, [z], bias=1.0)
            z = af(pab[:, :, :], pab[:, :, :], ACT.Ln, [z], bias=1.0)
            a = af(ktab[:, :], dt_, ACT.Ln, [z, *w], scale=pa[:, 1:2], bias=1.0)
            n0 = ts(dve, pa[:, 2:3], pa[:, 0:1], -1.0, None, ALU.mult, after=[z])
            n1 = ts(dve, pab[:, 0, :], pab[:, 0, :], -1.0, None, ALU.mult, after=[z])
            k1 = ts(dve, ktab[:, :], ktab[:, :], pa[:, 2:3], None, ALU.mult, after=[a, n0])
            for h in range(16):
                a = af(tmp[:, h, :], dn, ACT.Ln, [z, *w], scale=pab[:, 1, h:h + 1], bias=1.0)
                k2 = ts(dve, kn[:, h, :], tmp[:, h, :], pab[:, 0, h:h + 1], b2b[:, h:h + 1], ALU.mult, ALU.add,
                        [a, n1, *reg0_free])
            d = tt(dve, w1k[:, :], w1k[:, :], w1s[:, :], ALU.subtract, [got("a1")])
            bk = PS[5]
            m = mm(bk.ap[:, 0:1], w1s[0:64, :], b2r[:, :], True, True, [got("a1"), *bk.take()], True)
            e = tt(dve, b1c[:, :], b1c[:, :], bk.ap[:, 0:1], ALU.subtract, [m])
            bk.free = [e]
            return [k1, k2, d, e]

        def attn1(x_ready):
            nonlocal xt_free
            tabs = tables1()
            FL = wk(0, 8192)
            F = FL.rearrange("p (a h b) -> p a h b", h=16, b=4)
            QT = wk(8192, 4096).rearrange("p (b n) -> p b n", b=8)
            KT = wk(12288, 4096).rearrange("p (b n) -> p b n", b=8)
            vx = sb("vx", [128, 2, 16, 65])
            VX = [vx[:, 0], vx[:, 1]]
            VX += [wk(22016 + 1040 * i, 1040).rearrange("p (h d) -> p h d", h=16) for i in range(2)]
            TB = Ring([Slot(wk(16384 + 512 * i, 512)) for i in range(3)])
            GB = Ring([Slot(wk(17920 + 1024 * i, 1024)) for i in range(3)])
            OO = wk(20992, 1024)
            mx = small[:, 832:848]
            rd = small[:, 848:864]
            xt = layernorm(x_ready, [PS[7], PS[6]])
            for v in VX:
                v1 = ms(dve, v[:, :, 64:65], 1.0, work_free)
            x_done = []
            qk = Ring([PS[0], PS[1]])
            tr = Ring([PS[2], PS[3]])
            gp = Ring([(PS[4], PS[5]), (PS[6], PS[7])])
            wf = [*work_free, *tabs]
            qt_free, vx_free, f_free, oo_free, mx_free = [], [], [], [], []
            ident = idf[:, :]
            for c in range(4):
                pr = Ring([PS[0], PS[1], PS[4], PS[5]])
                for p in range(8):
                    for off, dst in ((0, QT), (2048, KT)):
                        b0, b1 = pr.next(), pr.next()
                        n = off + 128 * p
                        m0 = proj_t(b0.ap[:, :], wa_h[:, n:n + 128], wa_l[:, n:n + 128], c, [xt[c], *k_wa, *b0.take()])
                        n += 1024
                        m1 = proj_t(b1.ap[:, :], wa_h[:, n:n + 128], wa_l[:, n:n + 128], c, b1.take())
                        rt = GB.next()
                        ra, rb = rt.ap[:, 0:512], rt.ap[:, 512:1024]
                        a = tt(dve, ra, b0.ap[:, :], cs[:, 0, :], ALU.mult, [m0, got("a1"), *rt.take(), *wf])
                        b = tt(dve, rb, b1.ap[:, :], cs[:, 1, :], ALU.mult, [m1])
                        b0.free = [a]
                        b1.free = [b]
                        q_ = tt(pool, dst[:, p, :], ra, rb, ALU.add, [a, b, *qt_free, *wf])
                        rt.free = [q_]
                for j in range(4):
                    for n in range(2):
                        bk = pr.next()
                        s_ = slice(4096 + 512 * n, 4096 + 512 * n + 512)
                        m = proj_n(bk.ap[:, :], wa_h[:, s_], wa_l[:, s_], 4 * c + j, bk.take())
                        v_ = af(VX[j][:, 8 * n:8 * n + 8, 0:64], bk.ap[:, :].rearrange("p (h d) -> p h d", h=8),
                                ACT.Copy, [m, *vx_free])
                        bk.free = [v_]
                for it in range(4):
                    J = 128 * (it + 1)
                    i0 = 128 * it
                    for h in range(16):
                        bk = qk.next()
                        r = slice(64 * (h % 2), 64 * (h % 2) + 64)
                        m = mm(bk.ap[:, 0:J], QT[r, h // 2, i0:i0 + 128], KT[r, h // 2, 0:J], True, True,
                               [q_, *bk.take()], True)
                        s0 = stt(F[:, 0:J // 4, h, :], bk.ap[:, 0:J].rearrange("p (a b) -> p a b", b=4), 0.125, kn[:, h, 512 - J:512].rearrange("p (a b) -> p a b", b=4), ALU.mult, ALU.add,
                                 [m, *f_free, *wf])
                        bk.free = [s0]
                    wr = Ring([PS[0], PS[1]])
                    adds = []

                    def stage_a(q):
                        tb, bk = TB.next(), tr.next()
                        w = bk.take()
                        for g in range(4):
                            j0 = 32 * q + 8 * g
                            m_ = tp(bk.ap[:, 128 * g:128 * g + 128], FL[:, 16 * j0:16 * j0 + 128], ident, [s0, *w], g == 3)
                        a_ = af(tb.ap, bk.ap[:, :], ACT.Copy, [m_, *tb.take()])
                        bk.free = [a_]
                        return tb, a_, m_

                    def stage_b(q, tb, a_):
                        ba, bb = gp.next()
                        w = [*ba.take(), *bb.take()]
                        for g in range(4):
                            j0 = 32 * q + 8 * g
                            s_ = slice(128 * g, 128 * g + 128)
                            u = 128 + i0 - j0
                            for k_, bnk in enumerate((ba, bb)):
                                r = slice(64 * k_, 64 * k_ + 64)
                                mm(bnk.ap[:, s_], w1s[r, :], tb.ap[r, s_], True, False, [a_, *w, *tabs])
                            for k_, bnk in enumerate((ba, bb)):
                                r = slice(64 * k_, 64 * k_ + 64)
                                u_ = u - 4 * k_
                                m_ = mm(bnk.ap[:, s_], w1k[r, :], ktab[r, u_:u_ + 128], False, True, (),
                                        g == 3 and k_ == 1)
                        tb.free = [m_]
                        gb = GB.next()
                        w = [m_, *gb.take()]
                        z0 = af(gb.ap[:, 0:512], ba.ap[:, :], ACT.Gelu, w, bias=b1c[:, 0:1])
                        z1_ = af(gb.ap[:, 512:1024], bb.ap[:, :], ACT.Gelu, w, bias=b1c[:, 0:1])
                        ba.free = [z0]
                        bb.free = [z1_]
                        return gb, z1_

                    def stage_c(q, gb, z_):
                        bk = wr.next()
                        w = bk.take()
                        for k_ in range(2):
                            for g in range(4):
                                n_ = 128 * g + 64 * k_
                                m_ = mm(bk.ap[:, n_:n_ + 64], gb.ap[:, 512 * k_ + 128 * g:512 * k_ + 128 * g + 128],
                                        w2b[:, :], True, True, [z_, *w], k_ == 1 and g == 3)
                        gb.free = [m_]
                        fv = FL[:, 512 * q:512 * q + 512]
                        f_ = tt(dve, fv, fv, bk.ap[:, :], ALU.add, [m_, ta[q]])
                        bk.free = [f_]
                        return f_

                    nq = 4 * (it + 1)
                    sa, sb_, ta = {}, {}, {}
                    for q in range(nq + 2):
                        if q < nq:
                            tb, a_, t_ = stage_a(q)
                            sa[q] = (tb, a_)
                            ta[q] = t_
                        if 1 <= q <= nq:
                            sb_[q - 1] = stage_b(q - 1, *sa[q - 1])
                        if q >= 2:
                            adds.append(stage_c(q - 2, *sb_[q - 2]))
                    dg = F[:, i0 // 4:J // 4, :, :]
                    k_ = pool.add(lambda e, dg=dg: e.affine_select(
                        out=dg, in_=dg, compare_op=ALU.is_ge, fill=-3.0e38, base=0, pattern=[[-4, 32], [0, 16], [-1, 4]],
                        channel_multiplier=1), [adds[-1]])
                    mxd = []
                    for hq in range(4):
                        hs = slice(4 * hq, 4 * hq + 4)
                        v = F[:, 0:J // 4, hs, :].rearrange("p a h b -> p h a b")
                        b = dve.add(lambda e, hs=hs, v=v: e.tensor_reduce(mx[:, hs], v, mybir.AxisListType.XY, ALU.max),
                                    [k_, adds[-1], *mx_free])
                        mxd.append(ts(dve, mx[:, hs], mx[:, hs], -1.0, None, ALU.mult, after=[b]))
                    pvb = [PS[4], PS[5], PS[6]]
                    w3 = [b_.take() for b_ in pvb]
                    pend = []

                    def pv(h, tbs):
                        bk = pvb[h // 7]
                        o_ = bk.ap[:, 65 * (h % 7):65 * (h % 7) + 65]
                        tb, a_ = tbs
                        for jt in range(it + 1):
                            m_ = mm(o_, tb.ap[:, 128 * jt:128 * jt + 128], VX[jt][:, h, :], jt == 0, jt == it,
                                    [a_, v_, v1, *w3[h // 7]], jt == it)
                        tb.free = [m_]
                        return m_

                    for h in range(16):
                        if h % 2 == 0:
                            gb = GB.next()
                            w = gb.take()
                        pb = gb.ap[:, 512 * (h % 2):512 * (h % 2) + J]
                        x_ = af(pb.rearrange("p (a b) -> p a b", b=4), F[:, 0:J // 4, h, :], ACT.Exp,
                                [mxd[h // 4], *w], bias=mx[:, h:h + 1])
                        bk, tb = tr.next(), TB.next()
                        w_ = bk.take()
                        for jt in range(it + 1):
                            m = tp(bk.ap[:, 128 * jt:128 * jt + 128], pb[:, 128 * jt:128 * jt + 128], ident,
                                   [x_, *w_], jt == it)
                        gb.free = [m]
                        a = cp(dve, tb.ap[:, 0:J], bk.ap[:, 0:J], [m, *tb.take()])
                        bk.free = [a]
                        pend.append((h, (tb, a)))
                        if len(pend) > 1:
                            pv(*pend.pop(0))
                    f_free = [x_]
                    mx_free = [x_]
                    m = pv(*pend.pop(0))
                    for q, (ha, hb) in enumerate(((0, 7), (7, 14), (14, 16))):
                        n = hb - ha
                        v = pvb[q].ap[:, 0:65 * n].rearrange("p (h d) -> p h d", h=n)
                        a = dve.add(lambda e, v=v, ha=ha, hb=hb: e.reciprocal(rd[:, ha:hb], v[:, :, 64]), [m])
                        o2 = OO[:, 64 * ha:64 * hb].rearrange("p (h d) -> p h d", h=n)
                        b = tt(dve, o2, v[:, :, 0:64], rd[:, ha:hb].unsqueeze(2).to_broadcast([128, n, 64]), ALU.mult,
                               [a, *oo_free])
                        pvb[q].free = [b]
                    tbs = []
                    for q in range(2):
                        bk, tb = tr.next(), TB.next()
                        w = bk.take()
                        for u in range(4):
                            n = 512 * q + 128 * u
                            m = tp(bk.ap[:, 128 * u:128 * u + 128], OO[:, n:n + 128], ident, [b, *w], u == 3)
                        a = af(tb.ap, bk.ap[:, :], ACT.Copy, [m, *tb.take()])
                        bk.free = [a]
                        tbs.append((tb, a))
                    oo_free = [m]
                    bk = PS[7]
                    w = bk.take()
                    for q in range(2):
                        tb, a = tbs[q]
                        for u in range(4):
                            m = mm(bk.ap[:, 0:128], tb.ap[:, 128 * u:128 * u + 128], wo[:, 4 * q + u, :],
                                   q == 0 and u == 0, q == 1 and u == 3, [a, *w], u == 3)
                        tb.free = [m]
                    xv = x[:, 4 * c + it, :]
                    f = tt(dve, xv, bk.ap[:, 0:128], xv, ALU.add, [m])
                    bk.free = [f]
                qt_free = [m]
                vx_free = [m]
                x_done.append([f])
            xt_free = [m]
            return x_done, [m, f]

        work_free, reg0_free = [], []
        k_rf = got("a0")
        fr = Ring([PS[1], PS[2]])
        fold(wq_h, wq_l, [s_qk[:, p, :] for p in range(8)], [s_rf[:, p, :] for p in range(8)], 2, [k_rf], fr)
        k_fold0 = fold(wkr_h, wkr_l, [s_qk[:, 8 + p, :] for p in range(8)], [s_rf[:, p, :] for p in range(8)], 2,
                       [k_rf], fr)
        k_fold1 = fold(wk_h, wk_l, [s_wqT[:, p, :] for p in range(4)], [s_key[:, p, :] for p in range(4)], 1,
                       [got("f1")], fr)

        xr, free = ffn0([[got(f"x{c}")] for c in range(4)])
        k_wa = []
        stage = Ring([Slot(wk(16400 + 1024 * i, 1024)) for i in range(5)])
        for i in range(5):
            s_ = stage.next()
            load(f"wa{i}", s_.ap, t["wa"][:, 1024 * i:1024 * i + 1024], [k_fold1, k_fold0, k_de, k_gu, k_wv])
            k_wa.append(split(wa_h[:, 1024 * i:1024 * i + 1024], wa_l[:, 1024 * i:1024 * i + 1024], s_.ap,
                              [got(f"wa{i}")], pool))
        work_free = free
        xr, free = attn0(xr)
        work_free = free
        xr, free = ffn0(xr)
        work_free = [*free, *k_wa]
        reg0_free = free
        xr, free = ffn1(xr)
        work_free = free
        load("dst", wk(0, 512), t["c_dn"], work_free)
        load("dst", wk(512, 640), t["c_dt"], work_free)
        xr, free = attn1(xr)
        work_free = free
        xr, free = ffn1(xr)
        od = out.rearrange("b (q p) d -> p (b q) d", p=128)
        s_out = sem("s_out")
        for c in range(4):
            sp.add(lambda e, c=c: e.dma_start(od[:, 4 * c:4 * c + 4, :], x[:, 4 * c:4 * c + 4, :]).then_inc(s_out, 16),
                   xr[c], False)
        sp.add(lambda e: e.wait_ge(s_out, 64), (), False)

        block = ctx.enter_context(nc.Block())

        @block.sync
        def _(e):
            sp.issue(e)

        @block.tensor
        def _(e):
            pe.issue(e)

        @block.scalar
        def _(e):
            act.issue(e)

        @block.vector
        def _(e):
            dve.issue(e)

        @block.gpsimd
        def _(e):
            pool.issue(e)


def _layout(i):
    import numpy as np
    f4 = np.float32
    g = {k: np.asarray(v) for k, v in i.items()}
    t = {"x": g["L0_attn_x"]}
    t["w_gate"] = g["L0_ffn_w_gate"].T
    t["w13"] = np.concatenate([g["L0_ffn_w1_e"].reshape(1024, 128), g["L0_ffn_w1_s"],
                               g["L0_ffn_w3_e"].reshape(1024, 128), g["L0_ffn_w3_s"]]).T
    w2 = np.concatenate([g["L0_ffn_w2_e"].transpose(0, 2, 1).reshape(1024, 128), g["L0_ffn_w2_s"].T])
    t["w2"] = w2.reshape(9, 128, 128).transpose(1, 0, 2)

    def pairs(a):
        b = np.zeros((a.shape[0] // 2, 128, 128), f4)
        b[:, :64, :64] = a[0::2]
        b[:, 64:, 64:] = a[1::2]
        return b.transpose(1, 0, 2)

    wqkv = g["L0_attn_W_qkv"]
    t["wqkT"] = wqkv[:, :2048].T.reshape(16, 128, 128).transpose(1, 0, 2)
    t["wv0"] = wqkv[:, 2048:]
    t["rf"] = pairs(g["L0_attn_RF"])
    t["wout"] = g["L0_attn_W_out"].reshape(8, 128, 128).transpose(1, 0, 2)
    t["wgu"] = np.concatenate([g["L1_ffn_Wg"], g["L1_ffn_Wu"]], axis=1)
    t["wqT"] = g["L1_ffn_Wq"].T.reshape(4, 128, 128).transpose(1, 0, 2)
    t["keys"] = pairs(g["L1_ffn_keys"].transpose(2, 0, 3, 1).reshape(8, 64, 64))
    t["deT"] = g["L1_ffn_down_embed"].T
    t["wdue"] = np.concatenate([g["L1_ffn_Wd"], g["L1_ffn_up_embed"]]).reshape(8, 128, 128).transpose(1, 0, 2)
    t["bgu"] = np.concatenate([g["L1_ffn_bg"], g["L1_ffn_bu"]]).reshape(8, 128).T
    t["rows"] = np.concatenate([g["L0_attn_b_out"], g["L1_ffn_bd"]])[None]
    w = g["L1_attn_w_qkv"]

    def turned(a):
        return a.reshape(128, 16, 2, 32)[:, :, ::-1].reshape(128, 1024)

    t["wa"] = np.concatenate([w[:, :1024], turned(w[:, :1024]), w[:, 1024:2048], turned(w[:, 1024:2048]),
                              w[:, 2048:]], axis=1)
    t["wo"] = g["L1_attn_w_o"].reshape(8, 128, 128).transpose(1, 0, 2)

    def spaced(a, rep):
        b = np.zeros((a.shape[0], 4, a.shape[1], 4), f4)
        for j in range(4):
            b[:, j, :, j] = a
        return np.concatenate([b.reshape(a.shape[0] * 4, a.shape[1] * 4)] * rep)

    w1 = g["L1_attn_w1"]
    t["w1s"], t["w1k"] = spaced(w1[:16], 2), spaced(w1[16:], 2)
    t["w2b"] = spaced(g["L1_attn_w2"], 1)
    t["b1c"] = np.repeat(g["L1_attn_b1"], 4)[:, None]
    t["b2r"] = np.repeat(g["L1_attn_b2"], 4)[:, None]
    t["b2b"] = np.tile(g["L1_attn_b2"][None], (128, 1))
    lp, la = g["L1_attn_log_p"].reshape(16), g["L1_attn_log_a"].reshape(16)
    t["lp_c"] = np.tile(np.repeat(lp, 4), 2)[:, None]
    t["la_c"] = np.tile(np.repeat(la, 4), 2)[:, None]
    t["pab"] = np.tile(np.stack([lp, la])[None], (128, 1, 1))
    t["c_id"] = np.eye(128, dtype=f4)
    e = np.arange(48)[:, None, None] % 16
    t["c_sel"] = (e == 2 * np.arange(8)[None, :, None] + np.arange(128)[None, None] // 64).astype(f4)
    q = np.arange(4)
    t["c_tri"] = np.tile((q[None, :] < q[:, None]).astype(f4)[None], (128, 1, 1))
    inv = (f4(1.0) / np.power(f4(10000.0), np.arange(0, 64, 2, dtype=f4) / f4(64))).astype(f4)
    fr = np.outer(np.arange(512, dtype=f4), inv).astype(f4)
    emb = np.concatenate([fr, fr], -1)
    sign = np.where(np.arange(64) < 32, f4(-1), f4(1))
    t["c_rope"] = np.stack([np.tile(np.cos(emb).astype(f4).T, (2, 1)),
                            np.tile((np.sin(emb).astype(f4) * sign).T, (2, 1))], axis=1)
    p = np.arange(128)[:, None]
    t["c_dn"] = np.abs(p + 384 - np.arange(512)[None]).astype(f4)
    t["c_dt"] = np.abs(np.arange(640)[None] - 128 - p % 4).astype(f4)
    return {k: np.ascontiguousarray(v) for k, v in t.items()}


def kernel(**inputs):
    import numpy as _np
    import concourse.bacc as _bacc
    from concourse import mybir as _mybir
    from concourse.bass_utils import run_bass_kernel_spmd as _run

    nc = _bacc.Bacc("TRN2", target_bir_lowering=False, num_devices=1)
    arrays, t = {}, {}
    for name, a in _layout(inputs).items():
        arrays[f"in_{name}_dram"] = a
        t[name] = nc.dram_tensor(f"in_{name}_dram", a.shape, _mybir.dt.from_np(a.dtype), kind="ExternalInput").ap()
    o = nc.dram_tensor("out_0_dram", (4, 512, 128), _mybir.dt.float32, kind="ExternalOutput").ap()
    build(nc, t, o)
    r = _run(nc, [arrays], core_ids=[0])
    return r.results[0]["out_0_dram"]
```

```python
from contextlib import ExitStack

from concourse import bass, mybir

F32 = mybir.dt.float32
F16 = mybir.dt.float16
BF16 = mybir.dt.bfloat16
ALU = mybir.AluOpType
ACT = mybir.ActivationFunctionType
AX_X = mybir.AxisListType.X


class Lane:

    def __init__(self, sem):
        self.sem = sem
        self.items = []
        self.n = 0

    def add(self, fn, after=(), mark=True):
        self.items.append((fn, tuple(after), mark))
        if mark:
            self.n += 1
        return (self.sem, self.n)

    def issue(self, eng):
        seen = {}
        for fn, after, mark in self.items:
            for sem, value in after:
                if seen.get(sem.name, 0) < value:
                    eng.wait_ge(sem, value)
                    seen[sem.name] = value
            ins = fn(eng)
            if mark:
                ins.then_inc(self.sem, 1)


class Slot:

    def __init__(self, ap):
        self.ap = ap
        self.free = []

    def take(self):
        waits, self.free = self.free, []
        return waits


class Ring:
    def __init__(self, slots):
        self.slots = slots
        self.i = 0

    def next(self):
        s = self.slots[self.i % len(self.slots)]
        self.i += 1
        return s


def build(nc, t, out):
    with ExitStack() as ctx:
        def sb(name, shape, dt=F32):
            return ctx.enter_context(nc.sbuf_tensor(name, shape, dt))

        def sem(name):
            return ctx.enter_context(nc.semaphore(name))

        pe, act, dve, pool, sp = (Lane(sem(n)) for n in ("s_pe", "s_act", "s_dve", "s_pool", "s_sp"))
        PS = [Slot(ctx.enter_context(nc.psum_tensor(f"ps{i}", [128, 512], F32))) for i in range(8)]

        x = sb("x", [128, 16, 128])
        xth = sb("xth", [128, 2048], F16)
        xtl = sb("xtl", [128, 2048], F16)
        idf = sb("idf", [128, 128])
        idb = sb("idb", [128, 128], BF16)
        ones = sb("ones", [128, 128])
        tri = sb("tri", [128, 4, 4])
        small = sb("small", [128, 1024])

        park = sb("park", [128, 4096])

        def half(a, n):
            return park[:, a:a + n // 2].bitcast(F16)

        wgu_h, wgu_l = half(0, 1024), half(512, 1024)
        wk_h, wk_l = half(1024, 512), half(1280, 512)
        de_h, de_l = half(1536, 512), half(1792, 512)
        wdue = park[:, 2048:3072].rearrange("p (b n) -> p b n", b=8)
        parked = nc.dram_tensor("parked", (128, 3072), F32, kind="Internal").ap()
        bgu = sb("bgu", [128, 8])
        rows = sb("rows", [1, 256])

        wa_h, wa_l = sb("wa_h", [128, 5120], F16), sb("wa_l", [128, 5120], F16)
        wo = sb("wo", [128, 8, 128])
        cs = sb("cs", [128, 2, 512])
        ws_h, ws_l = sb("ws_h", [128, 128], F16), sb("ws_l", [128, 128], F16)
        idh = sb("idh", [128, 128], F16)
        w2b = sb("w2b", [128, 64])
        b1c = sb("b1c", [128, 1])
        b2r = sb("b2r", [128, 1])
        ct_h, ct_l = sb("ct_h", [128, 640], F16), sb("ct_l", [128, 640], F16)
        pa = sb("pa", [128, 4])
        pab = sb("pab", [128, 2, 16])
        b2b = sb("b2b", [128, 16])

        reg0 = sb("reg0", [128, 8192])
        o = 0

        def r0(n, dt=F32):
            nonlocal o
            w = n if dt == F32 else n // 2
            v = reg0[:, o:o + w]
            o += w
            return v if dt == F32 else v.bitcast(dt)

        w13_h, w13_l = r0(2304, F16), r0(2304, F16)
        w2 = r0(1152).rearrange("p (b n) -> p b n", b=9)
        wg_h, wg_l = r0(16, F16), r0(16, F16)
        wq_h, wq_l = r0(1024, F16), r0(1024, F16)
        wkr_h, wkr_l = r0(1024, F16), r0(1024, F16)
        wv_h, wv_l = r0(1024, F16), r0(1024, F16)
        wout = r0(1024).rearrange("p (b n) -> p b n", b=8)
        sel = r0(1024, BF16)[0:48, :].rearrange("p (b n) -> p b n", b=8)
        assert o <= 8192
        kn = reg0[:, :].rearrange("p (h v) -> p h v", h=16)

        NW = 24608
        work = sb("work", [128, NW])

        def wk(a, n, dt=F32):
            assert a + n <= NW
            v = work[:, a:a + n]
            return v if dt == F32 else v.bitcast(dt)

        ctb = wk(23000, 1024, BF16)[0:48, :]

        def mm(o_, l, r, start, stop, after=(), mark=False):
            return pe.add(lambda e: e.matmul(o_, l, r, start=start, stop=stop), after, mark)

        def tp(o_, i_, ident, after=(), mark=False):
            return pe.add(lambda e: e.transpose(o_, i_, ident), after, mark)

        def af(o_, i_, f, after=(), **kw):
            return act.add(lambda e: e.activation(o_, i_, f, **kw), after)

        def tt(lane, o_, a, b, op, after=()):
            return lane.add(lambda e: e.tensor_tensor(o_, a, b, op), after)

        def ts(lane, o_, a, s1, s2, op0, op1=None, after=()):
            if op1 is None:
                return lane.add(lambda e: e.tensor_scalar(o_, a, s1, None, op0), after)
            return lane.add(lambda e: e.tensor_scalar(o_, a, s1, s2, op0, op1), after)

        def stt(o_, a, s, b, op0, op1, after=(), **kw):
            return dve.add(lambda e: e.scalar_tensor_tensor(out=o_, in0=a, scalar=s, in1=b, op0=op0, op1=op1, **kw),
                           after)

        def cp(lane, o_, i_, after=()):
            return lane.add(lambda e: e.tensor_copy(o_, i_), after)

        def red(o_, i_, op, after=()):
            return dve.add(lambda e: e.tensor_reduce(o_, i_, AX_X, op), after)

        def ms(lane, o_, v, after=()):
            return lane.add(lambda e: e.memset(o_, v), after)

        loads = {}

        def load(key, dst, src, after=(), lane=sp):
            if key not in loads:
                loads[key] = [sem(f"l_{key}"), 0]
            s = loads[key]
            s[1] += 16
            sm = s[0]
            lane.add(lambda e: e.dma_start(dst, src).then_inc(sm, 16), after, False)

        def got(key):
            return (loads[key][0], loads[key][1])

        xin = t["x"].rearrange("b (q p) d -> p (b q) d", p=128)
        for c in range(4):
            load(f"x{c}", x[:, 4 * c:4 * c + 4, :], xin[:, 4 * c:4 * c + 4, :])
        load("id", idf[:, :], t["c_id"])
        st = 14000
        s_w13 = wk(st, 2304)
        s_gate = wk(st + 2304, 16)
        load("w13", s_gate, t["w_gate"])
        load("w13", s_w13, t["w13"])
        load("cst", tri[:, :, :], t["c_tri"])
        load("cst", wk(23000, 1024)[0:48, :].rearrange("p (b n) -> p b n", b=8), t["c_sel"])
        load("w2", w2, t["w2"])
        s_qk = wk(st + 2320, 2048).rearrange("p (b n) -> p b n", b=16)
        s_wv = wk(st + 4368, 1024)
        s_rf = wk(st + 5392, 1024).rearrange("p (b n) -> p b n", b=8)
        load("a0", s_qk, t["wqkT"])
        load("a0", s_rf, t["rf"])
        load("a0", s_wv, t["wv0"])
        load("a0", wout, t["wout"])
        s_gu = wk(st + 6416, 1024)
        s_wqT = wk(st + 7440, 512).rearrange("p (b n) -> p b n", b=4)
        s_key = wk(st + 7952, 512).rearrange("p (b n) -> p b n", b=4)
        s_de = wk(st + 8464, 512)
        load("f1", s_gu, t["wgu"])
        load("f1", s_wqT, t["wqT"])
        load("f1", s_key, t["keys"])
        load("f1", s_de, t["deT"])
        load("f1", wdue, t["wdue"])
        load("f1", bgu[:, :], t["bgu"])
        load("f1", rows[:, :], t["rows"])
        load("a1", wo[:, :, :], t["wo"])
        load("a1", cs[:, :, :], t["c_rope"])
        load("a1", w2b[:, :], t["w2b"])
        load("a1", b1c[:, :], t["b1c"])
        load("a1", b2r[64:128, :], t["b2r"])
        load("a1", pa[:, 0:1], t["lp_c"])
        load("a1", pa[:, 1:2], t["la_c"])
        load("a1", pab[:, :, :], t["pab"])
        load("a1", b2b[:, :], t["b2b"])

        k_ones = ms(dve, ones[:, :], 1.0)
        k_idb = cp(dve, idb[:, :], idf[:, :], [got("id")])
        k_idh = cp(dve, idh[:, :], idf[:, :], [got("id")])
        k_idf = got("id")
        k_sel = cp(dve, sel.rearrange("p b n -> p (b n)"), wk(23000, 1024)[0:48, :], [got("cst")])

        def split(hi, lo, src, after, lane):
            a = af(hi, src, ACT.Copy, after)
            return tt(lane, lo, src, hi, ALU.subtract, [a, *after])

        k_gate = split(wg_h, wg_l, s_gate, [got("w13")], dve)
        k_w13 = split(w13_h, w13_l, s_w13, [got("w13")], dve)
        k_wv = split(wv_h, wv_l, s_wv, [got("a0")], pool)
        k_gu = split(wgu_h, wgu_l, s_gu, [got("f1")], pool)
        k_de = split(de_h, de_l, s_de, [got("f1")], pool)

        def fold(dst_h, dst_l, lefts, rights, n, after, ring):
            done = []
            for q in range(n):
                bk = ring.next()
                w = bk.take()
                for j in range(4):
                    m = mm(bk.ap[:, 128 * j:128 * j + 128], lefts[4 * q + j], rights[4 * q + j], True, True,
                           [*after, *w], j == 3)
                h, l = dst_h[:, 512 * q:512 * q + 512], dst_l[:, 512 * q:512 * q + 512]
                a = af(h, bk.ap[:, :], ACT.Copy, [m])
                d = tt(dve, l, bk.ap[:, :], h, ALU.subtract, [a, m])
                bk.free = [d]
                done.append(d)
            return done[-1]

        mv = small[:, 0:32].rearrange("p (t s) -> p t s", s=2)
        rs = small[:, 32:96].rearrange("p (k t) -> p k t", t=16)
        bst = small[:, 96:192].rearrange("p (t s) -> p t s", s=6)
        XH = [Slot(park[:, 3072 + 512 * i:3584 + 512 * i].rearrange("p (t d) -> p t d", t=4)) for i in range(2)]
        xh_ring = Ring(XH)
        xt_free = []
        EPS = 1e-5

        def layernorm(x_ready, banks):
            nonlocal xt_free
            xt_wait, xt_free = xt_free, []
            done = []
            ring = Ring(banks)
            for c in range(4):
                r = slice(4 * c, 4 * c + 4)
                for i in range(4 * c, 4 * c + 4):
                    b = dve.add(lambda e, i=i: e.bn_stats(bst[:, i, :], x[:, i, :]), x_ready[c])
                for i in range(4 * c, 4 * c + 4):
                    a = dve.add(lambda e, i=i: e.bn_aggr(mv[:, i, :], bst[:, i, :]), [b])
                v = ts(dve, rs[:, 0, r], mv[:, r, 1], EPS, None, ALU.add, after=[a])
                s = af(rs[:, 1, r], rs[:, 0, r], ACT.Sqrt, [v])
                i0 = dve.add(lambda e, r=r: e.reciprocal(rs[:, 2, r], rs[:, 1, r]), [s])
                n1 = tt(dve, rs[:, 1, r], rs[:, 2, r], rs[:, 2, r], ALU.mult, [i0])
                n2 = tt(dve, rs[:, 1, r], rs[:, 1, r], rs[:, 0, r], ALU.mult, [n1])
                n3 = ts(dve, rs[:, 1, r], rs[:, 1, r], -0.5, 1.5, ALU.mult, ALU.add, [n2])
                n4 = tt(dve, rs[:, 2, r], rs[:, 2, r], rs[:, 1, r], ALU.mult, [n3])
                xs = xh_ring.next()
                w = xs.take()
                for j in range(4):
                    i = 4 * c + j
                    h = ts(dve, xs.ap[:, j, :], x[:, i, :], mv[:, i, 0:1], rs[:, 2, i:i + 1], ALU.subtract,
                           ALU.mult, [n4, *w])
                bk = ring.next()
                w = bk.take()
                for j in range(4):
                    m = tp(bk.ap[:, 128 * j:128 * j + 128], xs.ap[:, j, :], idf[:, :], [h, k_idf, *w], j == 3)
                xs.free = [m]
                s_ = slice(512 * c, 512 * c + 512)
                a = af(xth[:, s_], bk.ap[:, :], ACT.Copy, [m, *xt_wait])
                d = tt(dve, xtl[:, s_], bk.ap[:, :], xth[:, s_], ALU.subtract, [a, m, *xt_wait])
                bk.free = [d]
                done.append(d)
            return done

        def proj_t(o_, wh, wl, c, after, mark=True):
            s_ = slice(512 * c, 512 * c + 512)
            mm(o_, wh, xth[:, s_], True, False, after)
            mm(o_, wh, xtl[:, s_], False, False)
            return mm(o_, wl, xth[:, s_], False, True, mark=mark)

        def proj_n(o_, wh, wl, i, after, mark=True):
            s_ = slice(128 * i, 128 * i + 128)
            mm(o_, xth[:, s_], wh, True, False, after)
            mm(o_, xth[:, s_], wl, False, False)
            return mm(o_, xtl[:, s_], wh, False, True, mark=mark)

        spl = small[:, 192:576].bitcast(BF16).rearrange("p (t k e) -> p t k e", t=16, k=3)
        rem = small[:, 576:832].rearrange("p (t e) -> p t e", t=16)
        ct_free = []

        def spread(src, tiles, after, bk):
            nonlocal ct_free
            r = slice(tiles[0], tiles[-1] + 1)
            a = cp(dve, spl[:, r, 0, :], src, after)
            b = tt(dve, rem[:, r, :], src, spl[:, r, 0, :], ALU.subtract, [a, *after])
            a = cp(dve, spl[:, r, 1, :], rem[:, r, :], [b])
            b = tt(dve, spl[:, r, 2, :], rem[:, r, :], spl[:, r, 1, :], ALU.subtract, [a])
            done = []
            for q in range(len(tiles) // 4):
                w = bk.take()
                v = bk.ap[0:48, 0:256].bitcast(BF16)
                for j in range(4):
                    i = tiles[4 * q + j]
                    m = tp(v[:, 128 * j:128 * j + 128], spl[:, i, :, :].rearrange("p k e -> p (k e)"), idb[:, :],
                           [b, k_idb, *w], j == 3)
                s_ = slice(128 * tiles[4 * q], 128 * tiles[4 * q] + 512)
                d = cp(dve, ctb[:, s_], v, [m, *ct_free])
                bk.free = [d]
                done.append(d)
            ct_free = []
            return done

        def ffn0(x_ready):
            nonlocal ct_free, xt_free
            H = [Slot(wk(4608 * i, 4608).rearrange("p (b n) -> p b n", b=9)) for i in range(2)]
            SG = Ring([Slot(wk(9216 + 512 * i, 512)) for i in range(3)])
            HU = Ring([Slot(wk(10752 + 512 * i, 512)) for i in range(3)])
            xt = layernorm(x_ready, [PS[7], PS[6]])
            G = wk(12288, 1600)
            S = G[:, 0:256].rearrange("p (t e) -> p t e", t=16)
            S4 = G[:, 0:256].rearrange("p (t g e) -> p t g e", t=16, g=4)
            A1 = G[:, 256:384].rearrange("p (t g e) -> p t g e", t=16, g=4)
            A2 = G[:, 384:512].rearrange("p (t g e) -> p t g e", t=16, g=4)
            g1 = G[:, 512:576].rearrange("p (t g) -> p t g", t=16)
            g2 = G[:, 576:640].rearrange("p (t g) -> p t g", t=16)
            g3 = G[:, 640:704].rearrange("p (t g) -> p t g", t=16)
            q1 = G[:, 704:960].rearrange("p (t g e) -> p t g e", t=16, g=4)
            q2 = G[:, 960:1216].rearrange("p (t g e) -> p t g e", t=16, g=4)
            q2f = G[:, 960:1216].rearrange("p (t e) -> p t e", t=16)
            q1f = G[:, 704:960].rearrange("p (t e) -> p t e", t=16)
            m8 = G[:, 1216:1344].rearrange("p (t e) -> p t e", t=16)
            w1_ = G[:, 1344:1360]
            gb = PS[5]
            w = gb.take()
            for i in range(16):
                m = proj_n(gb.ap[:, 16 * i:16 * i + 16], wg_h, wg_l, i, [xt[i // 4], k_gate, *w], i == 15)
            z = af(G[:, 0:256], gb.ap[:, 0:256], ACT.Sigmoid, [m, *work_free])
            gb.free = [z]
            a = tt(dve, A1, S4[:, :, :, 0:2], S4[:, :, :, 2:4], ALU.max, [z])
            b = tt(dve, A2, S4[:, :, :, 0:2], S4[:, :, :, 2:4], ALU.min, [z])
            c_ = tt(dve, g1, A1[:, :, :, 0], A1[:, :, :, 1], ALU.max, [a])
            d = tt(dve, g2, A1[:, :, :, 0], A1[:, :, :, 1], ALU.min, [a])
            f = tt(dve, g3, A2[:, :, :, 0], A2[:, :, :, 1], ALU.max, [b])
            f = tt(dve, g2, g2, g3, ALU.max, [d, f])
            f = tt(dve, g1, g1, g2, ALU.add, [c_, f])
            other = g1.unsqueeze(2).to_broadcast([128, 16, 4, 4])
            own = g1.unsqueeze(3).to_broadcast([128, 16, 4, 4])
            a = tt(dve, q1, other, own, ALU.is_gt, [f])
            b = tt(dve, q2, other, own, ALU.is_equal, [f])
            trb = tri[:, :, :].unsqueeze(1).to_broadcast([128, 16, 4, 4])
            b = tt(dve, q2, q2, trb, ALU.mult, [b, got("cst")])
            b = tt(dve, q1, q1, q2, ALU.add, [a, b])
            b = red(g2, q1, ALU.add, [b])
            b = ts(dve, g2, g2, 1.5, None, ALU.is_lt, after=[b])
            al = g2.unsqueeze(3).to_broadcast([128, 16, 4, 4])
            a = tt(dve, q1, S4, al, ALU.mult, [b])
            b = ts(dve, g3, g2, -1.0, None, ALU.add, after=[b])
            am = g3.unsqueeze(3).to_broadcast([128, 16, 4, 4])
            a = tt(dve, q1, q1, am, ALU.add, [a, b])
            for i in range(16):
                b = dve.add(lambda e, i=i: e.max(m8[:, i, :], q1f[:, i, :]), [a])
            thr = m8[:, :, 3:4].to_broadcast([128, 16, 16])
            b = tt(dve, q2f, q1f, thr, ALU.is_ge, [b])
            b = tt(dve, q2f, q2f, S, ALU.mult, [b])
            a = red(w1_, q2f, ALU.add, [b])
            a = ts(dve, w1_, w1_, 1e-6, None, ALU.add, after=[a])
            a = dve.add(lambda e: e.reciprocal(w1_, w1_), [a])
            a = tt(dve, q2f, q2f, w1_.unsqueeze(2).to_broadcast([128, 16, 16]), ALU.mult, [a, b])
            ct = spread(q2f, list(range(16)), [a], PS[7])

            gr, ur, cr = Ring([PS[0], PS[1]]), Ring([PS[2], PS[3]]), Ring([PS[4], PS[5]])
            x_done = []

            def up(c):
                hs = H[c % 2]
                hw = hs.take()
                done = []
                for b_ in range(9):
                    g_, u_ = gr.next(), ur.next()
                    mg = proj_t(g_.ap[:, :], w13_h[:, 128 * b_:128 * b_ + 128], w13_l[:, 128 * b_:128 * b_ + 128], c,
                                [xt[c], k_w13, *g_.take()])
                    n = 1152 + 128 * b_
                    mu = proj_t(u_.ap[:, :], w13_h[:, n:n + 128], w13_l[:, n:n + 128], c, u_.take())
                    sg = SG.next()
                    z = af(sg.ap, g_.ap[:, :], ACT.Silu, [mg, *sg.take(), *work_free])
                    g_.free = [z]
                    if b_ == 8:
                        f = tt(dve, hs.ap[:, b_, :], sg.ap, u_.ap[:, :], ALU.mult, [z, mu, *hw, *work_free])
                        sg.free = [f]
                        u_.free = [f]
                    else:
                        k_ = cr.next()
                        mc = mm(k_.ap[:, :], sel[:, b_, :], ctb[:, 512 * c:512 * c + 512], True, True,
                                [ct[c], k_sel, *k_.take()], True)
                        hu = HU.next()
                        y = tt(dve, hu.ap, sg.ap, u_.ap[:, :], ALU.mult, [z, mu, *hu.take(), *work_free])
                        sg.free = [y]
                        u_.free = [y]
                        f = tt(dve, hs.ap[:, b_, :], hu.ap, k_.ap[:, :], ALU.mult, [y, mc, *hw])
                        hu.free = [f]
                        k_.free = [f]
                    done.append(f)
                return done[-1]

            def down(c, h_done):
                bk = PS[6]
                w = bk.take()
                for j in range(4):
                    for b_ in range(9):
                        m = mm(bk.ap[:, 128 * j:128 * j + 128], H[c % 2].ap[:, b_, 128 * j:128 * j + 128], w2[:, b_, :],
                               b_ == 0, b_ == 8, [h_done, got("w2"), *w], j == 3 and b_ == 8)
                H[c % 2].free = [m]
                xv = x[:, 4 * c:4 * c + 4, :].rearrange("p t d -> p (t d)")
                f = stt(xv, bk.ap[:, :], 0.5, xv, ALU.mult, ALU.add, [m])
                bk.free = [f]
                x_done.append([f])
                return m

            hd = [None] * 4
            for c in range(5):
                if c < 4:
                    hd[c] = up(c)
                if c > 0:
                    m = down(c - 1, hd[c - 1])
            xt_free = [m]
            ct_free = [m]
            return x_done, [m, x_done[-1][0]]

        def attn0(x_ready):
            nonlocal ct_free, xt_free
            PK = wk(0, 4096).rearrange("p (t n) -> p t n", t=4)
            VV = wk(4096, 4096).rearrange("p (t n) -> p t n", t=4)
            PQ = wk(8192, 4096).rearrange("p (b n) -> p b n", b=8)
            KVT = wk(12288, 1024).rearrange("p (b n) -> p b n", b=8)
            KW = wk(13312, 1024).rearrange("p (b n) -> p b n", b=8)
            KS = wk(14336, 16).rearrange("p (b n) -> p b n", b=8)
            NR = wk(14352, 64).rearrange("p (t e) -> p t e", t=4)
            xt = layernorm(x_ready, [PS[7], PS[6]])
            z1 = ms(dve, KVT, 0.0, work_free)
            z1 = ms(dve, KS, 0.0, work_free)
            x_done = []
            ring = Ring([PS[0], PS[1], PS[2], PS[3]])
            kw_free, kv_free, pk_free, pq_free, nr_free, ks_free = [], [z1], [], [], [], [z1]
            for c in range(4):
                ev, evp = [], []
                for j in range(4):
                    for n in range(2):
                        s_ = slice(512 * n, 512 * n + 512)
                        bk = ring.next()
                        m = proj_n(bk.ap[:, :], wkr_h[:, s_], wkr_l[:, s_], 4 * c + j, [xt[c], k_fold0, *bk.take()])
                        a = af(PK[:, j, s_], bk.ap[:, :], ACT.Relu, [m, *pk_free, *work_free])
                        bk.free = [a]
                        bk = ring.next()
                        m = proj_n(bk.ap[:, :], wv_h[:, s_], wv_l[:, s_], 4 * c + j, [k_wv, *bk.take()])
                        b = cp(dve, VV[:, j, s_], bk.ap[:, :], [m, *pk_free, *work_free])
                        bk.free = [b]
                        ev, evp = [a], [b]
                pq = []
                for p in range(8):
                    bk = ring.next()
                    m = proj_t(bk.ap[:, :], wq_h[:, 128 * p:128 * p + 128], wq_l[:, 128 * p:128 * p + 128], c,
                               bk.take())
                    if p % 2:
                        a = af(PQ[:, p, :], bk.ap[:, :], ACT.Relu, [m, *pq_free, *work_free])
                    else:
                        a = ts(dve, PQ[:, p, :], bk.ap[:, :], 0.0, None, ALU.max, after=[m, *pq_free, *work_free])
                    bk.free = [a]
                    pq.append(a)
                kb = PS[5]
                w = kb.take()
                for p in range(8):
                    for j in range(4):
                        m = mm(kb.ap[:, p:p + 1], PK[:, j, 128 * p:128 * p + 128], ones[:, 0:1], j == 0, j == 3,
                               [*ev, k_ones, *w], p == 7 and j == 3)
                a = cp(dve, KS[0:64, :, 0], kb.ap[0:64, 0:8], [m, *ks_free])
                ks = cp(dve, KS[64:128, :, 1], kb.ap[64:128, 0:8], [m, *ks_free])
                kb.free = [ks]
                kd = []
                for q in range(2):
                    bk = PS[6 + q]
                    w = bk.take()
                    for u in range(4):
                        p = 4 * q + u
                        for j in range(4):
                            m = mm(bk.ap[:, 128 * u:128 * u + 128], VV[:, j, 128 * p:128 * p + 128],
                                   PK[:, j, 128 * p:128 * p + 128], j == 0, j == 3, [*ev, *evp, *w], u == 3 and j == 3)
                    bv = bk.ap[:, :].rearrange("p (b n) -> p b n", b=4)
                    a = cp(dve, KVT[0:64, 4 * q:4 * q + 4, 0:64], bv[0:64, :, 0:64], [m, *kv_free])
                    b = cp(dve, KVT[64:128, 4 * q:4 * q + 4, 64:128], bv[64:128, :, 64:128], [m, *kv_free])
                    bk.free = [b]
                    kd.append(b)
                pk_free = [m]
                nb = PS[4]
                w = nb.take()
                for j in range(4):
                    for p in range(8):
                        m = mm(nb.ap[:, 16 * j + 2 * p:16 * j + 2 * p + 2], PQ[:, p, 128 * j:128 * j + 128], KS[:, p, :],
                               True, True, [pq[6], pq[7], ks, *w], j == 3 and p == 7)
                ks_free = [m]
                NRf = NR.rearrange("p t e -> p (t e)")
                a = ts(dve, NRf, nb.ap[:, 0:64], 1e-6, None, ALU.add, after=[m, *nr_free])
                nb.free = [a]
                a = dve.add(lambda e: e.reciprocal(NRf, NRf), [a])
                kw = []
                for q in range(2):
                    bk = PS[6 + q]
                    w = bk.take()
                    for u in range(4):
                        p = 4 * q + u
                        m = mm(bk.ap[:, 128 * u:128 * u + 128], KVT[:, p, :], wout[:, p, :], True, True,
                               [kd[q], got("a0"), *w], u == 3)
                    b = af(KW[:, 4 * q:4 * q + 4, :].rearrange("p b n -> p (b n)"), bk.ap[:, :], ACT.Copy,
                           [m, *kw_free])
                    bk.free = [b]
                    kw.append(b)
                kv_free = [m]
                ct = spread(NR, list(range(4 * c, 4 * c + 4)), [a], PS[5])
                nr_free = [ct[0]]
                for p in range(8):
                    bk = ring.next()
                    m = mm(bk.ap[:, :], sel[:, p, :], ctb[:, 512 * c:512 * c + 512], True, True,
                           [ct[0], *bk.take()], True)
                    b = tt(dve, PQ[:, p, :], PQ[:, p, :], bk.ap[:, :], ALU.mult, [m, pq[p]])
                    bk.free = [b]
                ct_free = [m]
                bk = PS[4]
                w = bk.take()
                for j in range(4):
                    o_ = bk.ap[:, 128 * j:128 * j + 128]
                    mm(o_, ones[0:1, :], rows[0:1, 0:128], True, False, [got("f1"), *w])
                    for p in range(8):
                        m = mm(o_, PQ[:, p, 128 * j:128 * j + 128], KW[:, p, :], False, p == 7, [b, *kw],
                               j == 3 and p == 7)
                pq_free = [m]
                kw_free = [m]
                xv = x[:, 4 * c:4 * c + 4, :].rearrange("p t d -> p (t d)")
                f = tt(dve, xv, bk.ap[:, :], xv, ALU.add, [m])
                bk.free = [f]
                x_done.append([f])
            xt_free = [m]
            return x_done, [m, f]

        def ffn1(x_ready):
            nonlocal xt_free
            PT = wk(0, 8192).rearrange("p (b n) -> p b n", b=4)
            HF = [Slot(wk(8192 + 4096 * i, 4096).rearrange("p (b n) -> p b n", b=8)) for i in range(2)]
            SG = Ring([Slot(wk(16384 + 512 * i, 512)) for i in range(2)])
            SM = Ring([Slot(wk(17408 + 512 * i, 512)) for i in range(2)])
            DD = Ring([Slot(wk(18432 + 2048 * i, 2048)) for i in range(1)])
            EE = Ring([Slot(wk(20480 + 512 * i, 512)) for i in range(3)])
            PP = Ring([Slot(wk(22016 + 512 * i, 512)) for i in range(2)])
            TK = Ring([Slot(wk(23040 + 400 * i, 400)) for i in range(2)])
            xt = layernorm(x_ready, [PS[7], PS[6]])
            sr, tr = Ring([PS[0], PS[1]]), Ring([PS[2], PS[3]])
            ptd = []
            pend = []

            def back(i, pp, f):
                bk = tr.next()
                w = bk.take()
                for q in range(4):
                    m = tp(bk.ap[:, 128 * q:128 * q + 128], pp.ap[:, 128 * q:128 * q + 128], idf[:, :], [f, *w], q == 3)
                pp.free = [m]
                a = af(PT[:, :, 128 * i:128 * i + 128], bk.ap[:, :].rearrange("p (b n) -> p b n", b=4), ACT.Copy,
                       [m, *work_free])
                bk.free = [a]
                ptd.append(a)

            for i in range(16):
                bk = sr.next()
                m = proj_n(bk.ap[:, :], wk_h[:, :], wk_l[:, :], i, [xt[i // 4], k_fold1, *bk.take()])
                sm = SM.next()
                a = af(sm.ap, bk.ap[:, :], ACT.Copy, [m, *sm.take(), *work_free])
                bk.free = [a]
                sv = sm.ap.rearrange("p (s h k) -> p s h k", s=2, h=4)
                tk = TK.next()
                w = [*tk.take(), *work_free]
                top = tk.ap[:, 0:64].rearrange("p (s h k) -> p s h k", s=2, h=4)
                cb = tk.ap[:, 64:320].rearrange("p (h a b) -> p h a b", h=4, a=8)
                cbf = tk.ap[:, 64:320].rearrange("p (h n) -> p h n", h=4)
                v8 = tk.ap[:, 320:352].rearrange("p (h k) -> p h k", h=4)
                e8 = tk.ap[:, 352:384].rearrange("p (h k) -> p h k", h=4)
                nm = tk.ap[:, 384:388]
                zz = tk.ap[:, 388:392]
                acc = tk.ap[:, 392:393]
                dd = DD.next()
                Dv = dd.ap.rearrange("p (h x y) -> p h x y", h=4, x=8)
                xb = sv[:, 0, :, 0:8].unsqueeze(3).to_broadcast([128, 4, 8, 64])
                yb = sv[:, 1, :, :].unsqueeze(2).to_broadcast([128, 4, 8, 64])
                dw = [a, *dd.take(), *work_free]
                dh = [tt(pool, Dv[:, h_], xb[:, h_], yb[:, h_], ALU.add, dw) for h_ in range(4)]
                for s_ in range(2):
                    for h_ in range(4):
                        b = dve.add(lambda e, s_=s_, h_=h_, top=top, sv=sv: e.max(top[:, s_, h_, :], sv[:, s_, h_, :]),
                                    [a, *w])
                b = tt(dve, cb, top[:, 0].unsqueeze(3).to_broadcast([128, 4, 8, 8]),
                       top[:, 1].unsqueeze(2).to_broadcast([128, 4, 8, 8]), ALU.add, [b])
                for h_ in range(4):
                    b = dve.add(lambda e, h_=h_, v8=v8, cbf=cbf: e.max(v8[:, h_, :], cbf[:, h_, :]), [b])
                n_ = ts(dve, nm, v8[:, :, 0], -1.0, None, ALU.mult, after=[b])
                b = tt(dve, e8, v8, nm.unsqueeze(2).to_broadcast([128, 4, 8]), ALU.add, [n_])
                z = af(tk.ap[:, 352:384], tk.ap[:, 352:384], ACT.Exp, [b])
                es = []
                for h_ in range(4):
                    ee = EE.next()
                    y = af(ee.ap, dd.ap[:, 512 * h_:512 * h_ + 512], ACT.Exp, [dh[h_], n_, *ee.take(), *work_free],
                           bias=nm[:, h_:h_ + 1])
                    es.append((ee, y))
                    if h_ == 0:
                        b = red(zz, e8, ALU.add, [z])
                        rz = dve.add(lambda e, zz=zz: e.reciprocal(zz, zz), [b])
                        pp = PP.next()
                        pw = [*pp.take(), *work_free]
                    f = stt(ee.ap, dd.ap[:, 512 * h_:512 * h_ + 512], v8[:, h_, 7:8], ee.ap, ALU.is_ge, ALU.mult,
                            [y])
                    if h_ == 0:
                        p_ = ts(dve, pp.ap, ee.ap, zz[:, 0:1], None, ALU.mult, after=[f, rz, *pw])
                    elif h_ < 3:
                        p_ = stt(pp.ap, ee.ap, zz[:, h_:h_ + 1], pp.ap, ALU.mult, ALU.add, [f, p_])
                    else:
                        p_ = stt(pp.ap, ee.ap, zz[:, h_:h_ + 1], pp.ap, ALU.mult, ALU.add, [f, p_], accum_out=acc)
                    ee.free = [p_]
                dd.free = [f]
                f = ts(dve, pp.ap[:, 511:512], pp.ap[:, 511:512], acc, 4.0, ALU.subtract, ALU.add, [p_])
                tk.free = [f]
                sm.free = [f, dh[3]]
                pend.append((i, pp, f))
                if len(pend) > 1:
                    back(*pend.pop(0))
            back(*pend.pop(0))

            gr, ur = Ring([PS[0], PS[1]]), Ring([PS[4], PS[5]])
            x_done = []

            def up(c):
                hs = HF[c % 2]
                hw = [*hs.take(), *work_free]
                for b_ in range(4):
                    g_, u_ = gr.next(), ur.next()
                    n = 128 * b_
                    mg = proj_t(g_.ap[:, :], wgu_h[:, n:n + 128], wgu_l[:, n:n + 128], c, [xt[c], k_gu, *g_.take()])
                    mu = proj_t(u_.ap[:, :], wgu_h[:, 512 + n:640 + n], wgu_l[:, 512 + n:640 + n], c, u_.take())
                    sg = SG.next()
                    z = af(sg.ap, g_.ap[:, :], ACT.Silu, [mg, got("f1"), *sg.take(), *work_free],
                           bias=bgu[:, b_:b_ + 1])
                    g_.free = [z]
                    f = stt(hs.ap[:, b_, :], u_.ap[:, :], bgu[:, 4 + b_:5 + b_], sg.ap, ALU.add, ALU.mult,
                            [z, mu, *hw])
                    sg.free = [f]
                    u_.free = [f]
                for b_ in range(4):
                    g_ = gr.next()
                    n = 128 * b_
                    mg = proj_t(g_.ap[:, :], de_h[:, n:n + 128], de_l[:, n:n + 128], c, [k_de, *g_.take()])
                    sg = SG.next()
                    z = af(sg.ap, g_.ap[:, :], ACT.Silu, [mg, *sg.take(), *work_free])
                    g_.free = [z]
                    f = tt(dve, hs.ap[:, 4 + b_, :], PT[:, b_, 512 * c:512 * c + 512], sg.ap, ALU.mult,
                           [z, ptd[4 * c + 3], *hw])
                    sg.free = [f]
                return f

            def down(c, h_done):
                bk = PS[6]
                w = bk.take()
                for j in range(4):
                    o_ = bk.ap[:, 128 * j:128 * j + 128]
                    mm(o_, ones[0:1, :], rows[0:1, 128:256], True, False, [got("f1"), k_ones, *w])
                    for b_ in range(8):
                        m = mm(o_, HF[c % 2].ap[:, b_, 128 * j:128 * j + 128], wdue[:, b_, :], False, b_ == 7,
                               [h_done, k_fold1], j == 3 and b_ == 7)
                HF[c % 2].free = [m]
                xv = x[:, 4 * c:4 * c + 4, :].rearrange("p t d -> p (t d)")
                f = stt(xv, bk.ap[:, :], 0.5, xv, ALU.mult, ALU.add, [m])
                bk.free = [f]
                x_done.append([f])
                return m

            hd = [None] * 4
            for c in range(5):
                if c < 4:
                    hd[c] = up(c)
                if c > 0:
                    m = down(c - 1, hd[c - 1])
            xt_free = [m]
            return x_done, [m, x_done[-1][0], dh[3]]

        def tables1():
            w = [*work_free, got("a1"), got("dst")]
            dn = wk(0, 512)
            dt_ = wk(512, 640)
            tmp = wk(1152, 8192).rearrange("p (h v) -> p h v", h=16)
            kt, w1d, w1k = wk(9344, 640), wk(9984, 128), wk(10112, 128)
            z = af(pa[:, 0:2], pa[:, 0:2], ACT.Exp, w)
            z = af(pab[:, :, :], pab[:, :, :], ACT.Exp, w)
            z = af(pa[:, 0:2], pa[:, 0:2], ACT.Ln, [z], bias=1.0)
            z = af(pab[:, :, :], pab[:, :, :], ACT.Ln, [z], bias=1.0)
            a = af(kt, dt_, ACT.Ln, [z, *w], scale=pa[:, 1:2], bias=1.0)
            n0 = ts(dve, pa[:, 2:3], pa[:, 0:1], -1.0, None, ALU.mult, after=[z])
            n1 = ts(dve, pab[:, 0, :], pab[:, 0, :], -1.0, None, ALU.mult, after=[z])
            k1 = ts(dve, kt, kt, pa[:, 2:3], None, ALU.mult, after=[a, n0])
            d = tt(dve, w1k[0:64, :], w1k[0:64, :], w1d[0:64, :], ALU.subtract, w)
            h = af(ws_h[:, :], w1d, ACT.Copy, w)
            e = tt(dve, ws_l[:, :], w1d, ws_h[:, :], ALU.subtract, [h])
            done = [e]
            for bk, r in ((PS[4], slice(0, 512)), (PS[6], slice(512, 640))):
                v = bk.ap[:, 0:r.stop - r.start]
                m = mm(v, w1k[0:64, :], kt[0:64, r], True, True, [d, k1, *bk.take()], True)
                h = af(ct_h[:, r], v, ACT.Copy, [m])
                e = tt(dve, ct_l[:, r], v, ct_h[:, r], ALU.subtract, [h, m])
                bk.free = [e]
                done.append(e)
            bk = PS[5]
            m = mm(bk.ap[:, 0:1], w1d[64:128, :], b2r[64:128, :], True, True, [*w, *bk.take()], True)
            e = tt(dve, b1c[:, :], b1c[:, :], bk.ap[:, 0:1], ALU.subtract, [m])
            bk.free = [e]
            done.append(e)
            for h in range(16):
                a = af(tmp[:, h, :], dn, ACT.Ln, [z, *w], scale=pab[:, 1, h:h + 1], bias=1.0)
                k2 = ts(dve, kn[:, h, :], tmp[:, h, :], pab[:, 0, h:h + 1], b2b[:, h:h + 1], ALU.mult, ALU.add,
                        [a, n1, *reg0_free])
            return [*done, k2]

        def attn1(x_ready):
            nonlocal xt_free
            tabs = tables1()
            FA = wk(0, 8192)
            QT = wk(8192, 4096).rearrange("p (b n) -> p b n", b=8)
            KT = wk(12288, 4096).rearrange("p (b n) -> p b n", b=8)
            vx = sb("vx", [128, 2, 16, 65])
            VX = [vx[:, 0], vx[:, 1]]
            VX += [wk(16384 + 1040 * i, 1040).rearrange("p (h d) -> p h d", h=16) for i in range(2)]
            TB = Ring([Slot(wk(18464 + 256 * i, 256, F16)) for i in range(4)])
            HL = Ring([Slot(v.rearrange("p (g s n) -> p g s n", g=8, s=2))
                       for v in (wk(19488, 512, F16), wk(20000, 512, F16), half(3072, 1024), half(3584, 1024))])
            GB = Ring([Slot(wk(20512 + 512 * i, 512)) for i in range(4)])
            PB = Ring([Slot(park[:, 512 * i:512 * i + 512]) for i in range(6)])
            TP = Ring([Slot(wk(22560 + 512 * i, 512)) for i in range(2)])
            OO = wk(23584, 1024)
            mx = small[:, 832:848]
            rd = small[:, 848:864]
            xt = layernorm(x_ready, [PS[7], PS[6]])
            for v in VX:
                v1 = ms(dve, v[:, :, 64:65], 1.0, work_free)
            qk_ring = Ring([PS[0], PS[1]])
            tr = Ring([PS[2], PS[3]])
            gr = Ring([PS[4], PS[5], PS[6]])
            pvb = PS[7]
            wf = [*work_free, *tabs]
            for b_ in PB.slots + HL.slots:
                b_.free = [*xt, *x_ready[3]]
            ident = idf[:, :]
            st = {"qt": [], "vx": [], "oo": [], "mx": [], "v": None, "q": None, "f": [[]] * 16}
            x_done = [[] for _ in range(4)]

            def project_qk(c):
                pr = Ring([PS[0], PS[1], PS[4], PS[5]])
                for p in range(8):
                    for off, dst in ((0, QT), (2048, KT)):
                        b0, b1 = pr.next(), pr.next()
                        n = off + 128 * p
                        m0 = proj_t(b0.ap[:, :], wa_h[:, n:n + 128], wa_l[:, n:n + 128], c, [xt[c], *k_wa, *b0.take()])
                        n += 1024
                        m1 = proj_t(b1.ap[:, :], wa_h[:, n:n + 128], wa_l[:, n:n + 128], c, b1.take())
                        ra, rb = GB.next(), GB.next()
                        a = tt(dve, ra.ap, b0.ap[:, :], cs[:, 0, :], ALU.mult, [m0, got("a1"), *ra.take(), *wf])
                        b = tt(dve, rb.ap, b1.ap[:, :], cs[:, 1, :], ALU.mult, [m1, *rb.take()])
                        b0.free = [a]
                        b1.free = [b]
                        q_ = tt(pool, dst[:, p, :], ra.ap, rb.ap, ALU.add, [a, b, *st["qt"], *wf])
                        ra.free = [q_]
                        rb.free = [q_]
                st["q"] = q_

            def project_v(c):
                pr = Ring([PS[0], PS[1]])
                for j in range(4):
                    for n in range(2):
                        bk = pr.next()
                        s_ = slice(4096 + 512 * n, 4096 + 512 * n + 512)
                        m = proj_n(bk.ap[:, :], wa_h[:, s_], wa_l[:, s_], 4 * c + j, bk.take())
                        v_ = af(VX[j][:, 8 * n:8 * n + 8, 0:64], bk.ap[:, :].rearrange("p (h d) -> p h d", h=8),
                                ACT.Copy, [m, *st["vx"], *wf])
                        bk.free = [v_]
                st["v"] = v_

            class Unit:
                pass

            def score(u, h):
                J, i0 = u.J, u.i0
                bk = qk_ring.next()
                r = slice(64 * (h % 2), 64 * (h % 2) + 64)
                m = mm(bk.ap[:, 0:J], QT[r, h // 2, i0:i0 + 128], KT[r, h // 2, 0:J], True, True,
                       [st["q"], *bk.take()], True)
                u.s0 = stt(u.F[:, 0:J // 4, h, :], bk.ap[:, 0:J].rearrange("p (a b) -> p a b", b=4), 0.125,
                           kn[:, h, 512 - J:512].rearrange("p (a b) -> p a b", b=4), ALU.mult, ALU.add,
                           [m, *st["f"][h], *wf])
                bk.free = [u.s0]
                st["qt"] = [m]

            def cut(u, q):
                hl = HL.next()
                w = hl.take()
                v = u.FL[:, 512 * q:512 * q + 512].rearrange("p (g n) -> p g n", g=8)
                a = af(hl.ap[:, :, 0, :], v, ACT.Copy, [u.s0, *w])
                b = tt(pool, hl.ap[:, :, 1, :], v, hl.ap[:, :, 0, :], ALU.subtract, [a, u.s0, *w])
                return hl, b

            def turn(hl, b, k):
                tb, bk = TB.next(), tr.next()
                v = bk.ap[:, 0:256].bitcast(F16)
                w = bk.take()
                for g in range(4):
                    n = 128 * (3 - g)
                    m_ = tp(v[:, n:n + 128], hl.ap[:, 4 * k + g].rearrange("p s n -> p (s n)"), idh[:, :],
                            [b, k_idh, *w], g == 3)
                if k == 1:
                    hl.free = [m_]
                c_ = cp(dve, tb.ap, v, [m_, *tb.take()])
                bk.free = [c_]
                return tb, c_

            def sliding(tab, n):
                v = tab[:, n:n + 128]
                return bass.AP(v.tensor, v.offset, [[640, 128], [4, 4], [1, 128]])

            def hidden_mix(u, h, m):
                def out_(g):
                    bk, w, k, gb, z = m
                    n, f = 256 * k + 64 * g, 128 * (3 - g)
                    return mm(bk.ap[:, n:n + 64], gb.ap[:, f:f + 128], w2b[:, :], True, True, [z, *w], g == 3)

                m_ = hb = None
                if h:
                    q, k, tb, ready = h
                    bk = gr.next()
                    o4 = bk.ap[:, :].rearrange("p (g n) -> p g n", g=4)
                    n = 128 + u.i0 - 32 * q - 16 * k - 12
                    w = [*bk.take(), *tabs, k_idh]
                for g in range(4):
                    if h:
                        if g < 2:
                            mm(o4, idh[:, :], sliding((ct_h, ct_l)[g], n), g == 0, False, w)
                        else:
                            e = mm(bk.ap[:, :], (ws_h, ws_l)[g - 2][:, :], tb.ap, False, g == 3, [ready], g == 3)
                    if m:
                        m_ = out_(g)
                if m:
                    m[3].free = [m_]
                if h:
                    tb.free = [e]
                    gb = GB.next()
                    z = af(gb.ap, bk.ap[:, :], ACT.Gelu, [e, *gb.take()], bias=b1c[:, 0:1])
                    bk.free = [z]
                    hb = (gb, z)
                return hb, m_

            def mlp(u):
                nq = 4 * (u.it + 1)
                order = list(range(nq - 4, nq)) + list(range(nq - 4))
                steps = [(q, k) for q in order for k in range(2)]
                cuts = [cut(u, q) for q in order[:2]]
                ta, hb, u.marks = [], [], []
                for n in range(len(steps) + 3):
                    if n < len(steps):
                        q, k = steps[n]
                        if k == 0 and n // 2 + 2 < len(order):
                            cuts.append(cut(u, order[n // 2 + 2]))
                        ta.append(turn(*cuts[n // 2], k))
                    h = m = None
                    if 1 <= n <= len(steps):
                        h = (*steps[n - 1], *ta[n - 1])
                    if n >= 3:
                        q, k = steps[n - 3]
                        if k == 0:
                            wb = qk_ring.next()
                            ww = wb.take()
                        m = (wb, ww, k, *hb[n - 3])
                    r, m_ = hidden_mix(u, h, m)
                    if r:
                        hb.append(r)
                    if n >= 3 and k == 1:
                        fv = u.FL[:, 512 * q:512 * q + 512]
                        f_ = tt(dve, fv, fv, wb.ap[:, :], ALU.add, [m_, cuts[(n - 3) // 2][1]])
                        wb.free = [f_]
                        if q >= nq - 4:
                            d = 32 * q - u.i0
                            v = fv.rearrange("p (a h b) -> p a h b", h=16, b=4)
                            p_ = pool.add(lambda e, v=v, d=d: e.affine_select(
                                out=v, in_=v, compare_op=ALU.is_ge, fill=-3.0e38, base=-d,
                                pattern=[[-4, 8], [0, 16], [-1, 4]], channel_multiplier=1), [f_])
                            u.marks.append(p_)
                u.marks.append(f_)

            def maxima(u, ha, hb):
                hs = slice(ha, hb)
                v = u.F[:, 0:u.J // 4, hs, :].rearrange("p a h b -> p h a b")
                b = dve.add(lambda e: e.tensor_reduce(mx[:, hs], v, mybir.AxisListType.XY, ALU.max),
                            [*u.marks, *st["mx"]])
                b = ts(dve, mx[:, hs], mx[:, hs], -1.0, None, ALU.mult, after=[b])
                u.mx += [b] * (hb - ha)

            MAXIMA = {0: (0, 1), 1: (1, 2), 2: (2, 4), 4: (4, 8), 6: (8, 12), 10: (12, 16)}

            def window(u, nxt):
                J, it, c = u.J, u.it, u.c
                ex, tps = [], []
                groups = {6: (0, 7), 13: (7, 14), 15: (14, 16)}
                for k in range(20):
                    if k in MAXIMA:
                        maxima(u, *MAXIMA[k])
                    if k < 16:
                        pb = PB.next()
                        e_ = af(pb.ap[:, 0:J].rearrange("p (a b) -> p a b", b=4), u.F[:, 0:J // 4, k, :], ACT.Exp,
                                [u.mx[k], *pb.take()], bias=mx[:, k:k + 1])
                        ex.append((pb, e_))
                        st["f"][k] = [e_]
                    if 1 <= k <= 16:
                        pb, e_ = ex[k - 1]
                        bk, tb = tr.next(), TP.next()
                        w = bk.take()
                        for jt in range(it + 1):
                            m = tp(bk.ap[:, 128 * jt:128 * jt + 128], pb.ap[:, 128 * jt:128 * jt + 128], ident,
                                   [e_, *w], jt == it)
                        pb.free = [m]
                        a = af(tb.ap[:, 0:J], bk.ap[:, 0:J], ACT.Copy, [m, *tb.take()])
                        bk.free = [a]
                        tps.append((tb, a))
                    if nxt and 1 <= k <= 16:
                        score(nxt, k - 1)
                    if 2 <= k <= 17:
                        h = k - 2
                        tb, a = tps[h]
                        if h in (0, 7, 14):
                            w = pvb.take()
                        o_ = pvb.ap[:, 65 * (h % 7):65 * (h % 7) + 65]
                        for jt in range(it + 1):
                            m = mm(o_, tb.ap[:, 128 * jt:128 * jt + 128], VX[jt][:, h, :], jt == 0, jt == it,
                                   [a, st["v"], v1, *w], jt == it)
                        tb.free = [m]
                        if h in groups:
                            ha, hb = groups[h]
                            n = hb - ha
                            v = pvb.ap[:, 0:65 * n].rearrange("p (h d) -> p h d", h=n)
                            a = dve.add(lambda e, v=v, ha=ha, hb=hb: e.reciprocal(rd[:, ha:hb], v[:, :, 64]), [m])
                            o2 = OO[:, 64 * ha:64 * hb].rearrange("p (h d) -> p h d", h=n)
                            b = tt(dve, o2, v[:, :, 0:64], rd[:, ha:hb].unsqueeze(2).to_broadcast([128, n, 64]),
                                   ALU.mult, [a, *st["oo"], *wf])
                            pvb.free = [b]
                st["mx"] = [ex[-1][1]]
                st["vx"] = [m]
                u.b = b

            def project_out(u):
                c, it, b = u.c, u.it, u.b
                tbs = []
                for q in range(2):
                    bk, tb = tr.next(), TP.next()
                    w = bk.take()
                    for i in range(4):
                        n = 512 * q + 128 * i
                        m = tp(bk.ap[:, 128 * i:128 * i + 128], OO[:, n:n + 128], ident, [b, *w], i == 3)
                    a = af(tb.ap, bk.ap[:, :], ACT.Copy, [m, *tb.take()])
                    bk.free = [a]
                    tbs.append((tb, a))
                    yield
                st["oo"] = [m]
                w = pvb.take()
                for q in range(2):
                    tb, a = tbs[q]
                    for i in range(4):
                        m = mm(pvb.ap[:, 0:128], tb.ap[:, 128 * i:128 * i + 128], wo[:, 4 * q + i, :],
                               q == 0 and i == 0, q == 1 and i == 3, [a, *w], i == 3)
                    tb.free = [m]
                xv = x[:, 4 * c + it, :]
                f = tt(dve, xv, pvb.ap[:, 0:128], xv, ALU.add, [m])
                pvb.free = [f]
                x_done[c].append(f)
                u.end = [m, f]

            def unit(c, it):
                u = Unit()
                u.c, u.it, u.i0, u.J = c, it, 128 * it, 128 * (it + 1)
                u.FL = FA[:, 0:16 * u.J]
                u.F = u.FL.rearrange("p (a h b) -> p a h b", h=16, b=4)
                u.mx = []
                return u

            units = [unit(c, it) for c in range(4) for it in (3, 2, 1, 0)]
            project_qk(0)
            for h in range(16):
                score(units[0], h)
            project_v(0)
            for u, nxt in zip(units, [*units[1:], None]):
                mlp(u)
                if nxt and nxt.it == 3:
                    project_qk(nxt.c)
                window(u, nxt)
                if nxt and nxt.it == 3:
                    project_v(nxt.c)
                for _ in project_out(u):
                    pass
            m_v = st["v"]
            prev = u
            xt_free = [m_v]
            return x_done, prev.end

        work_free, reg0_free = [], []
        k_rf = got("a0")
        fr = Ring([PS[1], PS[2]])
        fold(wq_h, wq_l, [s_qk[:, p, :] for p in range(8)], [s_rf[:, p, :] for p in range(8)], 2, [k_rf], fr)
        k_fold0 = fold(wkr_h, wkr_l, [s_qk[:, 8 + p, :] for p in range(8)], [s_rf[:, p, :] for p in range(8)], 2,
                       [k_rf], fr)
        k_fold1 = fold(wk_h, wk_l, [s_wqT[:, p, :] for p in range(4)], [s_key[:, p, :] for p in range(4)], 1,
                       [got("f1")], fr)

        xr, free = ffn0([[got(f"x{c}")] for c in range(4)])
        k_wa = []
        stage = Ring([Slot(wk(16400 + 1024 * i, 1024)) for i in range(5)])
        for i in range(5):
            s_ = stage.next()
            load(f"wa{i}", s_.ap, t["wa"][:, 1024 * i:1024 * i + 1024], [k_fold1, k_fold0, k_de, k_gu, k_wv])
            k_wa.append(split(wa_h[:, 1024 * i:1024 * i + 1024], wa_l[:, 1024 * i:1024 * i + 1024], s_.ap,
                              [got(f"wa{i}")], pool))
        work_free = free
        xr, free = attn0(xr)
        work_free = free
        xr, free = ffn0(xr)
        work_free = [*free, *k_wa]
        reg0_free = free
        xr, free = ffn1(xr)
        work_free = free
        load("dst", wk(0, 512), t["c_dn"], work_free)
        load("dst", wk(512, 640), t["c_dt"], work_free)
        load("dst", wk(9984, 128), t["w1d"], work_free)
        load("dst", wk(10112, 128)[0:64, :], t["w1k"], work_free)
        s_park = sem("s_park")
        sp.add(lambda e: e.dma_start(parked, park[:, 0:3072]).then_inc(s_park, 16), [k_gu, k_de, k_fold1, got("f1")],
               False)
        xr, free = attn1([[*w_, (s_park, 16)] for w_ in xr])
        work_free = free
        load("back", park[:, 0:3072], parked, [(s_park, 16), *free])
        k_gu = k_de = k_fold1 = got("back")
        xr, free = ffn1(xr)
        od = out.rearrange("b (q p) d -> p (b q) d", p=128)
        s_out = sem("s_out")
        for c in range(4):
            sp.add(lambda e, c=c: e.dma_start(od[:, 4 * c:4 * c + 4, :], x[:, 4 * c:4 * c + 4, :]).then_inc(s_out, 16),
                   xr[c], False)
        sp.add(lambda e: e.wait_ge(s_out, 64), (), False)

        block = ctx.enter_context(nc.Block())

        @block.sync
        def _(e):
            sp.issue(e)

        @block.tensor
        def _(e):
            pe.issue(e)

        @block.scalar
        def _(e):
            act.issue(e)

        @block.vector
        def _(e):
            dve.issue(e)

        @block.gpsimd
        def _(e):
            pool.issue(e)


def _layout(i):
    import numpy as np
    f4 = np.float32
    g = {k: np.asarray(v) for k, v in i.items()}
    t = {"x": g["L0_attn_x"]}
    t["w_gate"] = g["L0_ffn_w_gate"].T
    t["w13"] = np.concatenate([g["L0_ffn_w1_e"].reshape(1024, 128), g["L0_ffn_w1_s"],
                               g["L0_ffn_w3_e"].reshape(1024, 128), g["L0_ffn_w3_s"]]).T
    w2 = np.concatenate([g["L0_ffn_w2_e"].transpose(0, 2, 1).reshape(1024, 128), g["L0_ffn_w2_s"].T])
    t["w2"] = w2.reshape(9, 128, 128).transpose(1, 0, 2)

    def pairs(a):
        b = np.zeros((a.shape[0] // 2, 128, 128), f4)
        b[:, :64, :64] = a[0::2]
        b[:, 64:, 64:] = a[1::2]
        return b.transpose(1, 0, 2)

    wqkv = g["L0_attn_W_qkv"]
    t["wqkT"] = wqkv[:, :2048].T.reshape(16, 128, 128).transpose(1, 0, 2)
    t["wv0"] = wqkv[:, 2048:]
    t["rf"] = pairs(g["L0_attn_RF"])
    t["wout"] = g["L0_attn_W_out"].reshape(8, 128, 128).transpose(1, 0, 2)
    t["wgu"] = np.concatenate([g["L1_ffn_Wg"], g["L1_ffn_Wu"]], axis=1)
    t["wqT"] = g["L1_ffn_Wq"].T.reshape(4, 128, 128).transpose(1, 0, 2)
    t["keys"] = pairs(g["L1_ffn_keys"].transpose(2, 0, 3, 1).reshape(8, 64, 64))
    t["deT"] = g["L1_ffn_down_embed"].T
    t["wdue"] = np.concatenate([g["L1_ffn_Wd"], g["L1_ffn_up_embed"]]).reshape(8, 128, 128).transpose(1, 0, 2)
    t["bgu"] = np.concatenate([g["L1_ffn_bg"], g["L1_ffn_bu"]]).reshape(8, 128).T
    t["rows"] = np.concatenate([g["L0_attn_b_out"], g["L1_ffn_bd"]])[None]
    w = g["L1_attn_w_qkv"]

    def turned(a):
        return a.reshape(128, 16, 2, 32)[:, :, ::-1].reshape(128, 1024)

    t["wa"] = np.concatenate([w[:, :1024], turned(w[:, :1024]), w[:, 1024:2048], turned(w[:, 1024:2048]),
                              w[:, 2048:]], axis=1)
    t["wo"] = g["L1_attn_w_o"].reshape(8, 128, 128).transpose(1, 0, 2)

    def spaced(a):
        b = np.zeros((a.shape[0], 4, a.shape[1], 4), f4)
        for j in range(4):
            b[:, j, :, j] = a
        return b.reshape(a.shape[0] * 4, a.shape[1] * 4)

    w1 = g["L1_attn_w1"]
    t["w1d"] = np.concatenate([spaced(w1[:16])] * 2)
    t["w1k"] = spaced(w1[16:])
    t["w2b"] = spaced(g["L1_attn_w2"])
    t["b1c"] = np.repeat(g["L1_attn_b1"], 4)[:, None]
    t["b2r"] = np.repeat(g["L1_attn_b2"], 4)[:, None]
    t["b2b"] = np.tile(g["L1_attn_b2"][None], (128, 1))
    lp, la = g["L1_attn_log_p"].reshape(16), g["L1_attn_log_a"].reshape(16)
    t["lp_c"] = np.tile(np.repeat(lp, 4), 2)[:, None]
    t["la_c"] = np.tile(np.repeat(la, 4), 2)[:, None]
    t["pab"] = np.tile(np.stack([lp, la])[None], (128, 1, 1))
    t["c_id"] = np.eye(128, dtype=f4)
    e = np.arange(48)[:, None, None] % 16
    t["c_sel"] = (e == 2 * np.arange(8)[None, :, None] + np.arange(128)[None, None] // 64).astype(f4)
    q = np.arange(4)
    t["c_tri"] = np.tile((q[None, :] < q[:, None]).astype(f4)[None], (128, 1, 1))
    inv = (f4(1.0) / np.power(f4(10000.0), np.arange(0, 64, 2, dtype=f4) / f4(64))).astype(f4)
    fr = np.outer(np.arange(512, dtype=f4), inv).astype(f4)
    emb = np.concatenate([fr, fr], -1)
    sign = np.where(np.arange(64) < 32, f4(-1), f4(1))
    t["c_rope"] = np.stack([np.tile(np.cos(emb).astype(f4).T, (2, 1)),
                            np.tile((np.sin(emb).astype(f4) * sign).T, (2, 1))], axis=1)
    p = np.arange(128)[:, None]
    t["c_dn"] = np.abs(p + 384 - np.arange(512)[None]).astype(f4)
    t["c_dt"] = np.abs(np.arange(640)[None] - 128 - p % 4).astype(f4)
    return {k: np.ascontiguousarray(v) for k, v in t.items()}


def kernel(**inputs):
    import numpy as _np
    import concourse.bacc as _bacc
    from concourse import mybir as _mybir
    from concourse.bass_utils import run_bass_kernel_spmd as _run

    nc = _bacc.Bacc("TRN2", target_bir_lowering=False, num_devices=1)
    arrays, t = {}, {}
    for name, a in _layout(inputs).items():
        arrays[f"in_{name}_dram"] = a
        t[name] = nc.dram_tensor(f"in_{name}_dram", a.shape, _mybir.dt.from_np(a.dtype), kind="ExternalInput").ap()
    o = nc.dram_tensor("out_0_dram", (4, 512, 128), _mybir.dt.float32, kind="ExternalOutput").ap()
    build(nc, t, o)
    r = _run(nc, [arrays], core_ids=[0])
    return r.results[0]["out_0_dram"]
```

```python
from contextlib import ExitStack

from concourse import bass, mybir

F32 = mybir.dt.float32
F16 = mybir.dt.float16
BF16 = mybir.dt.bfloat16
ALU = mybir.AluOpType
ACT = mybir.ActivationFunctionType
AX_X = mybir.AxisListType.X


class Lane:

    def __init__(self, sem):
        self.sem = sem
        self.items = []
        self.n = 0

    def add(self, fn, after=(), mark=True):
        self.items.append((fn, tuple(after), mark))
        if mark:
            self.n += 1
        return (self.sem, self.n)

    def issue(self, eng):
        seen = {}
        for fn, after, mark in self.items:
            for sem, value in after:
                if seen.get(sem.name, 0) < value:
                    eng.wait_ge(sem, value)
                    seen[sem.name] = value
            ins = fn(eng)
            if mark:
                ins.then_inc(self.sem, 1)


class Slot:

    def __init__(self, ap):
        self.ap = ap
        self.free = []

    def take(self):
        waits, self.free = self.free, []
        return waits


class Ring:
    def __init__(self, slots):
        self.slots = slots
        self.i = 0

    def next(self):
        s = self.slots[self.i % len(self.slots)]
        self.i += 1
        return s


def build(nc, t, out):
    with ExitStack() as ctx:
        def sb(name, shape, dt=F32):
            return ctx.enter_context(nc.sbuf_tensor(name, shape, dt))

        def sem(name):
            return ctx.enter_context(nc.semaphore(name))

        pe, act, dve, pool, sp = (Lane(sem(n)) for n in ("s_pe", "s_act", "s_dve", "s_pool", "s_sp"))
        PS = [Slot(ctx.enter_context(nc.psum_tensor(f"ps{i}", [128, 512], F32))) for i in range(8)]

        x = sb("x", [128, 16, 128])
        xth = sb("xth", [128, 2048], F16)
        xtl = sb("xtl", [128, 2048], F16)
        idf = sb("idf", [128, 128])
        idb = sb("idb", [128, 128], BF16)
        ones = sb("ones", [128, 128])
        tri = sb("tri", [128, 4, 4])
        small = sb("small", [128, 1024])

        park = sb("park", [128, 4096])

        def half(a, n):
            return park[:, a:a + n // 2].bitcast(F16)

        wgu_h, wgu_l = half(0, 1024), half(512, 1024)
        wk_h, wk_l = half(1024, 512), half(1280, 512)
        de_h, de_l = half(1536, 512), half(1792, 512)
        wdue = park[:, 2048:3072].rearrange("p (b n) -> p b n", b=8)
        parked = nc.dram_tensor("parked", (128, 3072), F32, kind="Internal").ap()
        bgu = sb("bgu", [128, 8])
        rows = sb("rows", [1, 256])

        wa_h, wa_l = sb("wa_h", [128, 5120], F16), sb("wa_l", [128, 5120], F16)
        wo_h, wo_l = sb("wo_h", [128, 1024], F16), sb("wo_l", [128, 1024], F16)
        cs = sb("cs", [128, 2, 512])
        ws_h, ws_l = sb("ws_h", [128, 128], F16), sb("ws_l", [128, 128], F16)
        idh = sb("idh", [128, 128], F16)
        w2b = sb("w2b", [128, 64])
        b1c = sb("b1c", [128, 1])
        b2r = sb("b2r", [128, 1])
        ct_h, ct_l = sb("ct_h", [128, 640], F16), sb("ct_l", [128, 640], F16)
        pa = sb("pa", [128, 4])
        pab = sb("pab", [128, 2, 16])
        b2b = sb("b2b", [128, 16])

        scr = sb("scr", [128, 2080])

        reg0 = sb("reg0", [128, 8192])
        o = 0

        def r0(n, dt=F32):
            nonlocal o
            w = n if dt == F32 else n // 2
            v = reg0[:, o:o + w]
            o += w
            return v if dt == F32 else v.bitcast(dt)

        w13_h, w13_l = r0(2304, F16), r0(2304, F16)
        w2 = r0(1152).rearrange("p (b n) -> p b n", b=9)
        wg_h, wg_l = r0(16, F16), r0(16, F16)
        wq_h, wq_l = r0(1024, F16), r0(1024, F16)
        wkr_h, wkr_l = r0(1024, F16), r0(1024, F16)
        wv_h, wv_l = r0(1024, F16), r0(1024, F16)
        wout = r0(1024).rearrange("p (b n) -> p b n", b=8)
        sel = r0(1024, BF16)[0:48, :].rearrange("p (b n) -> p b n", b=8)
        assert o <= 8192
        kn = reg0[:, :].rearrange("p (h v) -> p h v", h=16)

        NW = 24608
        work = sb("work", [128, NW])

        def wk(a, n, dt=F32):
            assert a + n <= NW
            v = work[:, a:a + n]
            return v if dt == F32 else v.bitcast(dt)

        ctb = wk(23000, 1024, BF16)[0:48, :]

        def mm(o_, l, r, start, stop, after=(), mark=False):
            return pe.add(lambda e: e.matmul(o_, l, r, start=start, stop=stop), after, mark)

        def tp(o_, i_, ident, after=(), mark=False):
            return pe.add(lambda e: e.transpose(o_, i_, ident), after, mark)

        def af(o_, i_, f, after=(), **kw):
            return act.add(lambda e: e.activation(o_, i_, f, **kw), after)

        def tt(lane, o_, a, b, op, after=()):
            return lane.add(lambda e: e.tensor_tensor(o_, a, b, op), after)

        def ts(lane, o_, a, s1, s2, op0, op1=None, after=()):
            if op1 is None:
                return lane.add(lambda e: e.tensor_scalar(o_, a, s1, None, op0), after)
            return lane.add(lambda e: e.tensor_scalar(o_, a, s1, s2, op0, op1), after)

        def stt(o_, a, s, b, op0, op1, after=(), **kw):
            return dve.add(lambda e: e.scalar_tensor_tensor(out=o_, in0=a, scalar=s, in1=b, op0=op0, op1=op1, **kw),
                           after)

        def cp(lane, o_, i_, after=()):
            return lane.add(lambda e: e.tensor_copy(o_, i_), after)

        def red(o_, i_, op, after=()):
            return dve.add(lambda e: e.tensor_reduce(o_, i_, AX_X, op), after)

        def ms(lane, o_, v, after=()):
            return lane.add(lambda e: e.memset(o_, v), after)

        loads = {}

        def load(key, dst, src, after=(), lane=sp):
            if key not in loads:
                loads[key] = [sem(f"l_{key}"), 0]
            s = loads[key]
            s[1] += 16
            sm = s[0]
            lane.add(lambda e: e.dma_start(dst, src).then_inc(sm, 16), after, False)

        def got(key):
            return (loads[key][0], loads[key][1])

        xin = t["x"].rearrange("b (q p) d -> p (b q) d", p=128)
        for c in range(4):
            load(f"x{c}", x[:, 4 * c:4 * c + 4, :], xin[:, 4 * c:4 * c + 4, :])
        load("id", idf[:, :], t["c_id"])
        st = 14000
        s_w13 = wk(st, 2304)
        s_gate = wk(st + 2304, 16)
        load("w13", s_gate, t["w_gate"])
        load("w13", s_w13, t["w13"])
        load("cst", tri[:, :, :], t["c_tri"])
        load("cst", wk(23000, 1024)[0:48, :].rearrange("p (b n) -> p b n", b=8), t["c_sel"])
        load("w2", w2, t["w2"])
        s_qk = wk(st + 2320, 2048).rearrange("p (b n) -> p b n", b=16)
        s_wv = wk(st + 4368, 1024)
        s_rf = wk(st + 5392, 1024).rearrange("p (b n) -> p b n", b=8)
        load("a0", s_qk, t["wqkT"])
        load("a0", s_rf, t["rf"])
        load("a0", s_wv, t["wv0"])
        load("a0", wout, t["wout"])
        s_gu = wk(st + 6416, 1024)
        s_wqT = wk(st + 7440, 512).rearrange("p (b n) -> p b n", b=4)
        s_key = wk(st + 7952, 512).rearrange("p (b n) -> p b n", b=4)
        s_de = wk(st + 8464, 512)
        load("f1", s_gu, t["wgu"])
        load("f1", s_wqT, t["wqT"])
        load("f1", s_key, t["keys"])
        load("f1", s_de, t["deT"])
        load("f1", wdue, t["wdue"])
        load("f1", bgu[:, :], t["bgu"])
        load("f1", rows[:, :], t["rows"])
        load("a1", cs[:, :, :], t["c_rope"])
        load("a1", w2b[:, :], t["w2b"])
        load("a1", b1c[:, :], t["b1c"])
        load("a1", b2r[64:128, :], t["b2r"])
        load("a1", pa[:, 0:1], t["lp_c"])
        load("a1", pa[:, 1:2], t["la_c"])
        load("a1", pab[:, :, :], t["pab"])
        load("a1", b2b[:, :], t["b2b"])

        load("dst", scr[:, 0:640], t["c_dt"])
        load("dst", scr[:, 640:1152], t["c_dn"])
        load("dst", scr[:, 1152:1280], t["w1d"])
        load("dst", scr[0:64, 1280:1408], t["w1k"])

        k_ones = ms(dve, ones[:, :], 1.0)
        k_idb = cp(dve, idb[:, :], idf[:, :], [got("id")])
        k_idh = cp(dve, idh[:, :], idf[:, :], [got("id")])
        k_idf = got("id")

        def split(hi, lo, src, after, lane):
            a = af(hi, src, ACT.Copy, after)
            return tt(lane, lo, src, hi, ALU.subtract, [a, *after])

        def fold(dst_h, dst_l, lefts, rights, n, after, ring):
            done = []
            for q in range(n):
                bk = ring.next()
                w = bk.take()
                for j in range(4):
                    m = mm(bk.ap[:, 128 * j:128 * j + 128], lefts[4 * q + j], rights[4 * q + j], True, True,
                           [*after, *w], j == 3)
                h, l = dst_h[:, 512 * q:512 * q + 512], dst_l[:, 512 * q:512 * q + 512]
                a = af(h, bk.ap[:, :], ACT.Copy, [m])
                d = tt(dve, l, bk.ap[:, :], h, ALU.subtract, [a, m])
                bk.free = [d]
                done.append(d)
                yield
            return done[-1]

        mv = small[:, 0:32].rearrange("p (t s) -> p t s", s=2)
        rs = small[:, 32:96].rearrange("p (k t) -> p k t", t=16)
        bst = small[:, 96:192].rearrange("p (t s) -> p t s", s=6)
        XH = [Slot(park[:, 3072 + 512 * i:3584 + 512 * i]) for i in range(2)]
        xh_ring = Ring(XH)
        EPS = 1e-5

        behind = []

        def tick(n=1):
            for _ in range(n):
                if behind and next(behind[0], behind) is behind:
                    behind.pop(0)

        def layernorm(c, ready, xt_wait, xs, bk):
            r = slice(4 * c, 4 * c + 4)
            for i in range(4 * c, 4 * c + 4):
                b = dve.add(lambda e, i=i: e.bn_stats(bst[:, i, :], x[:, i, :]), ready)
            yield
            for i in range(4 * c, 4 * c + 4):
                a = dve.add(lambda e, i=i: e.bn_aggr(mv[:, i, :], bst[:, i, :]), [b])
            v = ts(dve, rs[:, 0, r], mv[:, r, 1], EPS, None, ALU.add, after=[a])
            s_ = af(rs[:, 1, r], rs[:, 0, r], ACT.Sqrt, [v])
            i0 = dve.add(lambda e: e.reciprocal(rs[:, 2, r], rs[:, 1, r]), [s_])
            yield
            n1 = tt(dve, rs[:, 1, r], rs[:, 2, r], rs[:, 2, r], ALU.mult, [i0])
            n2 = tt(dve, rs[:, 1, r], rs[:, 1, r], rs[:, 0, r], ALU.mult, [n1, v])
            n3 = ts(dve, rs[:, 1, r], rs[:, 1, r], -0.5, 1.5, ALU.mult, ALU.add, [n2])
            n4 = tt(dve, rs[:, 2, r], rs[:, 2, r], rs[:, 1, r], ALU.mult, [n3])
            yield
            xv = xs.ap[:, 0:512].rearrange("p (t d) -> p t d", t=4)
            w = xs.take()
            for j in range(4):
                i = 4 * c + j
                h = ts(dve, xv[:, j, :], x[:, i, :], mv[:, i, 0:1], rs[:, 2, i:i + 1], ALU.subtract,
                       ALU.mult, [n4, *w])
            yield
            yield
            w = bk.take()
            for j in range(4):
                m = tp(bk.ap[:, 128 * j:128 * j + 128], xv[:, j, :], idf[:, :], [h, k_idf, *w], j == 3)
            xs.free = [m]
            s_ = slice(512 * c, 512 * c + 512)
            a = af(xth[:, s_], bk.ap[:, :], ACT.Copy, [m, *xt_wait])
            d = tt(dve, xtl[:, s_], bk.ap[:, :], xth[:, s_], ALU.subtract, [a, m, *xt_wait])
            bk.free = [d]
            yield
            return d

        def run(gen):
            while True:
                try:
                    next(gen)
                except StopIteration as end:
                    return end.value

        def norm_only(c, ready, xt_wait, xs, bk):
            d = yield from layernorm(c, ready, xt_wait, xs, bk)
            return (d,)

        def proj_t(o_, wh, wl, c, after, mark=True):
            s_ = slice(512 * c, 512 * c + 512)
            mm(o_, wh, xth[:, s_], True, False, after)
            mm(o_, wh, xtl[:, s_], False, False)
            return mm(o_, wl, xth[:, s_], False, True, mark=mark)

        def proj_n(o_, wh, wl, i, after, mark=True):
            s_ = slice(128 * i, 128 * i + 128)
            mm(o_, xth[:, s_], wh, True, False, after)
            mm(o_, xth[:, s_], wl, False, False)
            return mm(o_, xtl[:, s_], wh, False, True, mark=mark)

        def weave(main, side, ratio):
            debt = 0
            for _ in main:
                debt += ratio
                while debt >= 1:
                    debt -= 1
                    next(side, None)
            for _ in side:
                pass

        def passes_n(o_, wh, wl, i, waits):
            s_ = slice(128 * i, 128 * i + 128)
            mm(o_, xth[:, s_], wh, True, False, waits)
            yield
            mm(o_, xth[:, s_], wl, False, False)
            yield
            return mm(o_, xtl[:, s_], wh, False, True, mark=True)

        def passes_t(o_, wh, wl, c, waits):
            s_ = slice(512 * c, 512 * c + 512)
            mm(o_, wh, xth[:, s_], True, False, waits)
            yield
            mm(o_, wh, xtl[:, s_], False, False)
            yield
            return mm(o_, wl, xth[:, s_], False, True, mark=True)

        spl = small[:, 192:576].bitcast(BF16).rearrange("p (t k e) -> p t k e", t=16, k=3)
        rem = small[:, 576:832].rearrange("p (t e) -> p t e", t=16)
        ct_free = []

        def spread(src, tiles, after, bk):
            nonlocal ct_free
            r = slice(tiles[0], tiles[-1] + 1)
            a = cp(dve, spl[:, r, 0, :], src, after)
            b = tt(dve, rem[:, r, :], src, spl[:, r, 0, :], ALU.subtract, [a, *after])
            a = cp(dve, spl[:, r, 1, :], rem[:, r, :], [b])
            b = tt(dve, spl[:, r, 2, :], rem[:, r, :], spl[:, r, 1, :], ALU.subtract, [a])
            yield
            yield
            done = []
            for q in range(len(tiles) // 4):
                w = bk.take()
                v = bk.ap[0:48, 0:256].bitcast(BF16)
                for j in range(4):
                    i = tiles[4 * q + j]
                    m = tp(v[:, 128 * j:128 * j + 128], spl[:, i, :, :].rearrange("p k e -> p (k e)"), idb[:, :],
                           [b, k_idb, *w], j == 3)
                s_ = slice(128 * tiles[4 * q], 128 * tiles[4 * q] + 512)
                d = cp(dve, ctb[:, s_], v, [m, *ct_free])
                bk.free = [d]
                done.append(d)
            ct_free = []
            return done

        G = wk(24024, 400)
        S = G[:, 0:64].rearrange("p (t e) -> p t e", t=4)
        S4 = G[:, 0:64].rearrange("p (t g e) -> p t g e", t=4, g=4)
        A1 = G[:, 64:96].rearrange("p (t g e) -> p t g e", t=4, g=4)
        A2 = G[:, 96:128].rearrange("p (t g e) -> p t g e", t=4, g=4)
        g1, g2, g3 = (G[:, 128 + 16 * i:144 + 16 * i].rearrange("p (t g) -> p t g", t=4) for i in range(3))
        q1 = G[:, 176:240].rearrange("p (t g e) -> p t g e", t=4, g=4)
        q2 = G[:, 240:304].rearrange("p (t g e) -> p t g e", t=4, g=4)
        q2f = G[:, 240:304].rearrange("p (t e) -> p t e", t=4)
        q1f = G[:, 176:240].rearrange("p (t e) -> p t e", t=4)
        m8 = G[:, 304:336].rearrange("p (t e) -> p t e", t=4)
        w1_ = G[:, 336:340]
        gate_free = []

        def norm_and_route(c, ready, xt_wait, xs, bk):
            nonlocal gate_free
            xt = yield from layernorm(c, ready, xt_wait, xs, bk)
            yield
            w = bk.take()
            for i in range(4):
                m = proj_n(bk.ap[:, 16 * i:16 * i + 16], wg_h, wg_l, 4 * c + i, [xt, k_gate, *w], i == 3)
            z = af(G[:, 0:64], bk.ap[:, 0:64], ACT.Sigmoid, [m, *gate_free, *work_free])
            bk.free = [z]
            yield
            a = tt(dve, A1, S4[:, :, :, 0:2], S4[:, :, :, 2:4], ALU.max, [z])
            b = tt(dve, A2, S4[:, :, :, 0:2], S4[:, :, :, 2:4], ALU.min, [z])
            c_ = tt(dve, g1, A1[:, :, :, 0], A1[:, :, :, 1], ALU.max, [a])
            d = tt(dve, g2, A1[:, :, :, 0], A1[:, :, :, 1], ALU.min, [a])
            yield
            f = tt(dve, g3, A2[:, :, :, 0], A2[:, :, :, 1], ALU.max, [b])
            f = tt(dve, g2, g2, g3, ALU.max, [d, f])
            f = tt(dve, g1, g1, g2, ALU.add, [c_, f])
            other = g1.unsqueeze(2).to_broadcast([128, 4, 4, 4])
            own = g1.unsqueeze(3).to_broadcast([128, 4, 4, 4])
            yield
            a = tt(dve, q1, other, own, ALU.is_gt, [f])
            b = tt(dve, q2, other, own, ALU.is_equal, [f])
            trb = tri[:, :, :].unsqueeze(1).to_broadcast([128, 4, 4, 4])
            b = tt(dve, q2, q2, trb, ALU.mult, [b, got("cst")])
            yield
            b = tt(dve, q1, q1, q2, ALU.add, [a, b])
            b = red(g2, q1, ALU.add, [b])
            b = ts(dve, g2, g2, 1.5, None, ALU.is_lt, after=[b])
            al = g2.unsqueeze(3).to_broadcast([128, 4, 4, 4])
            yield
            a = tt(dve, q1, S4, al, ALU.mult, [b])
            b = ts(dve, g3, g2, -1.0, None, ALU.add, after=[b])
            am = g3.unsqueeze(3).to_broadcast([128, 4, 4, 4])
            a = tt(dve, q1, q1, am, ALU.add, [a, b])
            yield
            for i in range(4):
                b = dve.add(lambda e, i=i: e.max(m8[:, i, :], q1f[:, i, :]), [a])
            yield
            thr = m8[:, :, 3:4].to_broadcast([128, 4, 16])
            b = tt(dve, q2f, q1f, thr, ALU.is_ge, [b])
            b = tt(dve, q2f, q2f, S, ALU.mult, [b])
            a = red(w1_, q2f, ALU.add, [b])
            yield
            a = ts(dve, w1_, w1_, 1e-6, None, ALU.add, after=[a])
            a = dve.add(lambda e: e.reciprocal(w1_, w1_), [a])
            a = tt(dve, q2f, q2f, w1_.unsqueeze(2).to_broadcast([128, 4, 16]), ALU.mult, [a, b])
            yield
            ct = yield from spread(q2f, list(range(4 * c, 4 * c + 4)), [a], bk)
            gate_free = ct
            return xt, ct[0]

        def ffn0(prep, after):
            nonlocal ct_free
            H = [Slot(wk(4608 * i, 4608).rearrange("p (b n) -> p b n", b=9)) for i in range(2)]
            SG = Ring([Slot(wk(9216 + 512 * i, 512)) for i in range(3)])
            HU = Ring([Slot(wk(10752 + 512 * i, 512)) for i in range(3)])
            gr, ur, cr = Ring([PS[0], PS[1]]), Ring([PS[2], PS[3]]), Ring([PS[4], PS[5]])
            x_done = []

            def up(c):
                xt, ct = prep(c)
                hs = H[c % 2]
                hw = hs.take()
                for b_ in range(9):
                    g_, u_ = gr.next(), ur.next()
                    n = 128 * b_
                    mg = yield from passes_t(g_.ap[:, :], w13_h[:, n:n + 128], w13_l[:, n:n + 128], c,
                                             [xt, k_w13, *g_.take()])
                    yield
                    n += 1152
                    mu = yield from passes_t(u_.ap[:, :], w13_h[:, n:n + 128], w13_l[:, n:n + 128], c, u_.take())
                    yield
                    sg = SG.next()
                    z = af(sg.ap, g_.ap[:, :], ACT.Silu, [mg, *sg.take(), *work_free])
                    g_.free = [z]
                    if b_ == 8:
                        f = tt(dve, hs.ap[:, b_, :], sg.ap, u_.ap[:, :], ALU.mult, [z, mu, *hw, *work_free])
                        sg.free = [f]
                        u_.free = [f]
                    else:
                        k_ = cr.next()
                        mc = mm(k_.ap[:, :], sel[:, b_, :], ctb[:, 512 * c:512 * c + 512], True, True,
                                [ct, k_sel, *k_.take()], True)
                        hu = HU.next()
                        y = tt(dve, hu.ap, sg.ap, u_.ap[:, :], ALU.mult, [z, mu, *hu.take(), *work_free])
                        sg.free = [y]
                        u_.free = [y]
                        f = tt(dve, hs.ap[:, b_, :], hu.ap, k_.ap[:, :], ALU.mult, [y, mc, *hw])
                        hu.free = [f]
                        k_.free = [f]
                        yield
                    tick(2)
                hd[c] = f
                read[c] = mu

            def down(c):
                bk = PS[6]
                w = bk.take()
                for j in range(4):
                    for b_ in range(9):
                        m = mm(bk.ap[:, 128 * j:128 * j + 128], H[c % 2].ap[:, b_, 128 * j:128 * j + 128], w2[:, b_, :],
                               b_ == 0, b_ == 8, [hd[c], got("w2"), *w], j == 3 and b_ == 8)
                        if not (j == 3 and b_ == 8):
                            yield
                H[c % 2].free = [m]
                xv = x[:, 4 * c:4 * c + 4, :].rearrange("p t d -> p (t d)")
                f = stt(xv, bk.ap[:, :], 0.5, xv, ALU.mult, ALU.add, [m])
                bk.free = [f]
                x_done.append([f])
                after(c, [f], [read[c]], xh_ring.next(), PS[7])
                hd[4] = m
                yield

            hd, read = [None] * 5, [None] * 4
            for c in range(5):
                weave(up(c) if c < 4 else [], down(c - 1) if c > 0 else iter(()), 0.6)
            m = hd[4]
            return x_done, [m, x_done[-1][0]]

        def attn0(prep, after):
            nonlocal ct_free
            PKH, PKL = (wk(2048 * i, 2048, F16).rearrange("p (t n) -> p t n", t=4) for i in range(2))
            VH, VL = (wk(4096 + 2064 * i, 2064, F16).rearrange("p (t b n) -> p t b n", t=4, b=8) for i in range(2))
            KVB = wk(12320, 1024).rearrange("p (b n) -> p b n", b=8)
            KS = wk(13344, 16).rearrange("p (b n) -> p b n", b=8)
            NR = wk(13360, 64).rearrange("p (t e) -> p t e", t=4)
            PQS = [wk(a, 4096).rearrange("p (b n) -> p b n", b=8) for a in (8224, 16496)]
            KVT = wk(13424, 1024).rearrange("p (b n) -> p b n", b=8)
            KWS = [wk(14448 + 1024 * i, 1024).rearrange("p (b n) -> p b n", b=8) for i in range(2)]
            NRf = NR.rearrange("p t e -> p (t e)")
            z1 = ms(dve, KVB, 0.0, work_free)
            ms(dve, KS, 0.0, work_free)
            ms(dve, VH[:, :, :, 128:129], 1.0, work_free)
            z1 = ms(dve, VL[:, :, :, 128:129], 0.0, work_free)
            x_done = []
            ring = Ring([PS[0], PS[1], PS[2], PS[3]])
            fr = {"pk": [], "kvb": [z1], "kvt": k_wa, "ks": [z1], "nr": [], "pq0": [], "pq1": k_wa, "kw0": k_wa,
                  "kw1": k_wa}

            class Chunk:
                pass

            def keys_values(u):
                for j in range(4):
                    for n in range(2):
                        s_ = slice(512 * n, 512 * n + 512)
                        w = [*fr["pk"], *work_free]
                        bk = ring.next()
                        m = yield from passes_n(bk.ap[:, :], wkr_h[:, s_], wkr_l[:, s_], 4 * u.c + j,
                                                [u.xt, k_fold0, *bk.take()])
                        a = af(PKH[:, j, s_], bk.ap[:, :], ACT.Relu, [m, *w])
                        u.kv = stt(PKL[:, j, s_], bk.ap[:, :], 0.0, PKH[:, j, s_], ALU.max, ALU.subtract, [a, m, *w])
                        bk.free = [u.kv]
                        yield
                        bk = ring.next()
                        m = yield from passes_n(bk.ap[:, :], wv_h[:, s_], wv_l[:, s_], 4 * u.c + j,
                                                [k_wv, *bk.take()])
                        v = bk.ap[:, :].rearrange("p (b n) -> p b n", b=4)
                        hi, lo = (y[:, j, 4 * n:4 * n + 4, 0:128] for y in (VH, VL))
                        a = af(hi, v, ACT.Copy, [m, *w])
                        u.kv = tt(dve, lo, v, hi, ALU.subtract, [a, m, *w])
                        bk.free = [u.kv]
                        tick(2)
                        yield

            def queries(u):
                for p in range(8):
                    bk = ring.next()
                    m = yield from passes_t(bk.ap[:, :], wq_h[:, 128 * p:128 * p + 128],
                                            wq_l[:, 128 * p:128 * p + 128], u.c, bk.take())
                    u.pq = af(u.PQ[:, p, :], bk.ap[:, :], ACT.Relu, [m, *fr[u.nq], *work_free])
                    bk.free = [u.pq]
                    tick(1)
                    yield
                u.xt_read = m

            def outer(u):
                done = []
                for bk, ps_ in ((PS[4], (0, 1, 2)), (PS[5], (3, 4, 5)), (PS[6], (6, 7))):
                    w = bk.take()
                    for n, p in enumerate(ps_):
                        o_ = bk.ap[:, 129 * n:129 * n + 129]
                        r = slice(128 * p, 128 * p + 128)
                        for j in range(4):
                            mm(o_, PKH[:, j, r], VH[:, j, p, :], j == 0, False, [u.kv, *w])
                            mm(o_, PKH[:, j, r], VL[:, j, p, :], False, False)
                            m = mm(o_, PKL[:, j, r], VH[:, j, p, :], False, j == 3, mark=p == ps_[-1] and j == 3)
                        yield
                    n, q = len(ps_), slice(ps_[0], ps_[-1] + 1)
                    v = bk.ap[:, 0:129 * n].rearrange("p (b n) -> p b n", b=n)
                    for r, h in ((slice(0, 64), 0), (slice(64, 128), 1)):
                        cp(dve, KVB[r, q, 64 * h:64 * h + 64], v[r, :, 64 * h:64 * h + 64], [m, *fr["kvb"]])
                        b = cp(dve, KS[r, q, h], v[r, :, 128], [m, *fr["ks"]])
                    bk.free = [b]
                    done += [b] * n
                fr["pk"] = [m]
                u.ks = b
                u.kvb = done

            def fold_out(u):
                kt, kw = [], []
                for q, bk in enumerate((PS[5], PS[6])):
                    w = bk.take()
                    for n in range(4):
                        p = 4 * q + n
                        m = tp(bk.ap[:, 128 * n:128 * n + 128], KVB[:, p, :], idf[:, :], [u.kvb[p], *w], n == 3)
                    a = af(KVT[:, 4 * q:4 * q + 4, :].rearrange("p b n -> p (b n)"), bk.ap[:, :], ACT.Copy,
                           [m, *fr["kvt"]])
                    bk.free = [a]
                    kt.append(a)
                    yield
                fr["kvb"] = [m]
                for q, bk in enumerate((PS[5], PS[6])):
                    w = bk.take()
                    for n in range(4):
                        p = 4 * q + n
                        m = mm(bk.ap[:, 128 * n:128 * n + 128], KVT[:, p, :], wout[:, p, :], True, True,
                               [kt[q], got("a0"), *w], n == 3)
                        yield
                    b = af(u.KW[:, 4 * q:4 * q + 4, :].rearrange("p b n -> p (b n)"), bk.ap[:, :], ACT.Copy,
                           [m, *fr[u.nw]])
                    bk.free = [b]
                    kw.append(b)
                fr["kvt"] = [m]
                u.kw = kw

            def normalizers(u):
                bk = PS[6]
                w = bk.take()
                for j in range(4):
                    for p in range(8):
                        m = mm(bk.ap[:, 16 * j + 2 * p:16 * j + 2 * p + 2], u.PQ[:, p, 128 * j:128 * j + 128],
                               KS[:, p, :], True, True, [u.pq, u.ks, *w], j == 3 and p == 7)
                        if u.c == 3 and p % 2:
                            tick(1)
                        if not (j == 3 and p == 7):
                            yield
                fr["ks"] = [m]
                a = ts(dve, NRf, bk.ap[:, 0:64], 1e-6, None, ALU.add, after=[m, *fr["nr"]])
                bk.free = [a]
                a = dve.add(lambda e: e.reciprocal(NRf, NRf), [a])
                u.spread = spread(NR, list(range(4 * u.c, 4 * u.c + 4)), [a], PS[5])
                next(u.spread)
                yield

            def divided(u):
                ct = run(u.spread)
                fr["nr"] = [ct[0]]
                for p in range(8):
                    bk = ring.next()
                    m = mm(bk.ap[:, :], sel[:, p, :], ctb[:, 512 * u.c:512 * u.c + 512], True, True,
                           [ct[0], *bk.take()], True)
                    u.d = tt(dve, u.PQ[:, p, :], u.PQ[:, p, :], bk.ap[:, :], ALU.mult, [m, u.pq])
                    bk.free = [u.d]
                    if u.c == 3:
                        tick(1)
                    yield

            def result(u):
                bk = PS[4]
                w = bk.take()
                for j in range(4):
                    o_ = bk.ap[:, 128 * j:128 * j + 128]
                    mm(o_, ones[0:1, :], rows[0:1, 0:128], True, False, [got("f1"), k_ones, *w])
                    for p in range(8):
                        m = mm(o_, u.PQ[:, p, 128 * j:128 * j + 128], u.KW[:, p, :], False, p == 7, [u.d, *u.kw],
                               j == 3 and p == 7)
                        if not (j == 3 and p == 7):
                            yield
                fr[u.nq] = [m]
                fr[u.nw] = [m]
                xv = x[:, 4 * u.c:4 * u.c + 4, :].rearrange("p t d -> p (t d)")
                f = tt(dve, xv, bk.ap[:, :], xv, ALU.add, [m])
                bk.free = [f]
                after(u.c, [f], [u.xt_read], xh_ring.next(), PS[7])
                u.end = [m, f]
                yield

            old = None
            for c in range(5):
                u = None
                if c < 4:
                    u = Chunk()
                    u.c, u.PQ, u.KW, u.nq, u.nw = c, PQS[c % 2], KWS[c % 2], f"pq{c % 2}", f"kw{c % 2}"
                    u.xt = prep(c)[0]
                weave(keys_values(u) if u else [], normalizers(old) if old else iter(()), 1)
                weave(outer(u) if u else [], divided(old) if old else iter(()), 1)
                weave(queries(u) if u else [], result(old) if old else iter(()), 1.4)
                if u:
                    for _ in fold_out(u):
                        pass
                old = u or old
            return None, old.end

        def ffn1(prep, after):
            PT = wk(0, 8192).rearrange("p (b n) -> p b n", b=4)
            HF = Slot(wk(8192, 4096).rearrange("p (b n) -> p b n", b=8))
            SG = Ring([Slot(wk(12288 + 512 * i, 512)) for i in range(2)])
            SM = Ring([Slot(wk(13312 + 512 * i, 512)) for i in range(2)])
            DD = Ring([Slot(wk(14336, 2048)), Slot(wk(16384, 2048)), Slot(scr[:, 0:2048])])
            DD.slots[2].free = [*tabs]
            EE = Ring([Slot(wk(18432 + 512 * i, 512)) for i in range(8)])
            TK = Ring([Slot(wk(22528 + 416 * i, 416)) for i in range(3)])
            sr, tr = Ring([PS[4]]), Ring([PS[2], PS[3]])
            ptd = []
            pend, late = [], []

            def rank(i):
                xt = prep(i // 4)[0]
                bk = sr.next()
                m = proj_n(bk.ap[:, :], wk_h[:, :], wk_l[:, :], i, [xt, k_fold1, *bk.take()])
                sm = SM.next()
                a = af(sm.ap, bk.ap[:, :], ACT.Copy, [m, *sm.take(), *work_free])
                bk.free = [a]
                sv = sm.ap.rearrange("p (s h k) -> p s h k", s=2, h=4)
                tk = TK.next()
                w = [*tk.take(), *work_free]
                top = tk.ap[:, 0:64].rearrange("p (s h k) -> p s h k", s=2, h=4)
                cb = tk.ap[:, 64:320].rearrange("p (h a b) -> p h a b", h=4, a=8)
                cbf = tk.ap[:, 64:320].rearrange("p (h n) -> p h n", h=4)
                v8 = tk.ap[:, 320:352].rearrange("p (h k) -> p h k", h=4)
                e8 = tk.ap[:, 352:384].rearrange("p (h k) -> p h k", h=4)
                nm, zz, rz = (tk.ap[:, 384 + 4 * j:388 + 4 * j] for j in range(3))
                dd = DD.next()
                Dv = dd.ap.rearrange("p (h x y) -> p h x y", h=4, x=8)
                xb = sv[:, 0, :, 0:8].unsqueeze(3).to_broadcast([128, 4, 8, 64])
                yb = sv[:, 1, :, :].unsqueeze(2).to_broadcast([128, 4, 8, 64])
                dw = [a, *dd.take(), *work_free]
                dh = [tt(pool, Dv[:, h_], xb[:, h_], yb[:, h_], ALU.add, dw) for h_ in range(4)]
                yield
                for s_ in range(2):
                    for h_ in range(4):
                        b = dve.add(lambda e, s_=s_, h_=h_: e.max(top[:, s_, h_, :], sv[:, s_, h_, :]), [a, *w])
                sm.free = [b, dh[3]]
                b = tt(dve, cb, top[:, 0].unsqueeze(3).to_broadcast([128, 4, 8, 8]),
                       top[:, 1].unsqueeze(2).to_broadcast([128, 4, 8, 8]), ALU.add, [b])
                for h_ in range(4):
                    b_ = dve.add(lambda e, h_=h_: e.max(v8[:, h_, :], cbf[:, h_, :]), [b])
                b = b_
                n_ = ts(dve, nm, v8[:, :, 0], -1.0, None, ALU.mult, after=[b])
                b = tt(dve, e8, v8, nm.unsqueeze(2).to_broadcast([128, 4, 8]), ALU.add, [n_])
                yield
                z = af(tk.ap[:, 352:384], tk.ap[:, 352:384], ACT.Exp, [b])
                es = []
                for h_ in range(4):
                    ee = EE.next()
                    y = af(ee.ap, dd.ap[:, 512 * h_:512 * h_ + 512], ACT.Exp, [dh[h_], n_, *ee.take(), *work_free],
                           bias=nm[:, h_:h_ + 1])
                    es.append((ee, y))
                pend.append((i, tk, dd, es, z))
                yield

            def weigh(i, tk, dd, es, z):
                v8 = tk.ap[:, 320:352].rearrange("p (h k) -> p h k", h=4)
                e8 = tk.ap[:, 352:384].rearrange("p (h k) -> p h k", h=4)
                zz, rz, sh = (tk.ap[:, 388 + 4 * j:392 + 4 * j] for j in range(3))
                acc = tk.ap[:, 400:401]
                b = red(zz, e8, ALU.add, [z])
                rz_ = dve.add(lambda e: e.reciprocal(rz, zz), [b])
                e = [ee.ap for ee, y in es]
                g = {}
                for h_ in (0, 2, 1, 3):
                    ee, y = es[h_]
                    f = stt(ee.ap, dd.ap[:, 512 * h_:512 * h_ + 512], v8[:, h_, 7:8], ee.ap, ALU.is_ge, ALU.mult,
                            [y], accum_out=sh[:, h_:h_ + 1])
                    if h_ % 2 == 0:
                        g[h_] = af(ee.ap, ee.ap, ACT.Copy, [f, rz_], scale=rz[:, h_:h_ + 1])
                k1 = stt(e[0], e[1], rz[:, 1:2], e[0], ALU.mult, ALU.add, [f, g[0], rz_])
                k = stt(e[2], e[3], rz[:, 3:4], e[2], ALU.mult, ALU.add, [f, g[2], rz_])
                es[1][0].free = [k1]
                es[3][0].free = [k]
                dd.free = [f]
                f = tt(dve, sh, sh, rz, ALU.mult, [f, rz_])
                f = red(acc, sh, ALU.add, [f])
                f = ts(dve, acc, acc, -1.0, 4.0, ALU.mult, ALU.add, after=[f])
                f = tt(dve, e[2][:, 511:512], e[2][:, 511:512], acc, ALU.add, [f, k])
                tk.free = [f]
                g_ = tt(pool, e[0], e[0], e[2], ALU.add, [f, k, k1])
                es[2][0].free = [g_]
                late.append((i, es[0][0], g_))
                return g_

            def back(i, ee, g_):
                bk = tr.next()
                w = bk.take()
                for q in range(4):
                    m = tp(bk.ap[:, 128 * q:128 * q + 128], ee.ap[:, 128 * q:128 * q + 128], idf[:, :], [g_, *w], q == 3)
                ee.free = [m]
                a = af(PT[:, :, 128 * i:128 * i + 128], bk.ap[:, :].rearrange("p (b n) -> p b n", b=4), ACT.Copy,
                       [m, *work_free])
                bk.free = [a]
                ptd.append(a)

            gr, ur = Ring([PS[0], PS[1]]), Ring([PS[5], PS[6]])
            x_done = []

            def up(c):
                xt = prep(c)[0]
                hs = HF
                hw = [*hs.take(), *work_free]
                for b_ in range(4):
                    g_, u_ = gr.next(), ur.next()
                    n = 128 * b_
                    mg = proj_t(g_.ap[:, :], wgu_h[:, n:n + 128], wgu_l[:, n:n + 128], c, [xt, k_gu, *g_.take()])
                    mu = proj_t(u_.ap[:, :], wgu_h[:, 512 + n:640 + n], wgu_l[:, 512 + n:640 + n], c, u_.take())
                    sg = SG.next()
                    z = af(sg.ap, g_.ap[:, :], ACT.Silu, [mg, got("f1"), *sg.take(), *work_free],
                           bias=bgu[:, b_:b_ + 1])
                    g_.free = [z]
                    f = stt(hs.ap[:, b_, :], u_.ap[:, :], bgu[:, 4 + b_:5 + b_], sg.ap, ALU.add, ALU.mult,
                            [z, mu, *hw])
                    sg.free = [f]
                    u_.free = [f]
                while late:
                    back(*late.pop(0))
                for b_ in range(4):
                    g_ = gr.next()
                    n = 128 * b_
                    mg = proj_t(g_.ap[:, :], de_h[:, n:n + 128], de_l[:, n:n + 128], c, [k_de, *g_.take()])
                    sg = SG.next()
                    z = af(sg.ap, g_.ap[:, :], ACT.Silu, [mg, *sg.take(), *work_free])
                    g_.free = [z]
                    f = tt(dve, hs.ap[:, 4 + b_, :], PT[:, b_, 512 * c:512 * c + 512], sg.ap, ALU.mult,
                           [z, ptd[4 * c + 3], *hw])
                    sg.free = [f]
                return f

            def down(c, h_done):
                bk = PS[4]
                w = bk.take()
                for j in range(4):
                    o_ = bk.ap[:, 128 * j:128 * j + 128]
                    mm(o_, ones[0:1, :], rows[0:1, 128:256], True, False, [got("f1"), k_ones, *w])
                    for b_ in range(8):
                        m = mm(o_, HF.ap[:, b_, 128 * j:128 * j + 128], wdue[:, b_, :], False, b_ == 7,
                               [h_done, k_fold1], j == 3 and b_ == 7)
                HF.free = [m]
                xv = x[:, 4 * c:4 * c + 4, :].rearrange("p t d -> p (t d)")
                f = stt(xv, bk.ap[:, :], 0.5, xv, ALU.mult, ALU.add, [m])
                bk.free = [f]
                x_done.append([f])
                after(c, [f], [m], xh_ring.next(), PS[7])
                return m

            ranks = [rank(i) for i in range(16)]
            for n in range(18):
                if n < 16:
                    next(ranks[n])
                tick(2)
                if late:
                    back(*late.pop(0))
                if 1 <= n < 17:
                    next(ranks[n - 1])
                if pend:
                    g_ = weigh(*pend.pop(0))
                if 1 <= n < 17:
                    next(ranks[n - 1])
                tick(2)
                if n % 4 == 3 and n > 3:
                    m = down(n // 4 - 1, hd)
                if n % 4 == 1 and n > 4:
                    hd = up(n // 4 - 1)
            m = down(3, hd)
            return x_done, [m, x_done[-1][0], g_]

        def tables1(w):
            w = [*w, got("a1"), got("dst")]
            kt, dn, w1d, w1k = (scr[:, a:b] for a, b in ((0, 640), (640, 1152), (1152, 1280), (1280, 1408)))
            z = af(pa[:, 0:2], pa[:, 0:2], ACT.Exp, w)
            z = af(pab[:, :, :], pab[:, :, :], ACT.Exp, w)
            z = af(pa[:, 0:2], pa[:, 0:2], ACT.Ln, [z], bias=1.0)
            z = af(pab[:, :, :], pab[:, :, :], ACT.Ln, [z], bias=1.0)
            a = af(kt, kt, ACT.Ln, [z, *w], scale=pa[:, 1:2], bias=1.0)
            n0 = ts(dve, pa[:, 2:3], pa[:, 0:1], -1.0, None, ALU.mult, after=[z])
            n1 = ts(dve, pab[:, 0, :], pab[:, 0, :], -1.0, None, ALU.mult, after=[z])
            k1 = ts(dve, kt, kt, pa[:, 2:3], None, ALU.mult, after=[a, n0])
            d = tt(dve, w1k[0:64, :], w1k[0:64, :], w1d[0:64, :], ALU.subtract, w)
            h = af(ws_h[:, :], w1d, ACT.Copy, w)
            e = tt(dve, ws_l[:, :], w1d, ws_h[:, :], ALU.subtract, [h])
            done = [e]
            for bk, r in ((PS[4], slice(0, 512)), (PS[6], slice(512, 640))):
                v = bk.ap[:, 0:r.stop - r.start]
                m = mm(v, w1k[0:64, :], kt[0:64, r], True, True, [d, k1, *bk.take()], True)
                h = af(ct_h[:, r], v, ACT.Copy, [m])
                e = tt(dve, ct_l[:, r], v, ct_h[:, r], ALU.subtract, [h, m])
                bk.free = [e]
                done.append(e)
            bk = PS[5]
            m = mm(bk.ap[:, 0:1], w1d[64:128, :], b2r[64:128, :], True, True, [*w, *bk.take()], True)
            e = tt(dve, b1c[:, :], b1c[:, :], bk.ap[:, 0:1], ALU.subtract, [m])
            bk.free = [e]
            done.append(e)
            for h in range(16):
                a = af(kn[:, h, :], dn, ACT.Ln, [z, *w, *reg0_free], scale=pab[:, 1, h:h + 1], bias=1.0)
                k2 = ts(pool, kn[:, h, :], kn[:, h, :], pab[:, 0, h:h + 1], b2b[:, h:h + 1], ALU.mult, ALU.add,
                        [a, n1])
            return [*done, k2]

        def attn1(xt, x_ready, after):
            xt = [xt(c)[0] for c in range(4)]
            FA = wk(0, 8192)
            QH, QL, KH, KL = (wk(8192 + 2048 * i, 2048, F16).rearrange("p (b n) -> p b n", b=8) for i in range(4))
            vx = scr[:, :].bitcast(F16).rearrange("p (i s h d) -> p i s h d", i=2, s=2, h=16)
            VX = [(vx[:, i, 0], vx[:, i, 1]) for i in range(2)]
            VX += [tuple(wk(16384 + 1040 * i + 520 * j, 520, F16).rearrange("p (h d) -> p h d", h=16)
                         for j in range(2)) for i in range(2)]
            TB = Ring([Slot(wk(18464 + 256 * i, 256, F16)) for i in range(4)])
            HL = Ring([Slot(v.rearrange("p (g s n) -> p g s n", g=8, s=2))
                       for v in (wk(19488, 512, F16), wk(20000, 512, F16), half(3072, 1024))])
            GB = Ring([Slot(wk(20512 + 512 * i, 512)) for i in range(4)])
            PB = Ring([Slot(park[:, 512 * i:512 * i + 512]) for i in range(4)])
            TP = Ring([Slot(v) for v in (wk(22560, 512, F16), half(2048, 1024), half(2560, 1024))])
            mxc = wk(23072, 256).rearrange("p (h q) -> p h q", h=16)
            OO = wk(23584, 1024)
            dummy = small[:, 864:865]
            z0 = [ms(dve, dummy, 0.0)]
            mx = small[:, 832:848]
            rd = small[:, 848:864]
            for v in VX:
                ms(dve, v[0][:, :, 64:65], 1.0, work_free)
                v1 = ms(dve, v[1][:, :, 64:65], 0.0, work_free)
            qk_ring = Ring([PS[0], PS[1]])
            tr = Ring([PS[2], PS[3]])
            gr = Ring([PS[4], PS[5]])
            pv_ring = Ring([PS[6], PS[7], PS[5]])
            sc_ring = Ring([PS[4], PS[0], PS[1]])
            wf = [*work_free, *tabs]
            for b_ in PB.slots + HL.slots + TP.slots + GB.slots:
                b_.free = [*xt, *x_ready, *wf]
            ident = idf[:, :]
            st = {"qt": [], "vx": [], "oo": [], "mx": [], "mc": [], "v": None, "q": [], "f": [[]] * 16}
            x_done = [[] for _ in range(4)]

            def project_qk(c, b0, b1, turning, adder):
                def step(p, off, hi, lo, b0, b1):
                    n = off + 128 * p
                    m0 = proj_t(b0.ap[:, :], wa_h[:, n:n + 128], wa_l[:, n:n + 128], c, [xt[c], *k_wa, *b0.take()])
                    n += 1024
                    m1 = proj_t(b1.ap[:, :], wa_h[:, n:n + 128], wa_l[:, n:n + 128], c, b1.take())
                    ra, rb = turning.next(), turning.next()
                    a = tt(dve, ra.ap, b0.ap[:, :], cs[:, 0, :], ALU.mult, [m0, got("a1"), *ra.take()])
                    b = tt(dve, rb.ap, b1.ap[:, :], cs[:, 1, :], ALU.mult, [m1, *rb.take()])
                    b0.free = [a]
                    b1.free = [b]
                    q_ = tt(adder, ra.ap, ra.ap, rb.ap, ALU.add, [a, b])
                    rb.free = [q_]
                    h = af(hi[:, p, :], ra.ap, ACT.Copy, [q_, *st["qt"], *wf])
                    l = tt(pool, lo[:, p, :], ra.ap, hi[:, p, :], ALU.subtract, [h, q_, *st["qt"], *wf])
                    ra.free = [l]
                    st["q"] = [l]
                for p in range(8):
                    for off, hi, lo in ((0, QH, QL), (2048, KH, KL)):
                        r = (p, off, hi, lo, b0.next(), b1.next())
                        yield lambda r=r: step(*r)

            def project_v(c):
                pr = Ring([PS[0], PS[1]])
                for j in range(4):
                    for n in range(2):
                        bk = pr.next()
                        s_ = slice(4096 + 512 * n, 4096 + 512 * n + 512)
                        m = proj_n(bk.ap[:, :], wa_h[:, s_], wa_l[:, s_], 4 * c + j, bk.take())
                        hi, lo = (v[:, 8 * n:8 * n + 8, 0:64] for v in VX[j])
                        v = bk.ap[:, :].rearrange("p (h d) -> p h d", h=8)
                        h = af(hi, v, ACT.Copy, [m, *st["vx"], *wf])
                        v_ = tt(dve, lo, v, hi, ALU.subtract, [h, m, *st["vx"], *wf])
                        bk.free = [v_]
                st["v"] = v_

            class Unit:
                pass

            def score(u, h):
                J, i0 = u.J, u.i0
                bk = sc_ring.next()
                r = slice(64 * (h % 2), 64 * (h % 2) + 64)
                qh, ql, kh, kl = QH[r, h // 2, i0:i0 + 128], QL[r, h // 2, i0:i0 + 128], KH[r, h // 2, 0:J], \
                    KL[r, h // 2, 0:J]
                mm(bk.ap[:, 0:J], ql, kh, True, False, [*st["q"], *bk.take()])
                mm(bk.ap[:, 0:J], qh, kh, False, False)
                m = mm(bk.ap[:, 0:J], qh, kl, False, True, mark=True)
                u.scores.append((h, bk, m))
                st["qt"] = [m]

            def add_bias(u):
                J = u.J
                h, bk, m = u.scores.pop(0)
                u.s0 = stt(u.F[:, 0:J // 4, h, :], bk.ap[:, 0:J].rearrange("p (a b) -> p a b", b=4), 0.125,
                           kn[:, h, 512 - J:512].rearrange("p (a b) -> p a b", b=4), ALU.mult, ALU.add,
                           [m, *st["f"][h], *wf])
                bk.free = [u.s0]

            def cut(u, q, lane=pool):
                hl = HL.next()
                w = hl.take()
                v = u.FL[:, 512 * q:512 * q + 512].rearrange("p (g n) -> p g n", g=8)
                a = af(hl.ap[:, :, 0, :], v, ACT.Copy, [u.s0, *w])
                b = tt(lane, hl.ap[:, :, 1, :], v, hl.ap[:, :, 0, :], ALU.subtract, [a, u.s0, *w])
                return hl, b

            def turn(hl, b, k):
                tb, bk = TB.next(), tr.next()
                v = bk.ap[:, 0:256].bitcast(F16)
                w = bk.take()
                for g in range(4):
                    n = 128 * (3 - g)
                    m_ = tp(v[:, n:n + 128], hl.ap[:, 4 * k + g].rearrange("p s n -> p (s n)"), idh[:, :],
                            [b, k_idh, *w], g == 3)
                if k == 1:
                    hl.free = [m_]
                c_ = cp(dve, tb.ap, v, [m_, *tb.take()])
                bk.free = [c_]
                return tb, c_

            def sliding(tab, n):
                v = tab[:, n:n + 128]
                return bass.AP(v.tensor, v.offset, [[640, 128], [4, 4], [1, 128]])

            def hidden_mix(u, h, m):
                def out_(g):
                    bk, w, k, gb, z = m
                    n, f = 256 * k + 64 * g, 128 * (3 - g)
                    return mm(bk.ap[:, n:n + 64], gb.ap[:, f:f + 128], w2b[:, :], True, True, [z, *w], g == 3)

                m_ = hb = None
                if h:
                    q, k, tb, ready = h
                    bk = gr.next()
                    o4 = bk.ap[:, :].rearrange("p (g n) -> p g n", g=4)
                    n = 128 + u.i0 - 32 * q - 16 * k - 12
                    w = [*bk.take(), *tabs, k_idh]
                for g in range(4):
                    if h:
                        if g < 2:
                            mm(o4, idh[:, :], sliding((ct_h, ct_l)[g], n), g == 0, False, w)
                        else:
                            e = mm(bk.ap[:, :], (ws_h, ws_l)[g - 2][:, :], tb.ap, False, g == 3, [ready], g == 3)
                    if m:
                        m_ = out_(g)
                if m:
                    m[3].free = [m_]
                if h:
                    tb.free = [e]
                    gb = GB.next()
                    z = af(gb.ap, bk.ap[:, :], ACT.Gelu, [e, *gb.take()], bias=b1c[:, 0:1])
                    bk.free = [z]
                    hb = (gb, z)
                return hb, m_

            def mlp(u, nxt, fill):
                nq = 4 * (u.it + 1)
                order = list(range(nq - 4, nq)) + list(range(nq - 4))
                steps = [(q, k) for q in order for k in range(2)]
                cuts = [cut(u, q, lane) for q, lane in zip(order[:2], (dve, pool))]
                af(small[:, 865:866], dummy, ACT.Gelu, z0)
                ta, hb, late, u.marks = [], [], [], []
                for n in range(len(steps) + 3):
                    if n < len(steps):
                        q, k = steps[n]
                        if k == 0 and n // 2 + 2 < len(order):
                            cuts.append(cut(u, order[n // 2 + 2]))
                        ta.append(turn(*cuts[n // 2], k))
                    h = m = None
                    if 1 <= n <= len(steps):
                        h = (*steps[n - 1], *ta[n - 1])
                    if n >= 3:
                        q, k = steps[n - 3]
                        if k == 0:
                            wb = qk_ring.next()
                            ww = wb.take()
                        m = (wb, ww, k, *hb[n - 3])
                    r, m_ = hidden_mix(u, h, m)
                    tick(1)
                    if 1 <= n and len(fill) > 1:
                        fill.pop(0)()
                    if r:
                        hb.append(r)
                    if n >= 3 and k == 1:
                        fv = u.FL[:, 512 * q:512 * q + 512]
                        f_ = tt(dve, fv, fv, wb.ap[:, :], ALU.add, [m_, cuts[(n - 3) // 2][1]])
                        wb.free = [f_]
                        v = fv.rearrange("p (a h b) -> p a h b", h=16, b=4)
                        if q >= nq - 4:
                            d = 32 * q - u.i0
                            f_ = pool.add(lambda e, v=v, d=d: e.affine_select(
                                out=v, in_=v, compare_op=ALU.is_ge, fill=-3.0e38, base=-d,
                                pattern=[[-4, 8], [0, 16], [-1, 4]], channel_multiplier=1), [f_])
                            u.marks.append(f_)
                        late.append((q, v, f_))
                        while len(late) > (2 if q >= nq - 4 else 1):
                            peak(late.pop(0), u)
                af(small[:, 865:866], dummy, ACT.Exp, z0)
                for r in late:
                    peak(r, u)
                u.marks.append(f_)

            def peak(r, u):
                q, v, f = r
                u.mc = dve.add(lambda e: e.tensor_reduce(mxc[:, :, q], v.rearrange("p a h b -> p h a b"),
                                                         mybir.AxisListType.XY, ALU.max), [f, *st["mc"]])

            def window(u, nxt, fill):
                J, it, c = u.J, u.it, u.c
                nq = 4 * (it + 1)
                b = red(mx, mxc[:, :, 0:nq], ALU.max, [u.mc, *st["mx"]])
                st["mc"] = [b]
                b = ts(dve, mx, mx, -1.0, None, ALU.mult, after=[b])
                if nxt:
                    score(nxt, 0)
                while fill:
                    fill.pop(0)()
                ex, tps = [], []
                for k_ in range(-1, 18):
                    k = k_ + 1
                    if k < 16:
                        pb = PB.next()
                        e_ = af(pb.ap[:, 0:J].rearrange("p (a b) -> p a b", b=4), u.F[:, 0:J // 4, k, :], ACT.Exp,
                                [b, *u.marks, *pb.take()], bias=mx[:, k:k + 1])
                        ex.append((pb, e_))
                        st["f"][k] = [e_]
                    k = k_
                    if 1 <= k <= 16:
                        pb, e_ = ex[k - 1]
                        bk, tb = tr.next(), TP.next()
                        w = bk.take()
                        for jt in range(it + 1):
                            m = tp(bk.ap[:, 128 * jt:128 * jt + 128], pb.ap[:, 128 * jt:128 * jt + 128], ident,
                                   [e_, *w], jt == it)
                        pb.free = [m]
                        tps.append((tb, halves(bk, tb, J, m)))
                    if nxt and 1 <= k <= 16:
                        if k < 16:
                            score(nxt, k)
                        add_bias(nxt)
                    if k == 17:
                        out_steps = project_out(u)
                        out_steps.pop(0)()
                    if 2 <= k <= 17:
                        h = k - 2
                        tb, a = tps[h]
                        if h % 4 == 0:
                            pvb = pv_ring.next()
                            w = pvb.take()
                        o_ = pvb.ap[:, 65 * (h % 4):65 * (h % 4) + 65]
                        for jt in range(it + 1):
                            n = 128 * jt
                            vh, vl = VX[jt][0][:, h, :], VX[jt][1][:, h, :]
                            mm(o_, tb.ap[:, 512 + n:640 + n], vh, jt == 0, False, [a, st["v"], v1, *w])
                            mm(o_, tb.ap[:, n:n + 128], vh, False, False)
                            m = mm(o_, tb.ap[:, n:n + 128], vl, False, jt == it, mark=jt == it)
                        tb.free = [m]
                        if h % 4 == 3:
                            v = pvb.ap[:, 0:260].rearrange("p (h d) -> p h d", h=4)
                            r_ = rd[:, h - 3:h + 1]
                            a = dve.add(lambda e, v=v, r_=r_: e.reciprocal(r_, v[:, :, 64]), [m])
                            o2 = OO[:, 64 * (h - 3):64 * h + 64].rearrange("p (h d) -> p h d", h=4)
                            u.b = tt(dve, o2, v[:, :, 0:64], r_.unsqueeze(2).to_broadcast([128, 4, 64]),
                                     ALU.mult, [a, *st["oo"], *wf])
                            pvb.free = [u.b]
                st["mx"] = [ex[-1][1]]
                st["vx"] = [m]
                return out_steps

            def halves(bk, tb, J, m):
                h = af(tb.ap[:, 0:J], bk.ap[:, 0:J], ACT.Copy, [m, *tb.take()])
                l = tt(dve, tb.ap[:, 512:512 + J], bk.ap[:, 0:J], tb.ap[:, 0:J], ALU.subtract, [h, m])
                bk.free = [l]
                return l

            def project_out(u):
                c, it = u.c, u.it
                tbs = []

                def turned(q):
                    b = u.b
                    bk, tb = tr.next(), TP.next()
                    w = bk.take()
                    for i in range(4):
                        n = 512 * q + 128 * i
                        m = tp(bk.ap[:, 128 * i:128 * i + 128], OO[:, n:n + 128], ident, [b, *w], i == 3)
                    tbs.append((tb, halves(bk, tb, 512, m)))
                    st["oo"] = [m]

                def product():
                    bk = PS[7]
                    w = bk.take()
                    o_ = bk.ap[:, 0:128]
                    for q in range(2):
                        tb, a = tbs[q]
                        for i in range(4):
                            n, r = 128 * i, slice(512 * q + 128 * i, 512 * q + 128 * i + 128)
                            mm(o_, tb.ap[:, 512 + n:640 + n], wo_h[:, r], q == 0 and i == 0, False, [a, *k_wa, *w])
                            mm(o_, tb.ap[:, n:n + 128], wo_h[:, r], False, False)
                            m = mm(o_, tb.ap[:, n:n + 128], wo_l[:, r], False, q == 1 and i == 3, mark=i == 3)
                        tb.free = [m]
                    xv = x[:, 4 * c + it, :]
                    f = tt(dve, xv, o_, xv, ALU.add, [m])
                    bk.free = [f]
                    x_done[c].append(f)
                    u.end = [m, f]
                    if it == 3:
                        after(c, [f], [m], XH[1], PS[6])

                return [lambda: turned(0), lambda: turned(1), product]

            def unit(c, it):
                u = Unit()
                u.c, u.it, u.i0, u.J = c, it, 128 * it, 128 * (it + 1)
                u.scores = []
                u.FL = FA[:, 0:16 * u.J]
                u.F = u.FL.rearrange("p (a h b) -> p a h b", h=16, b=4)
                return u

            units = [unit(c, it) for c in range(4) for it in range(4)]
            for f in project_qk(0, Ring([PS[0], PS[1]]), Ring([PS[4], PS[5]]), Ring(PB.slots + GB.slots), dve):
                f()
            for h in range(16):
                score(units[0], h)
                add_bias(units[0])
            project_v(0)
            fill = []
            for u, nxt in zip(units, [*units[1:], None]):
                if u.it == 3 and u.c < 3:
                    for f in project_qk(u.c + 1, Ring([PS[6]]), Ring([PS[7]]), PB, pool):
                        fill[-1:-1] = [f, lambda: None]
                mlp(u, nxt, fill)
                fill = window(u, nxt, fill)
                if nxt and nxt.it == 0:
                    project_v(nxt.c)
            for f in fill:
                f()
            prev = u
            return u.end

        work_free, reg0_free = [], []
        k_wv = k_gu = k_de = k_fold0 = k_fold1 = None

        def prepare_weights():
            nonlocal k_wv, k_gu, k_de, k_fold0, k_fold1
            k_rf = got("a0")
            fr = Ring([PS[1], PS[2]])
            yield from fold(wq_h, wq_l, [s_qk[:, p, :] for p in range(8)], [s_rf[:, p, :] for p in range(8)], 2,
                            [k_rf], fr)
            k_fold0 = yield from fold(wkr_h, wkr_l, [s_qk[:, 8 + p, :] for p in range(8)],
                                      [s_rf[:, p, :] for p in range(8)], 2, [k_rf], fr)
            k_fold1 = yield from fold(wk_h, wk_l, [s_wqT[:, p, :] for p in range(4)],
                                      [s_key[:, p, :] for p in range(4)], 1, [got("f1")], fr)
            k_wv = split(wv_h, wv_l, s_wv, [got("a0")], pool)
            yield
            k_gu = split(wgu_h, wgu_l, s_gu, [got("f1")], pool)
            yield
            k_de = split(de_h, de_l, s_de, [got("f1")], pool)
            yield

        def following(kind):
            marks = []

            def put(*a):
                marks.append((yield from kind(*a)))

            def get(c):
                while len(marks) <= c:
                    tick()
                return marks[c]

            return get, lambda *a: behind.append(put(*a))

        p0, hook = following(norm_and_route)
        hook(0, [got("x0")], [], xh_ring.next(), PS[6])
        tick(7)
        k_gate = split(wg_h, wg_l, s_gate, [got("w13")], dve)
        k_sel = cp(dve, sel.rearrange("p b n -> p (b n)"), wk(23000, 1024)[0:48, :], [got("cst")])
        ct_free = [k_sel]
        while behind:
            tick()
        k_w13 = split(w13_h, w13_l, s_w13, [got("w13")], dve)
        hook(1, [got("x1")], [], xh_ring.next(), PS[7])
        tick(8)
        behind.append(prepare_weights())
        hook(2, [got("x2")], [], xh_ring.next(), PS[7])
        hook(3, [got("x3")], [], xh_ring.next(), PS[7])
        p1, hook = following(norm_only)
        xr, free = ffn0(p0, hook)
        k_wa = []
        stage = Ring([Slot(wk(16400 + 1024 * i, 1024)) for i in range(6)])
        for i in range(5):
            s_ = stage.next()
            load(f"wa{i}", s_.ap, t["wa"][:, 1024 * i:1024 * i + 1024], [k_fold1, k_fold0, k_de, k_gu, k_wv])
            k_wa.append(split(wa_h[:, 1024 * i:1024 * i + 1024], wa_l[:, 1024 * i:1024 * i + 1024], s_.ap,
                              [got(f"wa{i}")], pool))
        s_ = stage.next()
        load("wo", s_.ap, t["wo"], [k_fold1, k_fold0, k_de, k_gu, k_wv])
        k_wa.append(split(wo_h[:, :], wo_l[:, :], s_.ap, [got("wo")], pool))
        work_free = free
        p2, hook = following(norm_and_route)
        xr, free = attn0(p1, hook)
        work_free = free
        p3, hook = following(norm_only)
        xr, free = ffn0(p2, hook)
        work_free = [*free, *k_wa]
        reg0_free = free
        tabs = tables1([])
        p4, hook = following(norm_only)
        xr, free = ffn1(p3, hook)
        work_free = free
        s_park = sem("s_park")
        sp.add(lambda e: e.dma_start(parked, park[:, 0:3072]).then_inc(s_park, 16), [k_gu, k_de, k_fold1, got("f1")],
               False)
        p5, hook = following(norm_only)
        free = attn1(p4, [(s_park, 16)], hook)
        work_free = free
        load("back", park[:, 0:3072], parked, [(s_park, 16), *free, p5(3)[0]])
        k_gu = k_de = k_fold1 = got("back")
        xr, free = ffn1(p5, lambda *a: None)
        od = out.rearrange("b (q p) d -> p (b q) d", p=128)
        s_out = sem("s_out")
        for c in range(4):
            sp.add(lambda e, c=c: e.dma_start(od[:, 4 * c:4 * c + 4, :], x[:, 4 * c:4 * c + 4, :]).then_inc(s_out, 16),
                   xr[c], False)
        sp.add(lambda e: e.wait_ge(s_out, 64), (), False)

        block = ctx.enter_context(nc.Block())

        @block.sync
        def _(e):
            sp.issue(e)

        @block.tensor
        def _(e):
            pe.issue(e)

        @block.scalar
        def _(e):
            act.issue(e)

        @block.vector
        def _(e):
            dve.issue(e)

        @block.gpsimd
        def _(e):
            pool.issue(e)


def _layout(i):
    import numpy as np
    f4 = np.float32
    g = {k: np.asarray(v) for k, v in i.items()}
    t = {"x": g["L0_attn_x"]}
    t["w_gate"] = g["L0_ffn_w_gate"].T
    t["w13"] = np.concatenate([g["L0_ffn_w1_e"].reshape(1024, 128), g["L0_ffn_w1_s"],
                               g["L0_ffn_w3_e"].reshape(1024, 128), g["L0_ffn_w3_s"]]).T
    w2 = np.concatenate([g["L0_ffn_w2_e"].transpose(0, 2, 1).reshape(1024, 128), g["L0_ffn_w2_s"].T])
    t["w2"] = w2.reshape(9, 128, 128).transpose(1, 0, 2)

    def pairs(a):
        b = np.zeros((a.shape[0] // 2, 128, 128), f4)
        b[:, :64, :64] = a[0::2]
        b[:, 64:, 64:] = a[1::2]
        return b.transpose(1, 0, 2)

    wqkv = g["L0_attn_W_qkv"]
    t["wqkT"] = wqkv[:, :2048].T.reshape(16, 128, 128).transpose(1, 0, 2)
    t["wv0"] = wqkv[:, 2048:]
    t["rf"] = pairs(g["L0_attn_RF"])
    t["wout"] = g["L0_attn_W_out"].reshape(8, 128, 128).transpose(1, 0, 2)
    t["wgu"] = np.concatenate([g["L1_ffn_Wg"], g["L1_ffn_Wu"]], axis=1)
    t["wqT"] = g["L1_ffn_Wq"].T.reshape(4, 128, 128).transpose(1, 0, 2)
    t["keys"] = pairs(g["L1_ffn_keys"].transpose(2, 0, 3, 1).reshape(8, 64, 64))
    t["deT"] = g["L1_ffn_down_embed"].T
    t["wdue"] = np.concatenate([g["L1_ffn_Wd"], g["L1_ffn_up_embed"]]).reshape(8, 128, 128).transpose(1, 0, 2)
    t["bgu"] = np.concatenate([g["L1_ffn_bg"], g["L1_ffn_bu"]]).reshape(8, 128).T
    t["rows"] = np.concatenate([g["L0_attn_b_out"], g["L1_ffn_bd"]])[None]
    w = g["L1_attn_w_qkv"]

    def turned(a):
        return a.reshape(128, 16, 2, 32)[:, :, ::-1].reshape(128, 1024)

    t["wa"] = np.concatenate([w[:, :1024], turned(w[:, :1024]), w[:, 1024:2048], turned(w[:, 1024:2048]),
                              w[:, 2048:]], axis=1)
    t["wo"] = g["L1_attn_w_o"].reshape(8, 128, 128).transpose(1, 0, 2).reshape(128, 1024)

    def spaced(a):
        b = np.zeros((a.shape[0], 4, a.shape[1], 4), f4)
        for j in range(4):
            b[:, j, :, j] = a
        return b.reshape(a.shape[0] * 4, a.shape[1] * 4)

    w1 = g["L1_attn_w1"]
    t["w1d"] = np.concatenate([spaced(w1[:16])] * 2)
    t["w1k"] = spaced(w1[16:])
    t["w2b"] = spaced(g["L1_attn_w2"])
    t["b1c"] = np.repeat(g["L1_attn_b1"], 4)[:, None]
    t["b2r"] = np.repeat(g["L1_attn_b2"], 4)[:, None]
    t["b2b"] = np.tile(g["L1_attn_b2"][None], (128, 1))
    lp, la = g["L1_attn_log_p"].reshape(16), g["L1_attn_log_a"].reshape(16)
    t["lp_c"] = np.tile(np.repeat(lp, 4), 2)[:, None]
    t["la_c"] = np.tile(np.repeat(la, 4), 2)[:, None]
    t["pab"] = np.tile(np.stack([lp, la])[None], (128, 1, 1))
    t["c_id"] = np.eye(128, dtype=f4)
    e = np.arange(48)[:, None, None] % 16
    t["c_sel"] = (e == 2 * np.arange(8)[None, :, None] + np.arange(128)[None, None] // 64).astype(f4)
    q = np.arange(4)
    t["c_tri"] = np.tile((q[None, :] < q[:, None]).astype(f4)[None], (128, 1, 1))
    inv = (f4(1.0) / np.power(f4(10000.0), np.arange(0, 64, 2, dtype=f4) / f4(64))).astype(f4)
    fr = np.outer(np.arange(512, dtype=f4), inv).astype(f4)
    emb = np.concatenate([fr, fr], -1)
    sign = np.where(np.arange(64) < 32, f4(-1), f4(1))
    t["c_rope"] = np.stack([np.tile(np.cos(emb).astype(f4).T, (2, 1)),
                            np.tile((np.sin(emb).astype(f4) * sign).T, (2, 1))], axis=1)
    p = np.arange(128)[:, None]
    t["c_dn"] = np.abs(p + 384 - np.arange(512)[None]).astype(f4)
    t["c_dt"] = np.abs(np.arange(640)[None] - 128 - p % 4).astype(f4)
    return {k: np.ascontiguousarray(v) for k, v in t.items()}


def kernel(**inputs):
    import numpy as _np
    import concourse.bacc as _bacc
    from concourse import mybir as _mybir
    from concourse.bass_utils import run_bass_kernel_spmd as _run

    nc = _bacc.Bacc("TRN2", target_bir_lowering=False, num_devices=1)
    arrays, t = {}, {}
    for name, a in _layout(inputs).items():
        arrays[f"in_{name}_dram"] = a
        t[name] = nc.dram_tensor(f"in_{name}_dram", a.shape, _mybir.dt.from_np(a.dtype), kind="ExternalInput").ap()
    o = nc.dram_tensor("out_0_dram", (4, 512, 128), _mybir.dt.float32, kind="ExternalOutput").ap()
    build(nc, t, o)
    r = _run(nc, [arrays], core_ids=[0])
    return r.results[0]["out_0_dram"]
```
